# Optimizing a Trainium2 kernel written in Bass

```python
import numpy as np
import jax
import jax.numpy as jnp

def _softmax(x, axis=-1):
    return jax.nn.softmax(x, axis=axis)

def _gelu(x):
    return jax.nn.gelu(x, approximate=True)

def _silu(x):
    return jax.nn.silu(x)

def _sigmoid(x):
    return jax.nn.sigmoid(x)

def _layernorm(x, axis=-1, eps=1e-05):
    m = jnp.mean(x, axis=axis, keepdims=True)
    v = jnp.var(x, axis=axis, keepdims=True)
    return (x - m) / jnp.sqrt(v + eps)

def _scatter_add(tgt, idx, src, axis=0):
    return tgt.at[idx].add(src)

def _segment_sum(src, seg, n):
    return jax.ops.segment_sum(src, seg, n)
kernel_name = 'mk_perceiver_d1_seqx_r2_cd80c0'

def setup_inputs(seed: int=0):
    np.random.seed(seed)
    _w = jnp.asarray

    def _rec_inputs():
        import jax
        import jax.numpy as jnp
        _rk = jax.random.key(seed)
        x = -0.0003929 + 0.9999 * jax.random.normal(jax.random.fold_in(_rk, 1), (2, 128, 1024), jnp.float32)
        _lenS = 128 - jax.random.randint(jax.random.fold_in(_rk, 7), (2,), 0, max(1, 128 // 4) + 1, jnp.int32)
        _lenS2 = 2048 - jax.random.randint(jax.random.fold_in(_rk, 8), (2,), 0, max(1, 2048 // 4) + 1, jnp.int32)
        _ctx_1024P = jax.random.normal(jax.random.fold_in(_rk, 11), (2, 16, 512), jnp.float32)
        _ctx_1024c = jax.random.dirichlet(jax.random.fold_in(_rk, 511), 0.3 * jnp.ones((16,), jnp.float32), (2, 2048))
        _ctx_1024t = jnp.einsum('bsk,bkd->bsd', _ctx_1024c, _ctx_1024P)
        _ctx_1024t = _ctx_1024t * jax.lax.rsqrt(jnp.mean(jnp.square(_ctx_1024t)) + 1e-12) * 0.953939
        ctx_1024 = -0.000494167 + 1.00018 * (_ctx_1024t + 0.3 * jax.random.normal(jax.random.fold_in(_rk, 611), (2, 2048, 512), jnp.float32))
        _validS = jnp.arange(128)[None, :] < _lenS[:, None]
        _validS2 = jnp.arange(2048)[None, :] < _lenS2[:, None]
        _causal = jnp.tril(jnp.ones((128, 128), dtype=bool))
        mask_BxS2_bf1 = jnp.ones((2, 2048), dtype=bool)
        return (x, ctx_1024, mask_BxS2_bf1)
    x, ctx_1024, mask_BxS2_bf1 = _rec_inputs()

    def _L0_xattn_setup():
        import jax, jax.numpy as jnp
        import numpy as np
        N_HEADS = 16
        N_KV_HEADS = 8
        HEAD_DIM = 128
        D_TEXT = 1024
        D_VISION = 512
        GROUPS = N_HEADS // N_KV_HEADS
        key = jax.random.key(seed)
        ks = jax.random.split(key, 6)
        B, T_text, T_vis = (4, 1024, 288)
        text_hidden = jax.random.normal(ks[0], (B, T_text, D_TEXT), dtype=jnp.float32)
        vision_tokens = jax.random.normal(ks[1], (B, T_vis, D_VISION), dtype=jnp.float32)
        vision_mask = jnp.ones((B, T_vis), dtype=bool)
        s = 0.02
        Wq = jax.random.normal(ks[2], (D_TEXT, N_HEADS * HEAD_DIM), dtype=jnp.float32) * s
        Wk = jax.random.normal(ks[3], (D_VISION, N_KV_HEADS * HEAD_DIM), dtype=jnp.float32) * s
        Wv = jax.random.normal(ks[4], (D_VISION, N_KV_HEADS * HEAD_DIM), dtype=jnp.float32) * s
        Wo = jax.random.normal(ks[5], (N_HEADS * HEAD_DIM, D_TEXT), dtype=jnp.float32) * s
        return {'text_hidden': text_hidden, 'vision_tokens': vision_tokens, 'vision_mask': vision_mask, 'Wq': Wq, 'Wk': Wk, 'Wv': Wv, 'Wo': Wo}
    _L0_xattn_all = _L0_xattn_setup()
    _L0_xattn_in = {k: v for k, v in _L0_xattn_all.items() if k in ('Wq', 'Wk', 'Wv', 'Wo')}
    del _L0_xattn_all

    def _L0_attn_setup():
        import jax, jax.numpy as jnp
        import numpy as np
        B_, S_, E_ = (2, 1024, 1024)
        H_, P_, N_, G_, K_, CH_ = (64, 64, 128, 1, 4, 128)
        INTER = H_ * P_
        CONV_DIM = INTER + 2 * G_ * N_
        PROJ = INTER + CONV_DIM + H_
        EPS = 1e-05

        def segsum(x):
            T = x.shape[-1]
            xe = jnp.broadcast_to(x[..., None], x.shape + (T,))
            m_excl = jnp.tril(jnp.ones((T, T), bool), -1)
            s = jnp.cumsum(jnp.where(m_excl, xe, 0.0), axis=-2)
            m_incl = jnp.tril(jnp.ones((T, T), bool), 0)
            return jnp.where(m_incl, s, -jnp.inf)

        def ssm_forward(input_states, in_proj_w, conv_w, conv_b, A_log, dt_bias, D, norm_w, out_proj_w):
            b, s, _ = input_states.shape
            proj = input_states @ in_proj_w.T
            gate, hBC, dt = jnp.split(proj, [INTER, INTER + CONV_DIM], axis=-1)
            x = hBC.transpose(0, 2, 1)
            x = jax.lax.conv_general_dilated(x, conv_w, (1,), [(K_ - 1, 0)], dimension_numbers=('NCH', 'OIH', 'NCH'), feature_group_count=CONV_DIM)
            hBC = jax.nn.silu((x + conv_b[None, :, None]).transpose(0, 2, 1))
            hs, Bmat, Cmat = jnp.split(hBC, [INTER, INTER + G_ * N_], axis=-1)
            A = -jnp.exp(A_log)
            dt = jax.nn.softplus(dt + dt_bias)
            xh = hs.reshape(b, s, H_, P_)
            Bf = jnp.repeat(Bmat.reshape(b, s, G_, N_), H_ // G_, axis=2)
            Cf = jnp.repeat(Cmat.reshape(b, s, G_, N_), H_ // G_, axis=2)
            D_res = D[:, None] * xh
            xh = xh * dt[..., None]
            Adt = A[None, None, :] * dt
            nch = s // CH_
            xc = xh.reshape(b, nch, CH_, H_, P_)
            Bc = Bf.reshape(b, nch, CH_, H_, N_)
            Cc = Cf.reshape(b, nch, CH_, H_, N_)
            Ac = Adt.reshape(b, nch, CH_, H_).transpose(0, 3, 1, 2)
            A_cum = jnp.cumsum(Ac, axis=-1)
            L = jnp.exp(segsum(Ac))
            Gm = jnp.einsum('bclhn,bcshn->bclsh', Cc, Bc)
            M = Gm * L.transpose(0, 2, 3, 4, 1)
            Y_diag = jnp.einsum('bclsh,bcshp->bclhp', M, xc)
            decay_states = jnp.exp(A_cum[..., -1:] - A_cum)
            states = jnp.einsum('bclhn,bhcl,bclhp->bchpn', Bc, decay_states, xc)
            states = jnp.concatenate([jnp.zeros_like(states[:, :1]), states], axis=1)
            A_last = jnp.pad(A_cum[..., -1], ((0, 0), (0, 0), (1, 0)))
            decay_chunk = jnp.exp(segsum(A_last))
            new_states = jnp.einsum('bhij,bjhpn->bihpn', decay_chunk, states)
            states = new_states[:, :-1]
            state_decay = jnp.exp(A_cum)
            Y_off = jnp.einsum('bclhn,bchpn,bhcl->bclhp', Cc, states, state_decay)
            y = (Y_diag + Y_off).reshape(b, s, H_, P_) + D_res
            y = y.reshape(b, s, INTER)
            yg = y * jax.nn.silu(gate)
            var = jnp.mean(yg * yg, axis=-1, keepdims=True)
            yn = norm_w * (yg * jax.lax.rsqrt(var + EPS))
            return yn @ out_proj_w.T
        key = jax.random.key(seed)
        ks = jax.random.split(key, 4)
        return {'input_states': jax.random.normal(ks[0], (B_, S_, E_), jnp.float32), 'mask': jnp.ones((B_, 1, S_), jnp.int32), 'in_proj_w': jax.random.normal(ks[1], (PROJ, E_), jnp.float32) * 0.02, 'conv_w': jax.random.normal(ks[2], (CONV_DIM, 1, K_), jnp.float32) * 0.2, 'conv_b': jnp.zeros((CONV_DIM,), jnp.float32), 'A_log': jnp.log(jnp.arange(1, H_ + 1, dtype=jnp.float32)), 'dt_bias': jnp.ones((H_,), jnp.float32), 'D': jnp.ones((H_,), jnp.float32), 'norm_w': jnp.ones((INTER,), jnp.float32), 'out_proj_w': jax.random.normal(ks[3], (E_, INTER), jnp.float32) * 0.02}
    _L0_attn_all = _L0_attn_setup()
    _L0_attn_in = {k: v for k, v in _L0_attn_all.items() if k in ('mask', 'in_proj_w', 'conv_w', 'conv_b', 'A_log', 'dt_bias', 'D', 'norm_w', 'out_proj_w')}
    del _L0_attn_all

    def _L0_ffn_setup():
        import jax, jax.numpy as jnp
        import numpy as np
        H, I, E, TOP_K = (1024, 704, 16, 6)
        IS = 1408
        NORM_TOPK_PROB = False

        def _silu_and_mul(gate_up):
            d = gate_up.shape[-1] // 2
            g, u = (gate_up[..., :d], gate_up[..., d:])
            return jax.nn.silu(g) * u
        key = jax.random.key(seed)
        ks = jax.random.split(key, 6)
        s = 0.02
        return {'x': jax.random.normal(ks[0], (1, 1024, H), jnp.float32), 'gate_w': jax.random.normal(ks[1], (E, H), jnp.float32) * s, 'w1': jax.random.normal(ks[2], (E, 2 * I, H), jnp.float32) * s, 'w2': jax.random.normal(ks[3], (E, H, I), jnp.float32) * s, 'shared_w1': jax.random.normal(ks[4], (2 * IS, H), jnp.float32) * s, 'shared_w2': jax.random.normal(ks[5], (H, IS), jnp.float32) * s}
    _L0_ffn_all = _L0_ffn_setup()
    _L0_ffn_in = {k: v for k, v in _L0_ffn_all.items() if k in ('gate_w', 'w1', 'w2', 'shared_w1', 'shared_w2')}
    del _L0_ffn_all
    return {'x': x, 'ctx_1024': ctx_1024, 'mask_BxS2_bf1': mask_BxS2_bf1, 'L0_xattn_Wq': _L0_xattn_in['Wq'], 'L0_xattn_Wk': _L0_xattn_in['Wk'], 'L0_xattn_Wv': _L0_xattn_in['Wv'], 'L0_xattn_Wo': _L0_xattn_in['Wo'], 'L0_attn_mask': _L0_attn_in['mask'], 'L0_attn_in_proj_w': _L0_attn_in['in_proj_w'], 'L0_attn_conv_w': _L0_attn_in['conv_w'], 'L0_attn_conv_b': _L0_attn_in['conv_b'], 'L0_attn_A_log': _L0_attn_in['A_log'], 'L0_attn_dt_bias': _L0_attn_in['dt_bias'], 'L0_attn_D': _L0_attn_in['D'], 'L0_attn_norm_w': _L0_attn_in['norm_w'], 'L0_attn_out_proj_w': _L0_attn_in['out_proj_w'], 'L0_ffn_gate_w': _L0_ffn_in['gate_w'], 'L0_ffn_w1': _L0_ffn_in['w1'], 'L0_ffn_w2': _L0_ffn_in['w2'], 'L0_ffn_shared_w1': _L0_ffn_in['shared_w1'], 'L0_ffn_shared_w2': _L0_ffn_in['shared_w2']}

def reference(x, ctx_1024, mask_BxS2_bf1, L0_xattn_Wq, L0_xattn_Wk, L0_xattn_Wv, L0_xattn_Wo, L0_attn_mask, L0_attn_in_proj_w, L0_attn_conv_w, L0_attn_conv_b, L0_attn_A_log, L0_attn_dt_bias, L0_attn_D, L0_attn_norm_w, L0_attn_out_proj_w, L0_ffn_gate_w, L0_ffn_w1, L0_ffn_w2, L0_ffn_shared_w1, L0_ffn_shared_w2):
    import jax
    import jax.numpy as jnp

    def _L0_xattn_ref(text_hidden, vision_tokens, vision_mask, Wq, Wk, Wv, Wo):
        import jax, jax.numpy as jnp
        import numpy as np
        N_HEADS = 16
        N_KV_HEADS = 8
        HEAD_DIM = 128
        D_TEXT = 1024
        D_VISION = 512
        GROUPS = N_HEADS // N_KV_HEADS
        B, T_text, _ = text_hidden.shape
        T_vis = vision_tokens.shape[1]
        scale = jnp.float32(np.sqrt(HEAD_DIM))
        q = (text_hidden @ Wq).reshape(B, T_text, N_HEADS, HEAD_DIM).transpose(0, 2, 1, 3)
        k = (vision_tokens @ Wk).reshape(B, T_vis, N_KV_HEADS, HEAD_DIM).transpose(0, 2, 1, 3)
        v = (vision_tokens @ Wv).reshape(B, T_vis, N_KV_HEADS, HEAD_DIM).transpose(0, 2, 1, 3)
        k = jnp.repeat(k, GROUPS, axis=1)
        v = jnp.repeat(v, GROUPS, axis=1)
        scores = jnp.einsum('bhtd,bhsd->bhts', q, k) / scale
        mask = vision_mask[:, None, None, :]
        scores = jnp.where(mask, scores, -jnp.inf)
        attn = jax.nn.softmax(scores, axis=-1)
        attn = jnp.nan_to_num(attn, nan=0.0)
        out = jnp.einsum('bhts,bhsd->bhtd', attn, v)
        out = out.transpose(0, 2, 1, 3).reshape(B, T_text, N_HEADS * HEAD_DIM)
        return out @ Wo

    def _L0_attn_ref(input_states, mask, in_proj_w, conv_w, conv_b, A_log, dt_bias, D, norm_w, out_proj_w):
        import jax, jax.numpy as jnp
        import numpy as np
        B_, S_, E_ = (2, 1024, 1024)
        H_, P_, N_, G_, K_, CH_ = (64, 64, 128, 1, 4, 128)
        INTER = H_ * P_
        CONV_DIM = INTER + 2 * G_ * N_
        PROJ = INTER + CONV_DIM + H_
        EPS = 1e-05

        def segsum(x):
            T = x.shape[-1]
            xe = jnp.broadcast_to(x[..., None], x.shape + (T,))
            m_excl = jnp.tril(jnp.ones((T, T), bool), -1)
            s = jnp.cumsum(jnp.where(m_excl, xe, 0.0), axis=-2)
            m_incl = jnp.tril(jnp.ones((T, T), bool), 0)
            return jnp.where(m_incl, s, -jnp.inf)

        def ssm_forward(input_states, in_proj_w, conv_w, conv_b, A_log, dt_bias, D, norm_w, out_proj_w):
            b, s, _ = input_states.shape
            proj = input_states @ in_proj_w.T
            gate, hBC, dt = jnp.split(proj, [INTER, INTER + CONV_DIM], axis=-1)
            x = hBC.transpose(0, 2, 1)
            x = jax.lax.conv_general_dilated(x, conv_w, (1,), [(K_ - 1, 0)], dimension_numbers=('NCH', 'OIH', 'NCH'), feature_group_count=CONV_DIM)
            hBC = jax.nn.silu((x + conv_b[None, :, None]).transpose(0, 2, 1))
            hs, Bmat, Cmat = jnp.split(hBC, [INTER, INTER + G_ * N_], axis=-1)
            A = -jnp.exp(A_log)
            dt = jax.nn.softplus(dt + dt_bias)
            xh = hs.reshape(b, s, H_, P_)
            Bf = jnp.repeat(Bmat.reshape(b, s, G_, N_), H_ // G_, axis=2)
            Cf = jnp.repeat(Cmat.reshape(b, s, G_, N_), H_ // G_, axis=2)
            D_res = D[:, None] * xh
            xh = xh * dt[..., None]
            Adt = A[None, None, :] * dt
            nch = s // CH_
            xc = xh.reshape(b, nch, CH_, H_, P_)
            Bc = Bf.reshape(b, nch, CH_, H_, N_)
            Cc = Cf.reshape(b, nch, CH_, H_, N_)
            Ac = Adt.reshape(b, nch, CH_, H_).transpose(0, 3, 1, 2)
            A_cum = jnp.cumsum(Ac, axis=-1)
            L = jnp.exp(segsum(Ac))
            Gm = jnp.einsum('bclhn,bcshn->bclsh', Cc, Bc)
            M = Gm * L.transpose(0, 2, 3, 4, 1)
            Y_diag = jnp.einsum('bclsh,bcshp->bclhp', M, xc)
            decay_states = jnp.exp(A_cum[..., -1:] - A_cum)
            states = jnp.einsum('bclhn,bhcl,bclhp->bchpn', Bc, decay_states, xc)
            states = jnp.concatenate([jnp.zeros_like(states[:, :1]), states], axis=1)
            A_last = jnp.pad(A_cum[..., -1], ((0, 0), (0, 0), (1, 0)))
            decay_chunk = jnp.exp(segsum(A_last))
            new_states = jnp.einsum('bhij,bjhpn->bihpn', decay_chunk, states)
            states = new_states[:, :-1]
            state_decay = jnp.exp(A_cum)
            Y_off = jnp.einsum('bclhn,bchpn,bhcl->bclhp', Cc, states, state_decay)
            y = (Y_diag + Y_off).reshape(b, s, H_, P_) + D_res
            y = y.reshape(b, s, INTER)
            yg = y * jax.nn.silu(gate)
            var = jnp.mean(yg * yg, axis=-1, keepdims=True)
            yn = norm_w * (yg * jax.lax.rsqrt(var + EPS))
            return yn @ out_proj_w.T
        return ssm_forward(input_states, in_proj_w, conv_w, conv_b, A_log, dt_bias, D, norm_w, out_proj_w)

    def _L0_ffn_ref(x, gate_w, w1, w2, shared_w1, shared_w2):
        import jax, jax.numpy as jnp
        import numpy as np
        H, I, E, TOP_K = (1024, 704, 16, 6)
        IS = 1408
        NORM_TOPK_PROB = False

        def _silu_and_mul(gate_up):
            d = gate_up.shape[-1] // 2
            g, u = (gate_up[..., :d], gate_up[..., d:])
            return jax.nn.silu(g) * u
        B, S, Hd = x.shape
        xf = x.reshape(-1, Hd)
        T = xf.shape[0]
        shared_out = _silu_and_mul(xf @ shared_w1.T) @ shared_w2.T
        logits = xf @ gate_w.T
        probs = jax.nn.softmax(logits.astype(jnp.float32), axis=-1)
        routing_weights, selected = jax.lax.top_k(probs, TOP_K)
        if NORM_TOPK_PROB:
            routing_weights = routing_weights / routing_weights.sum(-1, keepdims=True)
        combine = jnp.zeros((T, E), jnp.float32).at[jnp.arange(T)[:, None], selected].add(routing_weights).astype(x.dtype)
        gate_up = jnp.einsum('th,eoh->teo', xf, w1)
        act = _silu_and_mul(gate_up)
        moe_out = jnp.einsum('te,tei,ehi->th', combine, act, w2)
        return (moe_out + shared_out).reshape(B, S, Hd)
    x = x + _L0_xattn_ref(_layernorm(x, axis=-1), ctx_1024, mask_BxS2_bf1, L0_xattn_Wq, L0_xattn_Wk, L0_xattn_Wv, L0_xattn_Wo)
    x = x + _L0_attn_ref(_layernorm(x, axis=-1), L0_attn_mask, L0_attn_in_proj_w, L0_attn_conv_w, L0_attn_conv_b, L0_attn_A_log, L0_attn_dt_bias, L0_attn_D, L0_attn_norm_w, L0_attn_out_proj_w)
    x = x + _L0_ffn_ref(_layernorm(x, axis=-1), L0_ffn_gate_w, L0_ffn_w1, L0_ffn_w2, L0_ffn_shared_w1, L0_ffn_shared_w2)
    return x

_drawn_inputs = setup_inputs


def setup_inputs(seed=0):
    import zlib

    import numpy as np

    out = dict(_drawn_inputs(seed))
    spreads = {'L0_attn_conv_b': (0.0, 0.1),
     'L0_attn_dt_bias': (1.0, 0.56),
     'L0_attn_D': (1.0, 0.2),
     'L0_attn_norm_w': (1.0, 0.2)}
    factors = {'L0_attn_A_log': 2.844, 'L0_ffn_gate_w': 2.811}
    for name, (base, spread) in spreads.items():
        noise = np.random.default_rng([zlib.crc32(name.encode()), seed]).standard_normal(out[name].shape)
        drawn = base * np.exp(spread * noise) if base else spread * noise
        out[name] = jnp.asarray(drawn.astype(out[name].dtype))
    for name, factor in factors.items():
        out[name] = (out[name] * factor).astype(out[name].dtype)
    return out
```

```python
from contextlib import ExitStack

import concourse.bass as bass
from concourse import mybir

ALU = mybir.AluOpType
ACT = mybir.ActivationFunctionType
AX = mybir.AxisListType
F32 = mybir.dt.float32
F32R = mybir.dt.float32r
U8 = mybir.dt.uint8

P = 128
BATCH, SEQ, DM = 2, 128, 1024
KD = DM // P
TOK = BATCH * SEQ
CTX, DC = 2048, 512
KC = DC // P
HD = 128
KVH = 8
SCALE = 1.0 / float(HD) ** 0.5
MASKED = -1.0e30
LOWEST = -3.0e38
INTER, NST, SSM_H, HP = 4096, 128, 64, 64
XB = INTER // P
EXPERTS, TOPK, EI = 16, 6, 704
PAIR = 2 * EI
JB = PAIR // P
PAIRS = EXPERTS // 2
EPS = 1e-5
HALF = 512


class Chain:

    def __init__(self, eng, sem, base=0):
        self.eng, self.sem, self.base, self.n = eng, sem, base, 0

    def link(self, ins):
        self.n += 1
        ins.then_inc(self.sem, 1)
        self.eng.wait_ge(self.sem, self.base + self.n)


def bc(ap, dim, n):
    shape = list(ap.shape)
    shape[dim] = n
    return ap.broadcast_to(shape)


def split3(pe, out, pairs, first, last):
    n = len(pairs)
    for i, ((sh, sl), (mh, ml)) in enumerate(pairs):
        pe.matmul(out, sh, mh, start=first and i == 0, stop=False)
        pe.matmul(out, sh, ml, start=False, stop=False)
        mm = pe.matmul(out, sl, mh, start=False, stop=last and i == n - 1)
    return mm


def layernorm_block(nc, sems, round_, t, load_x=None):
    x_in, chain, var_ready, std_ready, xn_ready, turned, hi_written, lo_written = sems
    two, four = 2 * round_, 4 * round_
    with nc.Block() as block:
        @block.sync
        def _(sp):
            if load_x is not None:
                for b in range(BATCH):
                    sp.dma_start(t.x_res[:, b, :], load_x[b]).then_inc(x_in, 16)

        @block.vector
        def _(dve):
            c = Chain(dve, chain, 5 * round_)
            if load_x is not None:
                dve.wait_ge(x_in, 16 * BATCH)
            c.link(dve.memset(t.eps[:, :], EPS))
            for b in range(BATCH):
                for h in range(2):
                    ins = dve.bn_stats(t.stats[:, b, h, :], t.x_res[:, b, h * HALF:(h + 1) * HALF])
                c.link(ins)
                dve.bn_aggr(t.meanvar[:, b, :], t.stats[:, b, :, :]).then_inc(var_ready, 1)
            for b in range(BATCH):
                dve.wait_ge(std_ready, two + b + 1)
                c.link(dve.reciprocal(t.rstd[:, b:b + 1], t.std[:, b:b + 1]))
                dve.tensor_scalar(t.xn[:, b, :], t.x_res[:, b, :], t.meanvar[:, b, 0:1],
                                  t.rstd[:, b:b + 1], ALU.subtract, ALU.mult).then_inc(xn_ready, 1)
            for b in range(BATCH):
                for g in range(2):
                    n = 2 * b + g
                    dve.wait_ge(hi_written, four + n + 1)
                    bank = t.bank[n][:, :].rearrange("p (k s) -> p k s", k=4)
                    at = (slice(None), slice(4 * g, 4 * g + 4), slice(b * SEQ, (b + 1) * SEQ))
                    dve.tensor_tensor(t.xn_lo[at], bank, t.xn_hi[at].bitcast(F32),
                                      ALU.subtract).then_inc(lo_written, 1)

        @block.scalar
        def _(act):
            for b in range(BATCH):
                act.wait_ge(var_ready, two + b + 1)
                act.activation(t.std[:, b:b + 1], t.meanvar[:, b, 1:2], ACT.Sqrt,
                               bias=t.eps[:, 0:1]).then_inc(std_ready, 1)
            for b in range(BATCH):
                for g in range(2):
                    n = 2 * b + g
                    act.wait_ge(turned, four + n + 1)
                    bank = t.bank[n][:, :].rearrange("p (k s) -> p k s", k=4)
                    act.activation(t.xn_hi[:, 4 * g:4 * g + 4, b * SEQ:(b + 1) * SEQ], bank,
                                   ACT.Copy).then_inc(hi_written, 1)

        @block.tensor
        def _(pe):
            for b in range(BATCH):
                pe.wait_ge(xn_ready, two + b + 1)
                for g in range(2):
                    for k in range(4):
                        at = (4 * g + k) * P
                        mm = pe.transpose(t.bank[2 * b + g][:, k * P:(k + 1) * P],
                                          t.xn[:, b, at:at + P], t.ident[:, :])
                    mm.then_inc(turned, 1)


def attention_block(nc, sem, ctx_in, mask, Wq, Wk, Wv, Wo, t, a):
    LOOP = KVH - 1
    ctx_loaded = [sem("ctx_loaded0"), sem("ctx_loaded1")]
    ctx_turned, ctx_hi, ctx_lo = (sem(f"ctx_{x}") for x in ("turned", "hi", "lo"))
    mask_loaded, mask_ready = sem("mask_loaded"), sem("mask_ready")
    kv_loaded, kv_hi, kv_lo = sem("kv_loaded"), sem("kv_hi"), sem("kv_lo")
    wq_loaded, wq_hi, wq_lo = sem("wq_loaded"), sem("wq_hi"), sem("wq_lo")
    wo_loaded, wo_hi, wo_lo = sem("wo_loaded"), sem("wo_hi"), sem("wo_lo")
    k_filled, k_hi, k_lo = sem("k_filled"), sem("k_hi"), sem("k_lo")
    q_filled, q_hi, q_lo = sem("q_filled"), sem("q_hi"), sem("q_lo")
    v_filled, v_raw, vt_filled, vt_hi, vt_lo = (sem(x) for x in ("v_filled", "v_raw", "vt_filled", "vt_hi", "vt_lo"))
    scores_filled, scores_read, negmax_ready, exp_done = (
        sem(x) for x in ("scores_filled", "scores_read", "negmax_ready", "exp_done"))
    diag_ready, rb_filled, rb_read = sem("diag_ready"), sem("rb_filled"), sem("rb_read")
    pt_filled, pt_hi, pt_lo = sem("pt_filled"), sem("pt_hi"), sem("pt_lo")
    pv_filled, ot_ready, ot_hi, ot_lo = sem("pv_filled"), sem("ot_ready"), sem("ot_hi"), sem("ot_lo")
    out_filled, out_read, zeroed = sem("out_filled"), sem("out_read"), sem("att_zeroed")
    chain, max_done, rinv_done = sem("att_chain"), sem("max_done"), sem("rinv_done")
    S = [t.bank[3], t.bank[4]]
    J = [t.bank[5], t.bank[6]]
    PTB = [S[0], S[1], J[1]]
    R = t.bank[7]
    PVB = t.bank[2]
    CH = CTX // HALF
    SB = CTX // P
    GR = SB // 2

    with nc.Block() as block:
        @block.sync
        def _(sp):
            def load_kv(n, g):
                sp.wait_ge(kv_lo, n + 1)
                for i, w in enumerate((Wk, Wv)):
                    src = w.rearrange("(k p) n -> p k n", p=P)[:, :, bass.ds(g * HD, HD)]
                    sp.dma_start(a.kv_nat[:, i, :, :], src).then_inc(kv_loaded, 16)

            def load_wq(n, g, first=False):
                if not first:
                    sp.wait_ge(wq_lo, n + 1)
                    sp.wait_ge(wo_lo, n + 1)
                src = Wq.rearrange("(k p) n -> p k n", p=P)[:, :, bass.ds(g * 2 * HD, 2 * HD)]
                sp.dma_start(a.w_nat[:, :].rearrange("p (k n) -> p k n", k=KD), src).then_inc(wq_loaded, 16)

            def load_wo(n, g, last=False):
                if last:
                    sp.wait_ge(wo_lo, n + 2)
                else:
                    sp.wait_ge(wq_lo, n + 3)
                src = Wo.rearrange("(m p) n -> p m n", p=P)[:, bass.ds(g * 2, 2), :]
                sp.dma_start(a.w_nat[:, :].rearrange("p (j n) -> p j n", j=2), src).then_inc(wo_loaded, 16)

            for b in range(BATCH):
                n0 = KVH * b
                if b:
                    sp.wait_ge(mask_ready, 1)
                sp.dma_start(a.mask_raw[:, :], bc(mask[b:b + 1, :], 0, P)).then_inc(mask_loaded, 16)
                for i in range(SB // 2):
                    m = 8 * b + i
                    if i >= 2:
                        sp.wait_ge(ctx_turned, 2 * (m - 2) + 2)
                    elif b:
                        sp.wait_ge(wo_lo, n0 + 2)
                    dst = a.w_nat[:, (i % 2) * DM:(i % 2 + 1) * DM].rearrange("p (r c) -> p r c", r=2)
                    src = ctx_in[b, i * 2 * P:(i + 1) * 2 * P, :].rearrange("(r p) c -> p r c", p=P)
                    sp.dma_start(dst, src).then_inc(ctx_loaded[i % 2], 16)
                load_kv(n0, 0)
                sp.wait_ge(ctx_turned, SB * (b + 1))
                load_wq(n0, 0, first=True)
                with sp.Fori(0, LOOP) as g:
                    load_kv(g + (n0 + 1), g + 1)
                    load_wq(g + (n0 + 1), g + 1)
                    load_wo(g + n0, g)
                load_wo(n0 + LOOP, LOOP, last=True)

        @block.gpsimd
        def _(pool):
            def lo_of(lo, nat, hi, sem_done):
                pool.tensor_tensor(lo, nat, hi.bitcast(F32), ALU.subtract).then_inc(sem_done, 1)

            def split_kv(n):
                pool.wait_ge(kv_hi, n + 2)
                lo_of(a.kv_lo[:, :, :, :], a.kv_nat[:, :, :, :], a.kv_hi[:, :, :, :], kv_lo)

            def split_wq(n):
                pool.wait_ge(wq_hi, n + 2)
                lo_of(a.w_lo[:, :], a.w_nat[:, :], a.w_hi[:, :], wq_lo)

            def split_wo(n):
                pool.wait_ge(wo_hi, n + 2)
                lo_of(a.w_lo[:, :], a.w_nat[:, :], a.w_hi[:, :], wo_lo)

            pool.sem_inc(kv_lo, 1)
            pool.sem_inc(wq_lo, 1)
            pool.sem_inc(wo_lo, 2)
            for b in range(BATCH):
                n0 = KVH * b
                split_kv(n0)
                split_wq(n0)
                with pool.Fori(0, LOOP) as g:
                    split_kv(g + n0 + 1)
                    split_wq(g + n0 + 1)
                    split_wo(g + n0)
                split_wo(n0 + LOOP)

        @block.scalar
        def _(act):
            def split_kv(n):
                act.wait_ge(kv_loaded, 32 * n + 32)
                act.wait_ge(v_filled, 4 * n + 1)
                act.activation(a.kv_hi[:, :, :, :], a.kv_nat[:, :, :, :], ACT.Copy).then_inc(kv_hi, 1)

            def split_wq(n, first=False):
                act.wait_ge(wq_loaded, 16 * n + 16)
                act.wait_ge(out_filled, n + 1 if first else n)
                if not first:
                    act.wait_ge(q_filled, n)
                act.activation(a.w_hi[:, :], a.w_nat[:, :], ACT.Copy).then_inc(wq_hi, 1)

            def split_wo(n, last=False):
                act.wait_ge(wo_loaded, 16 * n + 16)
                if last:
                    act.wait_ge(out_filled, n + 1)
                else:
                    act.wait_ge(q_filled, n + 2)
                act.activation(a.w_hi[:, :], a.w_nat[:, :], ACT.Copy).then_inc(wo_hi, 1)

            def hi_k(n, chunks=range(CH)):
                for c in chunks:
                    act.wait_ge(k_filled, CH * n + c + 1)
                    act.activation(a.k_hi[:, c * HALF:(c + 1) * HALF], J[c % 2][:, :], ACT.Copy).then_inc(k_hi, 1)

            def hi_q(n):
                act.wait_ge(q_filled, n + 1)
                act.activation(a.q_hi[:, :], J[0][:, 0:2 * HD], ACT.Copy).then_inc(q_hi, 1)

            def raw_v(n, c):
                act.wait_ge(v_filled, CH * n + c + 2)
                act.wait_ge(vt_filled, CH * n + c + 1)
                act.activation(a.v_stage[:, c % 2, :], J[(c + 1) % 2][:, :], ACT.Copy).then_inc(v_raw, 1)

            def hi_v(n, c):
                act.wait_ge(vt_filled, CH * n + c + 3)
                act.activation(a.v_hi[:, 4 * c:4 * c + 4, :],
                               R[:, :].rearrange("p (r d) -> p r d", r=4), ACT.Copy).then_inc(vt_hi, 1)

            def v_steps(n):
                raw_v(n, 0)
                for c in range(1, CH):
                    raw_v(n, c)
                    hi_v(n, c - 1)
                hi_v(n, CH - 1)

            def softmax(n, j):
                act.wait_ge(negmax_ready, 2 * n + (j + 1))
                act.activation(a.p[:, j, :], a.p[:, j, :], ACT.Exp, bias=a.negmax[:, j:j + 1],
                               scale=SCALE, accum_out=a.psum[:, j:j + 1]).then_inc(exp_done, 1)

            def weigh_steps(n, last=False):
                for r in range(GR):
                    act.wait_ge(pt_filled, GR * n + r + 1)
                    act.activation(a.pt_hi[:, r % 3, :], PTB[r % 3][:, :], ACT.Copy).then_inc(pt_hi, 1)
                act.wait_ge(rb_filled, n + 1)
                act.activation(a.rb[:, :], R[:, 0:2 * SEQ], ACT.Copy).then_inc(rb_read, 1)
                split_wo(n, last)
                act.wait_ge(ot_ready, n + 1)
                act.activation(a.ot_hi[:, :], a.ot[:, :], ACT.Copy).then_inc(ot_hi, 1)

            act.sem_inc(kv_hi, 1)
            act.sem_inc(wq_hi, 1)
            act.sem_inc(wo_hi, 1)
            act.sem_inc(v_raw, 1)
            for b in range(BATCH):
                n0 = KVH * b
                for i in range(SB):
                    u = SB * b + i
                    act.wait_ge(ctx_turned, u + 1)
                    act.activation(a.ctx_hi[:, :, i * P:(i + 1) * P],
                                   t.bank[2 + i % 4][:, :].rearrange("p (c s) -> p c s", c=KC),
                                   ACT.Copy).then_inc(ctx_hi, 1)
                split_kv(n0)
                split_wq(n0, first=True)
                hi_k(n0)
                hi_q(n0)
                v_steps(n0)
                with act.Fori(0, LOOP) as g:
                    n = g + n0
                    split_kv(n + 1)
                    split_wq(n + 1)
                    softmax(n, 0)
                    hi_k(n + 1, range(1))
                    softmax(n, 1)
                    hi_k(n + 1, range(1, CH))
                    hi_q(n + 1)
                    weigh_steps(n)
                    v_steps(n + 1)
                softmax(n0 + LOOP, 0)
                softmax(n0 + LOOP, 1)
                weigh_steps(n0 + LOOP, last=True)

        @block.vector
        def _(dve):
            c = Chain(dve, chain)
            dve.sem_inc(pt_lo, 1)

            def lo_k(n, chunks=range(CH)):
                for ch in chunks:
                    dve.wait_ge(k_hi, CH * n + ch + 1)
                    at = slice(ch * HALF, (ch + 1) * HALF)
                    dve.tensor_tensor(a.k_lo[:, at], J[ch % 2][:, :], a.k_hi[:, at].bitcast(F32),
                                      ALU.subtract).then_inc(k_lo, 1)

            def lo_q(n):
                dve.wait_ge(q_hi, n + 1)
                dve.tensor_tensor(a.q_lo[:, :], J[0][:, 0:2 * HD], a.q_hi[:, :].bitcast(F32),
                                  ALU.subtract).then_inc(q_lo, 1)

            def lo_v(n):
                for ch in range(CH):
                    dve.wait_ge(vt_hi, CH * n + ch + 1)
                    at = (slice(None), slice(4 * ch, 4 * ch + 4), slice(None))
                    dve.tensor_tensor(a.v_lo[at], R[:, :].rearrange("p (r d) -> p r d", r=4),
                                      a.v_hi[at].bitcast(F32), ALU.subtract).then_inc(vt_lo, 1)

            def scores(n):
                for j in range(2):
                    for ch in range(CH):
                        u = j * CH + ch
                        dve.wait_ge(scores_filled, 2 * CH * n + u + 1)
                        dve.memset(a.mark[:, u:u + 1], 0.0)
                        at = slice(ch * HALF, (ch + 1) * HALF)
                        dve.tensor_tensor_reduce(out=a.p[:, j, at], in0=S[u % 2][:, :], in1=a.mask_bias[:, at],
                                                 scale=1.0, scalar=LOWEST, op0=ALU.add, op1=ALU.max,
                                                 accum_out=a.chunkmax[:, u:u + 1]).then_inc(scores_read, 1)
                    dve.wait_ge(scores_read, 2 * CH * n + (j + 1) * CH)
                    dve.tensor_reduce(a.rowmax[:, j:j + 1], a.chunkmax[:, j * CH:(j + 1) * CH], AX.X,
                                      ALU.max).then_inc(max_done, 1)
                    dve.wait_ge(max_done, 2 * n + (j + 1))
                    dve.tensor_scalar(a.negmax[:, j:j + 1], a.rowmax[:, j:j + 1], -SCALE, None,
                                      ALU.mult).then_inc(negmax_ready, 1)

            def inverse_sum(n, b):
                dve.wait_ge(exp_done, 2 * n + 2)
                dve.reciprocal(a.rinv[:, :], a.psum[:, :]).then_inc(rinv_done, 1)
                dve.wait_ge(rinv_done, 2 * n + 1)
                dve.tensor_scalar(a.rinv[:, :], a.rinv[:, :], a.any_valid[:, b:b + 1], None,
                                  ALU.mult).then_inc(rinv_done, 1)
                dve.wait_ge(rinv_done, 2 * n + 2)
                for j in range(2):
                    dve.tensor_scalar(a.diag[:, j * SEQ:(j + 1) * SEQ], t.ident[:, :], a.rinv[:, j:j + 1],
                                      None, ALU.mult).then_inc(diag_ready, 1)

            def pv_steps(n):
                for r in range(GR):
                    dve.wait_ge(pt_hi, GR * n + r + 1)
                    dve.tensor_tensor(a.pt_lo[:, r % 3, :], PTB[r % 3][:, :],
                                      a.pt_hi[:, r % 3, :].bitcast(F32), ALU.subtract).then_inc(pt_lo, 1)
                dve.wait_ge(pv_filled, n + 1)
                dve.wait_ge(rb_read, n + 1)
                dve.tensor_tensor(a.ot[:, :], PVB[:, 0:2 * SEQ], a.rb[:, :], ALU.mult).then_inc(ot_ready, 1)
                dve.wait_ge(ot_hi, n + 1)
                dve.tensor_tensor(a.ot_lo[:, :], a.ot[:, :], a.ot_hi[:, :].bitcast(F32),
                                  ALU.subtract).then_inc(ot_lo, 1)

            for b in range(BATCH):
                n0 = KVH * b
                dve.wait_ge(mask_loaded, 16 * (b + 1))
                dve.tensor_copy(a.mask_bias[:, :], a.mask_raw[:, :]).then_inc(mask_ready, 1)
                dve.wait_ge(mask_ready, b + 1)
                c.link(dve.tensor_reduce(a.any_valid[:, b:b + 1], a.mask_bias[:, :], AX.X, ALU.max))
                c.link(dve.tensor_scalar(a.mask_bias[:, :], a.mask_bias[:, :], 1.0, -MASKED,
                                         ALU.subtract, ALU.mult))
                for i in range(SB):
                    dve.wait_ge(ctx_hi, SB * b + i + 1)
                    at = (slice(None), slice(None), slice(i * P, (i + 1) * P))
                    dve.tensor_tensor(a.ctx_lo[at], t.bank[2 + i % 4][:, :].rearrange("p (c s) -> p c s", c=KC),
                                      a.ctx_hi[at].bitcast(F32), ALU.subtract).then_inc(ctx_lo, 1)
                lo_k(n0)
                lo_q(n0)
                lo_v(n0)
                with dve.Fori(0, LOOP) as g:
                    n = g + n0
                    scores(n)
                    lo_k(n + 1, range(2))
                    inverse_sum(n, b)
                    lo_k(n + 1, range(2, CH))
                    lo_q(n + 1)
                    pv_steps(n)
                    lo_v(n + 1)
                scores(n0 + LOOP)
                inverse_sum(n0 + LOOP, b)
                pv_steps(n0 + LOOP)
                dve.wait_ge(out_filled, KVH * (b + 1) + 1)
                for h in range(2):
                    at = slice(h * HALF, (h + 1) * HALF)
                    dve.tensor_tensor(t.x_res[:, b, at], t.bank[h][:, :], t.x_res[:, b, at],
                                      ALU.add).then_inc(out_read, 1)

        @block.tensor
        def _(pe):
            def project_k(n):
                pe.wait_ge(kv_lo, n + 2)
                for c in range(CH):
                    if c < 2:
                        pe.wait_ge(v_raw, CH * n + 1)
                    else:
                        pe.wait_ge(k_lo, CH * n + (c - 1))
                    at = slice(c * HALF, (c + 1) * HALF)
                    split3(pe, J[c % 2][:, :], [((a.kv_hi[:, 0, k, :], a.kv_lo[:, 0, k, :]),
                                                 (a.ctx_hi[:, k, at], a.ctx_lo[:, k, at])) for k in range(KC)],
                           True, True).then_inc(k_filled, 1)

            def project_q(n, b):
                pe.wait_ge(wq_lo, n + 2)
                pe.wait_ge(k_lo, CH * n + 4)
                at = slice(b * SEQ, (b + 1) * SEQ)
                for j in range(2):
                    ws = [slice(k * 2 * HD + j * HD, k * 2 * HD + (j + 1) * HD) for k in range(KD)]
                    mm = split3(pe, J[0][:, j * SEQ:(j + 1) * SEQ],
                                [((a.w_hi[:, ws[k]], a.w_lo[:, ws[k]]),
                                  (t.xn_hi[:, k, at], t.xn_lo[:, k, at])) for k in range(KD)], True, True)
                mm.then_inc(q_filled, 1)

            def project_v(n, first=False, out_before_last_turn=None):
                def chunk(c):
                    if c < 2:
                        pe.wait_ge(q_lo, n + 1)
                    else:
                        pe.wait_ge(v_raw, CH * n + c)
                    at = slice(c * HALF, (c + 1) * HALF)
                    split3(pe, J[(c + 1) % 2][:, :], [((a.kv_hi[:, 1, k, :], a.kv_lo[:, 1, k, :]),
                                                       (a.ctx_hi[:, k, at], a.ctx_lo[:, k, at])) for k in range(KC)],
                           True, True).then_inc(v_filled, 1)

                def turn(c):
                    pe.wait_ge(v_raw, CH * n + c + 2)
                    if c > 0:
                        pe.wait_ge(vt_lo, CH * n + c)
                    elif not first:
                        pe.wait_ge(rb_read, n)
                    for r in range(4):
                        mm = pe.transpose(R[:, r * P:(r + 1) * P], a.v_stage[:, c % 2, r * P:(r + 1) * P],
                                          t.ident[:, :])
                    mm.then_inc(vt_filled, 1)
                chunk(0)
                for c in range(1, CH):
                    chunk(c)
                    turn(c - 1)
                if out_before_last_turn is not None:
                    project_out(out_before_last_turn, False)
                turn(CH - 1)

            def scores(n):
                pe.wait_ge(k_lo, CH * n + CH)
                pe.wait_ge(q_lo, n + 1)
                for j in range(2):
                    for c in range(CH):
                        u = j * CH + c
                        if u < 2:
                            pe.wait_ge(pt_lo, GR * n + 1)
                        else:
                            pe.wait_ge(scores_read, 2 * CH * n + u - 1)
                        qs, at = slice(j * SEQ, (j + 1) * SEQ), slice(c * HALF, (c + 1) * HALF)
                        split3(pe, S[u % 2][:, :], [((a.q_hi[:, qs], a.q_lo[:, qs]),
                                                     (a.k_hi[:, at], a.k_lo[:, at]))],
                               True, True).then_inc(scores_filled, 1)

            def broadcast_inverse(n):
                pe.wait_ge(diag_ready, 2 * n + 2)
                pe.wait_ge(vt_lo, CH * n + CH)
                pe.matmul(R[:, 0:2 * SEQ], t.ones[:, :], a.diag[:, :], start=True, stop=True).then_inc(rb_filled, 1)

            def weigh_values(n):
                def turn(r):
                    if r >= 3:
                        pe.wait_ge(pt_lo, GR * n + r - 1)
                    for q in range(2):
                        for j in range(2):
                            s = (2 * r + q) * P
                            mm = pe.transpose(PTB[r % 3][:, (2 * q + j) * P:(2 * q + j + 1) * P],
                                              a.p[:, j, s:s + P], t.ident[:, :])
                    mm.then_inc(pt_filled, 1)

                def weigh(r):
                    pe.wait_ge(pt_lo, GR * n + r + 2)
                    pairs = [((a.v_hi[:, 2 * r + q, :], a.v_lo[:, 2 * r + q, :]),
                              (a.pt_hi[:, r % 3, q * 2 * SEQ:(q + 1) * 2 * SEQ],
                               a.pt_lo[:, r % 3, q * 2 * SEQ:(q + 1) * 2 * SEQ])) for q in range(2)]
                    return split3(pe, PVB[:, 0:2 * SEQ], pairs, r == 0, r == GR - 1)
                pe.wait_ge(exp_done, 2 * n + 2)
                for r in range(3):
                    turn(r)
                for r in range(GR):
                    if r == 5:
                        broadcast_inverse(n)
                    mm = weigh(r)
                    if r + 3 < GR:
                        turn(r + 3)
                mm.then_inc(pv_filled, 1)

            def project_out(n, last):
                pe.wait_ge(wo_lo, n + 3)
                pe.wait_ge(ot_lo, n + 1)
                for j in range(2):
                    at = slice(j * SEQ, (j + 1) * SEQ)
                    for h in range(2):
                        w = slice(j * DM + h * HALF, j * DM + (h + 1) * HALF)
                        mm = split3(pe, t.bank[h][:, :], [((a.ot_hi[:, at], a.ot_lo[:, at]),
                                                           (a.w_hi[:, w], a.w_lo[:, w]))],
                                    False, last and j == 1)
                mm.then_inc(out_filled, 1)

            pe.sem_inc(out_filled, 1)
            pe.sem_inc(v_filled, 1)
            pe.sem_inc(vt_filled, 2)
            for b in range(BATCH):
                n0 = KVH * b
                if b:
                    pe.wait_ge(out_read, 2 * b)
                for h in range(2):
                    pe.matmul(t.bank[h][:, :], t.zeros[:, :], t.xn_hi[:, 0:2, :], start=True, stop=False)
                for i in range(SB):
                    u = SB * b + i
                    pe.wait_ge(ctx_loaded[i // 2 % 2], 16 * (SB // 4 * b + i // 4 + 1))
                    if i >= 4:
                        pe.wait_ge(ctx_lo, u - 3)
                    elif b:
                        pe.wait_ge(ot_lo, n0)
                        pe.wait_ge(pt_lo, GR * n0 + 1)
                    half = a.w_nat[:, (i // 2 % 2) * DM + (i % 2) * DC:(i // 2 % 2) * DM + (i % 2 + 1) * DC]
                    for c in range(KC):
                        mm = pe.transpose(t.bank[2 + i % 4][:, c * P:(c + 1) * P], half[:, c * P:(c + 1) * P],
                                          t.ident[:, :])
                    mm.then_inc(ctx_turned, 1)
                pe.wait_ge(ctx_lo, SB * (b + 1))
                project_k(n0)
                project_q(n0, b)
                project_v(n0, first=b == 0)
                with pe.Fori(0, LOOP) as g:
                    n = g + n0
                    scores(n)
                    project_k(n + 1)
                    project_q(n + 1, b)
                    weigh_values(n)
                    project_v(n + 1, out_before_last_turn=n)
                scores(n0 + LOOP)
                weigh_values(n0 + LOOP)
                project_out(n0 + LOOP, True)


T_CREDIT, LO_CREDIT = 12, 2


class Turn:

    def __init__(self, sem, t, f, name, slots):
        self.t, self.f = t, f
        self.turned, self.hi, self.lo = sem(name + "_turned"), sem(name + "_hi"), sem(name + "_lo")
        self.loaded = [[sem(f"{name}_loaded{w}_{s}") for s in range(slots)] for w in range(3)]

    def tensor(self, pe, m, w, s, loaded):
        pe.wait_ge(self.loaded[w][s], loaded)
        for half in range(2):
            pe.wait_ge(self.lo, 6 * m + (2 * w + half + 1))
            for r in range(4):
                mm = pe.transpose(self.t.bank[4 + half][:, r * P:(r + 1) * P],
                                  self.f.nat[:, s, w, (4 * half + r) * P:(4 * half + r + 1) * P],
                                  self.t.ident[:, :])
            mm.then_inc(self.turned, 1)

    def scalar(self, act, m, w, s):
        for half in range(2):
            act.wait_ge(self.turned, 6 * m + (2 * w + half + 1 + T_CREDIT))
            act.activation(self.f.w_hi[:, s, w, half * HALF:(half + 1) * HALF],
                           self.t.bank[4 + half][:, :], ACT.Copy).then_inc(self.hi, 1)

    def vector(self, dve, m, w, s):
        for half in range(2):
            at = (slice(None), s, w, slice(half * HALF, (half + 1) * HALF))
            dve.wait_ge(self.hi, 6 * m + (2 * w + half + 1))
            dve.tensor_tensor(self.f.w_lo[at], self.t.bank[4 + half][:, :],
                              self.f.w_hi[at].bitcast(F32), ALU.subtract).then_inc(self.lo, 1)

    def stage_free(self, sp, m):
        sp.wait_ge(self.turned, 6 * m + 6)

    def ready(self, pe, m, w):
        pe.wait_ge(self.lo, 6 * m + (2 * w + 2 + LO_CREDIT))

    def project(self, pe, out, w, s):
        f, t = self.f, self.t
        ks = [slice(k * P, (k + 1) * P) for k in range(KD)]
        return split3(pe, out, [((f.w_hi[:, s, w, ks[k]], f.w_lo[:, s, w, ks[k]]),
                                 (t.xn_hi[:, k, :], t.xn_lo[:, k, :])) for k in range(KD)], True, True)

    def accumulate(self, pe, hi, lo, s, last):
        for b in range(BATCH):
            rows = slice(b * SEQ, (b + 1) * SEQ)
            for h in range(2):
                at = slice(h * HALF, (h + 1) * HALF)
                mm = split3(pe, self.t.bank[2 * b + h][:, :],
                            [((hi[:, rows], lo[:, rows]), (self.f.w_hi[:, s, 2, at], self.f.w_lo[:, s, 2, at]))],
                            False, last)
        return mm

    def zero_sums(self, pe):
        for n in range(4):
            pe.matmul(self.t.bank[n][:, :], self.t.zeros[:, :], self.t.xn_hi[:, 0:2, :], start=True, stop=False)


def mixer_head_block(nc, sem, in_proj, conv_w, conv_b, A_log, dt_bias, D, norm_w, t, m):
    nat, wh, wl = m.nat, m.w_hi, m.w_lo
    tiles, consts = [sem(f"head_tile{w}") for w in range(3)], sem("head_consts")
    turned, hi_w, lo_w = sem("head_turned"), sem("head_hi"), sem("head_lo")
    projected, copied, conved, tanhed, bc_ready = (sem(f"head_{x}") for x in ("proj", "copied", "conved", "tanhed", "bc"))
    g_filled, zdt_ready, exp_dt, w_ready, ln_dt, a_ready, padded, m_zeroed = (
        sem(f"head_{x}") for x in ("g", "zdt", "expdt", "w", "lndt", "a", "padded", "mzero"))
    chain, dtT_ready = sem("head_chain"), sem("head_dtT")
    BANKS = [0, 1, 2, 3, 4]
    with nc.Block() as block:
        @block.sync
        def _(sp):
            r0 = 2 * INTER
            for w, (r, n) in enumerate(((r0, P), (r0 + P, P), (r0 + 2 * P, SSM_H))):
                sp.dma_start(nat[0:n, 0, w, :], in_proj[r:r + n, :]).then_inc(tiles[w], 16)
            sp.dma_start(m.convw[:, :, :], conv_w.rearrange("(i p) o k -> p i (o k)", p=P)).then_inc(consts, 16)
            sp.dma_start(m.convb[:, :], conv_b.rearrange("(i p) -> p i", p=P), allow_slow_non_contiguous=True).then_inc(consts, 16)
            sp.dma_start(m.normw[:, :], norm_w.rearrange("(i p) -> p i", p=P), allow_slow_non_contiguous=True).then_inc(consts, 16)
            for j in range(2):
                src = bc(D.rearrange("(a i two) -> a two i", a=1, two=2)[:, j, :], 0, HP)
                sp.dma_start(m.dcol[j * HP:(j + 1) * HP, :], src, allow_slow_non_contiguous=True).then_inc(consts, 16)
            sp.dma_start(m.dtb[:, :], bc(dt_bias.rearrange("(a h) -> a h", a=1), 0, P)).then_inc(consts, 16)
            sp.dma_start(m.alog[:, :], bc(A_log.rearrange("(a h) -> a h", a=1), 0, P)).then_inc(consts, 16)

        @block.gpsimd
        def _(pool):
            pool.memset(m.xpad[:, :, :], 0.0).then_inc(padded, 1)
            pool.memset(m.xdt[:, :, :, :], 0.0).then_inc(m_zeroed, 1)
            pool.memset(m.sumsq[:, :], 0.0).then_inc(m_zeroed, 1)
            pool.wait_ge(m_zeroed, 2)

        @block.scalar
        def _(act):
            for q in range(5):
                act.wait_ge(turned, q + 1)
                w, half = q // 2, q % 2
                act.activation(wh[:, 0, w, half * HALF:(half + 1) * HALF], t.bank[q][:, :],
                               ACT.Copy).then_inc(hi_w, 1)
            act.wait_ge(padded, 1)
            for n in range(2):
                act.wait_ge(projected, n + 1)
                if n:
                    act.wait_ge(conved, 1)
                act.activation(m.xpad[:, :, 3:3 + SEQ], t.bank[5 + n][:, 0:TOK].rearrange("p (b s) -> p b s", b=BATCH),
                               ACT.Copy).then_inc(copied, 1)
                act.wait_ge(conved, n + 1)
                if n:
                    act.wait_ge(bc_ready, 1)
                act.activation(m.th[:, :], m.z[:, :], ACT.Tanh, scale=0.5).then_inc(tanhed, 1)
            act.wait_ge(zdt_ready, 1)
            act.activation(m.e_dt[:, :, :], m.nabs[:, :, :], ACT.Exp).then_inc(exp_dt, 1)
            act.activation(m.ea[:, :], m.alog[:, :], ACT.Exp).then_inc(exp_dt, 1)
            act.wait_ge(w_ready, 1)
            act.activation(m.ln_dt[:, :, :], m.w_dt[:, :, :], ACT.Ln).then_inc(ln_dt, 1)
            act.wait_ge(a_ready, 1)
            act.activation(m.a_hi[:, :, :], m.a[:, :, :], ACT.Copy).then_inc(ln_dt, 1)

        @block.vector
        def _(dve):
            c = Chain(dve, chain)
            for q in range(5):
                dve.wait_ge(hi_w, q + 1)
                w, half = q // 2, q % 2
                at = (slice(None), 0, w, slice(half * HALF, (half + 1) * HALF))
                dve.tensor_tensor(wl[at], t.bank[q][:, :], wh[at].bitcast(F32), ALU.subtract).then_inc(lo_w, 1)
            dve.wait_ge(projected, 3)
            dve.tensor_copy(m.dtT[:, :], t.bank[7][0:SSM_H, 0:TOK]).then_inc(dtT_ready, 1)
            dve.wait_ge(consts, 16 * 7)
            for n in range(2):
                dve.wait_ge(copied, n + 1)
                if n:
                    dve.wait_ge(bc_ready, 1)
                conv(dve, c, m, XB + n, conved)
                dve.wait_ge(tanhed, n + 1)
                dve.scalar_tensor_tensor(m.bc[:, n, :], m.th[:, :], 1.0, m.z[:, :], ALU.add,
                                         ALU.mult).then_inc(bc_ready, 1)
            dve.wait_ge(projected, 4)
            c.link(dve.tensor_tensor(m.zdt[:, :, :], t.bank[1][:, 0:2 * SSM_H].rearrange("p (b h) -> p b h", b=BATCH),
                                     bc(m.dtb[:, :].rearrange("p (a h) -> p a h", a=1), 1, BATCH), ALU.add))
            dve.scalar_tensor_tensor(m.nabs[:, :, :], m.zdt[:, :, :], -1.0, m.zdt[:, :, :], ALU.mult, ALU.min).then_inc(zdt_ready, 1)
            dve.wait_ge(exp_dt, 1)
            dve.tensor_scalar(m.w_dt[:, :, :], m.e_dt[:, :, :], 1.0, None, ALU.add).then_inc(w_ready, 1)
            dve.wait_ge(w_ready, 1)
            c.link(dve.tensor_scalar(m.d_dt[:, :, :], m.w_dt[:, :, :], 1.0, None, ALU.subtract))
            c.link(dve.tensor_scalar(m.is0[:, :, :], m.d_dt[:, :, :], 0.0, None, ALU.is_equal))
            c.link(dve.tensor_tensor(m.d_dt[:, :, :], m.d_dt[:, :, :], m.is0[:, :, :], ALU.add))
            c.link(dve.reciprocal(m.d_dt[:, :, :], m.d_dt[:, :, :]))
            c.link(dve.tensor_tensor(m.d_dt[:, :, :], m.d_dt[:, :, :], m.e_dt[:, :, :], ALU.mult))
            c.link(dve.tensor_tensor(m.is0[:, :, :], m.is0[:, :, :], m.e_dt[:, :, :], ALU.mult))
            dve.wait_ge(ln_dt, 1)
            c.link(dve.tensor_tensor(m.d_dt[:, :, :], m.d_dt[:, :, :], m.ln_dt[:, :, :], ALU.mult))
            c.link(dve.tensor_tensor(m.d_dt[:, :, :], m.d_dt[:, :, :], m.is0[:, :, :], ALU.add))
            c.link(dve.scalar_tensor_tensor(m.zdt[:, :, :], m.zdt[:, :, :], 0.0, m.d_dt[:, :, :], ALU.max, ALU.add))
            dve.tensor_scalar(m.dth[:, :, :], m.zdt[:, :, :], 0.5, None, ALU.mult)
            dve.wait_ge(exp_dt, 2)
            dve.scalar_tensor_tensor(m.a[:, :, :], m.zdt[:, :, :], -1.0,
                                     bc(m.ea[:, :].rearrange("p (a h) -> p a h", a=1), 1, BATCH),
                                     ALU.mult, ALU.mult).then_inc(a_ready, 1)
            dve.wait_ge(ln_dt, 2)
            dve.tensor_tensor(m.a_lo[:, :, :], m.a[:, :, :], m.a_hi[:, :, :].bitcast(F32), ALU.subtract)
            dve.tensor_scalar(m.dcol[:, :], m.dcol[:, :], 0.5, None, ALU.mult)
            c.link(dve.tensor_scalar(m.normw[:, :], m.normw[:, :], 0.5, None, ALU.mult))
            dve.wait_ge(g_filled, 1)
            c.link(dve.scalar_tensor_tensor(m.gm[:, :, :], t.bank[0][:, 0:TOK].rearrange("p (b s) -> p b s", b=BATCH),
                                            0.25, bc(t.tri[:, :].rearrange("p (a l) -> p a l", a=1), 1, BATCH),
                                            ALU.mult, ALU.mult))

        @block.tensor
        def _(pe):
            for w in range(3):
                n = SSM_H if w == 2 else P
                pe.wait_ge(tiles[w], 16)
                for half in range(1 if w == 2 else 2):
                    blocks = KD if w == 2 else 4
                    for r in range(blocks):
                        k = 4 * half + r
                        mm = pe.transpose(t.bank[2 * w + half][:, r * n:(r + 1) * n],
                                          nat[0:n, 0, w, k * P:(k + 1) * P], t.ident[0:n, 0:n])
                    mm.then_inc(turned, 1)
            for w in range(2):
                pe.wait_ge(lo_w, 2 * w + 2)
                ks = [slice(k * P, (k + 1) * P) for k in range(KD)]
                split3(pe, t.bank[5 + w][:, 0:TOK], [((wh[:, 0, w, ks[k]], wl[:, 0, w, ks[k]]),
                                                       (t.xn_hi[:, k, :], t.xn_lo[:, k, :])) for k in range(KD)],
                       True, True).then_inc(projected, 1)
            pe.wait_ge(lo_w, 5)
            hs = [slice(k * SSM_H, (k + 1) * SSM_H) for k in range(KD)]
            split3(pe, t.bank[7][0:SSM_H, 0:TOK],
                   [((wh[:, 0, 2, hs[k]], wl[:, 0, 2, hs[k]]), (t.xn_hi[:, k, :], t.xn_lo[:, k, :]))
                    for k in range(KD)], True, True).then_inc(projected, 1)
            pe.wait_ge(dtT_ready, 1)
            for b in range(BATCH):
                mm = pe.transpose(t.bank[1][:, b * SSM_H:(b + 1) * SSM_H], m.dtT[:, b * SEQ:(b + 1) * SEQ],
                                  t.ident[0:SSM_H, 0:SSM_H])
            mm.then_inc(projected, 1)
            pe.wait_ge(bc_ready, 2)
            for b in range(BATCH):
                at = slice(b * SEQ, (b + 1) * SEQ)
                mm = pe.matmul(t.bank[0][:, at], m.bc[:, 0, at], m.bc[:, 1, at], start=True, stop=True)
            mm.then_inc(g_filled, 1)


def conv(dve, c, m, i, done):
    z = m.z[:, :].rearrange("p (b s) -> p b s", b=BATCH)

    def col(k):
        return m.convw[:, bass.ds(i, 1), k:k + 1].rearrange("p a k -> p (a k)")
    c.link(dve.tensor_scalar(z, m.xpad[:, :, 0:SEQ], col(0), m.convb[:, bass.ds(i, 1)], ALU.mult, ALU.add))
    for k in range(1, 4):
        ins = dve.scalar_tensor_tensor(z, m.xpad[:, :, k:k + SEQ], col(k), z, ALU.mult, ALU.add)
        if k < 3:
            c.link(ins)
        else:
            ins.then_inc(done, 1)


def mixer_block(nc, sem, in_proj, out_proj, t, m):
    T = Turn(sem, t, m, "mix", 2)
    XBK, GBK = t.bank[6], t.bank[7]
    x_filled, x_copied, conved, tanh_x, xs_ready = (sem("mix_" + x) for x in ("x", "xcopied", "conved", "tanhx", "xs"))
    xt_filled, xdt_ready, atri_ready, s_filled, exp_done, m_ready = (
        sem("mix_" + x) for x in ("xt", "xdt", "atri", "s", "exp", "m"))
    gate_filled, tanh_g, sg_ready, y_filled, y_ready, ynw_ready, sq_done = (
        sem("mix_" + x) for x in ("gate", "tanhg", "sg", "y", "yready", "ynw", "sq"))
    yn_hi, yn_lo, mixed, sum_filled, var_ready, std_ready, rstd_ready = (
        sem("mix_" + x) for x in ("ynhi", "ynlo", "mixed", "sum", "var", "std", "rstd"))
    dchain, pchain, pready = sem("mix_dchain"), sem("mix_pchain"), sem("mix_pool")
    STEPS = XB
    W = 2

    with nc.Block() as block:
        @block.sync
        def _(sp):
            def load(i, s):
                T.stage_free(sp, i)
                for w, base in ((0, INTER), (1, 0)):
                    sp.dma_start(m.nat[:, s, w, :], in_proj[bass.ds(i * P + base, P), :]).then_inc(T.loaded[w][s], 16)
                src = out_proj.rearrange("(h p) i -> p h i", p=P)[:, :, bass.ds(i * P, P)]
                sp.dma_start(m.nat[:, s, 2, :].rearrange("p (h i) -> p h i", h=KD), src).then_inc(T.loaded[2][s], 16)
            with sp.Fori(0, STEPS // W) as r:
                for u in range(W):
                    load(r * W + u, u)

        @block.gpsimd
        def _(pool):
            def scan_weights(i):
                tri = bc(bc(t.tri[:, :].rearrange("p (x y l) -> p x y l", x=1, y=1), 1, BATCH), 2, 2)
                for dst, src in ((m.atri_hi, m.a_hi[:, :, :].bitcast(F32)), (m.atri_lo, m.a_lo[:, :, :])):
                    col = bc(src[:, :, bass.ds(i * 2, 2)].rearrange("p b (j l) -> p b j l", l=1), 3, SEQ)
                    ins = pool.tensor_tensor(dst[:, :].rearrange("p (b j l) -> p b j l", b=BATCH, j=2), tri, col, ALU.mult)
                ins.then_inc(atri_ready, 1)

            def step(i, last=False):
                pool.wait_ge(exp_done, i + 1)
                ev = m.e[:, :].rearrange("p (b j l) -> p b j l", b=BATCH, j=2)
                gm = bc(m.gm[:, :, :].rearrange("p b (x l) -> p b x l", x=1), 2, 2)
                pool.tensor_tensor(m.mt[:, :].rearrange("p (b j l) -> p b j l", b=BATCH, j=2), ev, gm,
                                   ALU.mult).then_inc(m_ready, 1)
                if not last:
                    scan_weights(i + 1)
                pool.wait_ge(y_ready, i + 1)
                c = Chain(pool, pchain, 2 * i)
                c.link(pool.tensor_tensor(m.yg[:, :], m.y[:, :], m.sg[:, :], ALU.mult))
                c.link(pool.tensor_tensor(m.yg[:, :], m.yg[:, :], m.yg[:, :], ALU.mult))
                pool.tensor_tensor(m.sumsq[:, :], m.sumsq[:, :], m.yg[:, :], ALU.add).then_inc(sq_done, 1)

            pool.sem_inc(sq_done, 1)
            scan_weights(0)
            with pool.Fori(0, STEPS // W - 1) as r:
                for u in range(W):
                    step(r * W + u)
            for i in range(STEPS - W, STEPS):
                step(i, i == STEPS - 1)

        @block.scalar
        def _(act):
            def copy_x(i):
                act.wait_ge(x_filled, i + 1)
                act.wait_ge(conved, i + 1)
                act.activation(m.xpad[:, :, 3:3 + SEQ], XBK[:, 0:TOK].rearrange("p (b s) -> p b s", b=BATCH),
                               ACT.Copy).then_inc(x_copied, 1)

            def tanh_of_x(i):
                act.wait_ge(conved, i + 2)
                act.activation(m.th[:, :], m.z[:, :], ACT.Tanh, scale=0.5).then_inc(tanh_x, 1)

            def step(i, u, last=False):
                act.wait_ge(s_filled, i + 1)
                act.activation(m.e[:, :], GBK[:, :], ACT.Exp).then_inc(exp_done, 1)
                if not last:
                    T.scalar(act, i + 1, 0, 1 - u)
                act.wait_ge(gate_filled, i + 1)
                act.activation(m.thg[:, :], GBK[:, 0:TOK], ACT.Tanh, scale=0.5).then_inc(tanh_g, 1)
                if not last:
                    T.scalar(act, i + 1, 1, 1 - u)
                act.wait_ge(ynw_ready, i + 1)
                act.activation(m.yn_hi[:, :], m.ynw[:, :], ACT.Copy).then_inc(yn_hi, 1)
                if not last:
                    copy_x(i + 1)
                    tanh_of_x(i + 1)
                    T.scalar(act, i + 1, 2, 1 - u)

            for w in range(3):
                T.scalar(act, 0, w, 0)
            copy_x(0)
            tanh_of_x(0)
            with act.Fori(0, STEPS // W - 1) as r:
                for u in range(W):
                    step(r * W + u, u)
            for i in range(STEPS - W, STEPS):
                step(i, i % W, i == STEPS - 1)
            act.wait_ge(var_ready, 1)
            act.activation(m.std[:, :], m.var[:, :], ACT.Sqrt, bias=t.eps[:, 0:1]).then_inc(std_ready, 1)

        @block.vector
        def _(dve):
            def make_x(i):
                dve.wait_ge(tanh_x, i + 1)
                dve.scalar_tensor_tensor(m.xs[:, :], m.th[:, :], 1.0, m.z[:, :], ALU.add,
                                         ALU.mult).then_inc(xs_ready, 1)

            def convolve(i):
                dve.wait_ge(x_copied, i + 1)
                conv(dve, Chain(dve, dchain, 3 * i), m, i, conved)

            def step(i, u, last=False):
                dve.wait_ge(xt_filled, i + 1)
                for j in range(2):
                    at = slice(j * HP, (j + 1) * HP)
                    ins = dve.tensor_tensor(
                        m.xdt[:, :, j, at],
                        XBK[:, 0:TOK].rearrange("p (b c) -> p b c", b=BATCH)[:, :, at],
                        bc(m.dth[:, :, bass.ds(i * 2 + j, 1)], 2, HP), ALU.mult)
                ins.then_inc(xdt_ready, 1)
                if not last:
                    T.vector(dve, i + 1, 0, 1 - u)
                dve.wait_ge(tanh_g, i + 1)
                dve.wait_ge(sq_done, i + 1)
                dve.scalar_tensor_tensor(m.sg[:, :], m.thg[:, :], 1.0, GBK[:, 0:TOK], ALU.add,
                                         ALU.mult).then_inc(sg_ready, 1)
                dve.wait_ge(y_filled, i + 1)
                dve.scalar_tensor_tensor(m.y[:, :], m.xs[:, :], m.dcol[:, bass.ds(i, 1)], XBK[:, 0:TOK], ALU.mult,
                                         ALU.add).then_inc(y_ready, 1)
                dve.wait_ge(y_ready, i + 1)
                dve.scalar_tensor_tensor(m.ynw[:, :], m.y[:, :], m.normw[:, bass.ds(i, 1)], m.sg[:, :], ALU.mult,
                                         ALU.mult).then_inc(ynw_ready, 1)
                if not last:
                    T.vector(dve, i + 1, 1, 1 - u)
                dve.wait_ge(yn_hi, i + 1)
                dve.tensor_tensor(m.yn_lo[:, :], m.ynw[:, :], m.yn_hi[:, :].bitcast(F32),
                                  ALU.subtract).then_inc(yn_lo, 1)
                if not last:
                    convolve(i + 1)
                    make_x(i + 1)
                    T.vector(dve, i + 1, 2, 1 - u)

            dve.sem_inc(T.lo, LO_CREDIT)
            dve.sem_inc(conved, 1)
            dve.sem_inc(sg_ready, 1)
            for w in range(3):
                T.vector(dve, 0, w, 0)
            convolve(0)
            make_x(0)
            with dve.Fori(0, STEPS // W - 1) as r:
                for u in range(W):
                    step(r * W + u, u)
            for i in range(STEPS - W, STEPS):
                step(i, i % W, i == STEPS - 1)
            dve.wait_ge(sum_filled, 1)
            dve.tensor_scalar(m.var[:, :], XBK[:, 0:BATCH], 0.25 / INTER, None, ALU.mult).then_inc(var_ready, 1)
            dve.wait_ge(std_ready, 1)
            dve.reciprocal(m.rstd[:, :], m.std[:, :]).then_inc(rstd_ready, 1)
            dve.wait_ge(rstd_ready, 1)
            dve.wait_ge(mixed, 1)
            for b in range(BATCH):
                for h in range(2):
                    at = slice(h * HALF, (h + 1) * HALF)
                    dve.scalar_tensor_tensor(t.x_res[:, b, at], t.bank[2 * b + h][:, :], m.rstd[:, b:b + 1],
                                             t.x_res[:, b, at], ALU.mult, ALU.add)

        @block.tensor
        def _(pe):
            def project_x(i, s):
                T.ready(pe, i, 0)
                T.project(pe, XBK[:, 0:TOK], 0, s).then_inc(x_filled, 1)

            def step(r, u, last=False):
                i = r * W + u
                landed = 16 * r + 16 * (1 + u)
                pe.wait_ge(xs_ready, i + 1)
                for b in range(BATCH):
                    mm = pe.transpose(XBK[:, b * P:(b + 1) * P], m.xs[:, b * SEQ:(b + 1) * SEQ], t.ident[:, :])
                mm.then_inc(xt_filled, 1)
                pe.wait_ge(atri_ready, i + 1)
                pe.wait_ge(sg_ready, i + 1)
                pe.matmul(GBK[:, :], t.after[:, :], m.atri_hi[:, :], start=True, stop=False)
                pe.matmul(GBK[:, :], t.after[:, :], m.atri_lo[:, :], start=False, stop=True).then_inc(s_filled, 1)
                if not last:
                    T.tensor(pe, i + 1, 0, 1 - u, landed)
                T.ready(pe, i, 1)
                pe.wait_ge(exp_done, i + 1)
                T.project(pe, GBK[:, 0:TOK], 1, u).then_inc(gate_filled, 1)
                pe.wait_ge(xdt_ready, i + 1)
                pe.wait_ge(m_ready, i + 1)
                for b in range(BATCH):
                    for j in range(2):
                        at = (2 * b + j) * SEQ
                        mm = pe.matmul(XBK[:, b * SEQ:(b + 1) * SEQ], m.xdt[:, b, j, :], m.mt[:, at:at + SEQ],
                                       start=j == 0, stop=j == 1)
                mm.then_inc(y_filled, 1)
                if not last:
                    T.tensor(pe, i + 1, 1, 1 - u, landed)
                    pe.wait_ge(y_ready, i + 1)
                    project_x(i + 1, 1 - u)
                    T.tensor(pe, i + 1, 2, 1 - u, landed)
                T.ready(pe, i, 2)
                pe.wait_ge(yn_lo, i + 1)
                mm = T.accumulate(pe, m.yn_hi, m.yn_lo, u, last)
                if last:
                    mm.then_inc(mixed, 1)

            pe.sem_inc(T.turned, T_CREDIT)
            T.zero_sums(pe)
            for w in range(3):
                T.tensor(pe, 0, w, 0, 16)
            project_x(0, 0)
            with pe.Fori(0, STEPS // W - 1) as r:
                for u in range(W):
                    step(r, u)
            for i in range(STEPS - W, STEPS):
                step(i // W, i % W, i == STEPS - 1)
            pe.wait_ge(sq_done, STEPS + 1)
            for b in range(BATCH):
                mm = pe.matmul(XBK[:, b:b + 1], m.sumsq[:, b * SEQ:(b + 1) * SEQ], t.ones[:, 0:1],
                               start=True, stop=True)
            mm.then_inc(sum_filled, 1)


def router_block(nc, sem, gate_w, t, r):
    loaded, turned, gw_hi, gw_lo = (sem("rt_" + x) for x in ("loaded", "turned", "hi", "lo"))
    logits_filled, max_ready, exp_done, comb_ready, comb_turned, combT_ready, spread, spread_read = (
        sem("rt_" + x) for x in ("logits", "max", "exp", "comb", "cturned", "cT", "spread", "sread"))
    logitT_ready = sem("rt_logitT")
    sel_steps, ltri_ready, chain = sem("rt_sel"), sem("rt_ltri"), sem("rt_chain")
    TILES = 3 * PAIRS
    with nc.Block() as block:
        @block.sync
        def _(sp):
            sp.dma_start(r.gw[:, :], gate_w).then_inc(loaded, 16)

        @block.gpsimd
        def _(pool):
            pool.memset(r.sel[:, :, :], 0.0).then_inc(sel_steps, 1)
            pool.memset(r.ltri[:, :, :], 1.0).then_inc(sel_steps, 1)
            pool.memset(r.comb[:, TILES:TILES + 3, :], 1.0).then_inc(sel_steps, 1)
            pool.wait_ge(sel_steps, 3)
            pool.affine_select(out=r.ltri[:, :, :], in_=r.ltri[:, :, :], compare_op=ALU.is_gt, fill=0.0, base=0,
                               pattern=[[1, EXPERTS], [-1, EXPERTS]], channel_multiplier=0).then_inc(ltri_ready, 1)
            sel = r.sel[:, :, :].rearrange("e (q part) p -> e q part p", part=3)
            for part in range(3):
                for half in range(2):
                    second = 1 if part + half >= 2 else 0
                    view = sel[:, :, part, half * HP:(half + 1) * HP]
                    ins = pool.affine_select(out=view, in_=view, compare_op=ALU.not_equal, fill=1.0, base=-second,
                                             pattern=[[-2, PAIRS], [0, HP]], channel_multiplier=1)
                    ins.then_inc(sel_steps, 1)

        @block.scalar
        def _(act):
            act.wait_ge(turned, 1)
            act.activation(r.gw_hi[:, :], t.bank[0][:, 0:KD * EXPERTS], ACT.Copy).then_inc(gw_hi, 1)
            for b in range(BATCH):
                act.wait_ge(max_ready, 1)
                act.activation(r.prob[:, b, :], r.logit[:, b, :], ACT.Exp, bias=r.negmax[:, b:b + 1],
                               accum_out=r.psum[:, b:b + 1]).then_inc(exp_done, 1)
            act.wait_ge(comb_turned, 1)
            act.activation(r.combT[:, :], t.bank[7][0:EXPERTS, 0:TOK], ACT.Copy).then_inc(combT_ready, 1)
            for n in range(TILES // 2):
                act.wait_ge(spread, n + 1)
                act.activation(r.comb[:, 2 * n:2 * n + 2, :], t.bank[n % 4 + 3][:, :].rearrange("p (a s) -> p a s", a=2),
                               ACT.Copy).then_inc(spread_read, 1)

        @block.vector
        def _(dve):
            c = Chain(dve, chain)
            dve.wait_ge(gw_hi, 1)
            dve.tensor_tensor(r.gw_lo[:, :], t.bank[0][:, 0:KD * EXPERTS], r.gw_hi[:, :].bitcast(F32),
                              ALU.subtract).then_inc(gw_lo, 1)
            dve.wait_ge(logits_filled, 1)
            dve.tensor_copy(r.logitT[:, :], t.bank[1][0:EXPERTS, 0:TOK]).then_inc(logitT_ready, 1)
            dve.wait_ge(logits_filled, 2)
            c.link(dve.tensor_copy(r.logit[:, :, :], t.bank[2][:, 0:BATCH * EXPERTS].rearrange("p (b e) -> p b e", b=BATCH)))
            c.link(dve.tensor_reduce(r.negmax[:, :], r.logit[:, :, :], AX.X, ALU.max))
            dve.tensor_scalar(r.negmax[:, :], r.negmax[:, :], -1.0, None, ALU.mult).then_inc(max_ready, 1)
            dve.wait_ge(exp_done, 2)
            c.link(dve.reciprocal(r.psum[:, :], r.psum[:, :]))
            dve.wait_ge(ltri_ready, 1)
            for b in range(BATCH):
                c.link(dve.tensor_scalar(r.prob[:, b, :], r.prob[:, b, :], r.psum[:, b:b + 1], None, ALU.mult))
                pj = bc(r.prob[:, b, :].rearrange("p (a j) -> p a j", a=1), 1, EXPERTS)
                pe_ = bc(r.prob[:, b, :].rearrange("p (e a) -> p e a", a=1), 2, EXPERTS)
                c.link(dve.tensor_tensor(r.eq[:, :, :], pj, pe_, ALU.is_equal))
                c.link(dve.tensor_tensor(r.eq[:, :, :], r.eq[:, :, :], r.ltri[:, :, :], ALU.mult))
                c.link(dve.tensor_tensor(r.gt[:, :, :], pj, pe_, ALU.is_gt))
                c.link(dve.tensor_tensor(r.gt[:, :, :], r.gt[:, :, :], r.eq[:, :, :], ALU.add))
                c.link(dve.tensor_reduce(r.rank[:, :], r.gt[:, :, :], AX.X, ALU.add))
                dve.scalar_tensor_tensor(r.weight[:, b, :], r.rank[:, :], TOPK - 0.5, r.prob[:, b, :], ALU.is_lt,
                                         ALU.mult).then_inc(comb_ready, 1)

        @block.tensor
        def _(pe):
            pe.wait_ge(loaded, 16)
            for k in range(KD):
                mm = pe.transpose(t.bank[0][:, k * EXPERTS:(k + 1) * EXPERTS], r.gw[:, k * P:(k + 1) * P],
                                  t.ident[0:EXPERTS, 0:EXPERTS])
            mm.then_inc(turned, 1)
            pe.wait_ge(gw_lo, 1)
            out = t.bank[1][0:EXPERTS, 0:TOK]
            for k in range(KD):
                es = slice(k * EXPERTS, (k + 1) * EXPERTS)
                pe.matmul(out, r.gw_hi[:, es], t.xn_hi[:, k, :], start=k == 0, stop=False)
                pe.matmul(out, r.gw_hi[:, es], t.xn_lo[:, k, :], start=False, stop=False)
                pe.matmul(out, r.gw_lo[:, es], t.xn_hi[:, k, :], start=False, stop=False)
                mm = pe.matmul(out, r.gw_lo[:, es], t.xn_lo[:, k, :], start=False, stop=k == KD - 1)
            mm.then_inc(logits_filled, 1)
            pe.wait_ge(logitT_ready, 1)
            for b in range(BATCH):
                mm = pe.transpose(t.bank[2][:, b * EXPERTS:(b + 1) * EXPERTS], r.logitT[:, b * SEQ:(b + 1) * SEQ],
                                  t.ident[0:EXPERTS, 0:EXPERTS])
            mm.then_inc(logits_filled, 1)
            for b in range(BATCH):
                pe.wait_ge(comb_ready, b + 1)
                mm = pe.transpose(t.bank[7][0:EXPERTS, b * SEQ:(b + 1) * SEQ], r.weight[:, b, :], t.ident[:, :])
            mm.then_inc(comb_turned, 1)
            pe.wait_ge(combT_ready, 1)
            pe.wait_ge(sel_steps, 9)
            for n in range(TILES // 2):
                if n >= 4:
                    pe.wait_ge(spread_read, n - 3)
                for v in range(2):
                    mm = pe.matmul(t.bank[n % 4 + 3][:, v * TOK:(v + 1) * TOK], r.sel[:, 2 * n + v, :],
                                   r.combT[:, :], start=True, stop=True)
                mm.then_inc(spread, 1)


def ffn_block(nc, sem, w1, w2, sw1, sw2, out, t, f, comb):
    T = Turn(sem, t, f, "ffn", 3)
    GBK, UBK = t.bank[6], t.bank[7]
    gate_filled, silu_done, sgc_ready, up_filled, act_ready, act_hi, act_lo, summed, y_ready, stored = (
        sem("ffn_" + x) for x in ("gate", "silu", "sgc", "up", "act", "acthi", "actlo", "summed", "y", "stored"))
    cw_ready = sem("ffn_cw")
    SHARED = PAIRS

    def slot(j):
        return j % 3

    def landed(q, j):
        return 64 * q + 16 * (j // 3 + 1 + (j in (5, 8)))

    def shared_landed(j):
        return 64 * SHARED + 16 * (j // 3 + 1)

    with nc.Block() as block:
        @block.sync
        def _(sp):
            w1f = w1.rearrange("e o h -> (e o) h")
            w2f = w2.rearrange("e (b p) i -> p e b i", p=P)

            def load_pair(q):
                for j in range(JB):
                    step = q * JB + j
                    T.stage_free(sp, step)
                    for w in range(2):
                        row = j * P + w * EI
                        if j == 5:
                            sp.dma_start(f.nat[0:HP, slot(j), w, :],
                                         w1f[bass.ds(q * 4 * EI + row, HP), :]).then_inc(T.loaded[w][slot(j)], 16)
                            sp.dma_start(f.nat[HP:P, slot(j), w, :],
                                         w1f[bass.ds(q * 4 * EI + 2 * EI + w * EI, HP), :]).then_inc(T.loaded[w][slot(j)], 16)
                        else:
                            if j > 5:
                                row += EI
                            sp.dma_start(f.nat[:, slot(j), w, :],
                                         w1f[bass.ds(q * 4 * EI + row, P), :]).then_inc(T.loaded[w][slot(j)], 16)
                    dst = f.nat[:, slot(j), 2, :].rearrange("p (b i) -> p b i", b=KD)
                    pieces = {5: ((0, 5 * P, 0, HP), (1, 0, HP, HP))}.get(j, ((j > 5, j * P - (j > 5) * EI, 0, P),))
                    for e, col, at, n in pieces:
                        src = w2f[:, bass.ds(q * 2 + int(e), 1), :, col:col + n].rearrange("p e b i -> p (e b) i")
                        sp.dma_start(dst[:, :, at:at + n], src).then_inc(T.loaded[2][slot(j)], 16)

            with sp.Fori(0, PAIRS) as q:
                load_pair(q)
            for j in range(JB):
                T.stage_free(sp, SHARED * JB + j)
                for w in range(2):
                    row = j * P + w * PAIR
                    sp.dma_start(f.nat[:, slot(j), w, :], sw1[row:row + P, :]).then_inc(T.loaded[w][slot(j)], 16)
                sp.dma_start(f.nat[:, slot(j), 2, :].rearrange("p (b i) -> p b i", b=KD),
                             sw2.rearrange("(b p) i -> p b i", p=P)[:, :, j * P:(j + 1) * P]).then_inc(T.loaded[2][slot(j)], 16)
            for b in range(BATCH):
                sp.wait_ge(y_ready, 2 * b + 2)
                sp.dma_start(out[b], t.x_res[:, b, :]).then_inc(stored, 16)
            sp.wait_ge(stored, 16 * BATCH)

        @block.gpsimd
        def _(pool):
            def weigh(q, j):
                step = q * JB + j
                pool.wait_ge(silu_done, step + 2)
                pool.wait_ge(act_ready, step + 1)
                part = 0 if j < 5 else 1 if j == 5 else 2
                pool.tensor_tensor(f.sgc[:, :], f.sg[:, :], f.cw[:, part, :], ALU.mult).then_inc(sgc_ready, 1)
            with pool.Fori(0, PAIRS + 1) as q:
                pool.tensor_copy(f.cw[:, :, :], comb[:, bass.ds(q * 3, 3), :]).then_inc(cw_ready, 1)
                pool.wait_ge(cw_ready, q + 1)
                for j in range(JB):
                    weigh(q, j)
                pool.wait_ge(sgc_ready, q * JB + JB)

        @block.scalar
        def _(act):
            def pair(q, last=False):
                for j in range(JB):
                    step, end = q * JB + j, last and j == JB - 1
                    nxt = slot((j + 1) % JB)
                    act.wait_ge(gate_filled, step + 1)
                    act.activation(f.sg[:, :], GBK[:, 0:TOK], ACT.Silu).then_inc(silu_done, 1)
                    if not end:
                        T.scalar(act, step + 1, 0, nxt)
                        T.scalar(act, step + 1, 1, nxt)
                    act.wait_ge(act_ready, step + 2)
                    act.activation(f.a_hi[:, :], f.a[:, :], ACT.Copy).then_inc(act_hi, 1)
                    if not end:
                        T.scalar(act, step + 1, 2, nxt)
            act.sem_inc(silu_done, 1)
            for w in range(3):
                T.scalar(act, 0, w, 0)
            with act.Fori(0, PAIRS) as q:
                pair(q)
            pair(SHARED, last=True)

        @block.vector
        def _(dve):
            def pair(q, last=False):
                for j in range(JB):
                    step, end = q * JB + j, last and j == JB - 1
                    nxt = slot((j + 1) % JB)
                    if not end:
                        T.vector(dve, step + 1, 0, nxt)
                    dve.wait_ge(up_filled, step + 1)
                    dve.wait_ge(sgc_ready, step + 1)
                    dve.tensor_tensor(f.a[:, :], UBK[:, 0:TOK], f.sgc[:, :], ALU.mult).then_inc(act_ready, 1)
                    if not end:
                        T.vector(dve, step + 1, 1, nxt)
                    dve.wait_ge(act_hi, step + 1)
                    dve.tensor_tensor(f.a_lo[:, :], f.a[:, :], f.a_hi[:, :].bitcast(F32),
                                      ALU.subtract).then_inc(act_lo, 1)
                    if not end:
                        T.vector(dve, step + 1, 2, nxt)
            dve.sem_inc(T.lo, LO_CREDIT)
            dve.sem_inc(act_ready, 1)
            for w in range(3):
                T.vector(dve, 0, w, 0)
            with dve.Fori(0, PAIRS) as q:
                pair(q)
            pair(SHARED, last=True)
            dve.wait_ge(summed, 1)
            for b in range(BATCH):
                for h in range(2):
                    at = slice(h * HALF, (h + 1) * HALF)
                    dve.tensor_tensor(t.x_res[:, b, at], t.bank[2 * b + h][:, :], t.x_res[:, b, at],
                                      ALU.add).then_inc(y_ready, 1)

        @block.tensor
        def _(pe):
            def gate(step, s):
                T.ready(pe, step, 0)
                pe.wait_ge(silu_done, step + 1)
                T.project(pe, GBK[:, 0:TOK], 0, s).then_inc(gate_filled, 1)

            def pair(q, last=False):
                for j in range(JB):
                    step, end = q * JB + j, last and j == JB - 1
                    nxt = slot((j + 1) % JB)
                    if last:
                        arrived = shared_landed(j + 1)
                    elif j == JB - 1:
                        arrived = landed(q + 1, 0)
                    else:
                        arrived = landed(q, j + 1)
                    if not end:
                        T.tensor(pe, step + 1, 0, nxt, arrived)
                    T.ready(pe, step, 1)
                    pe.wait_ge(act_ready, step + 1)
                    T.project(pe, UBK[:, 0:TOK], 1, slot(j)).then_inc(up_filled, 1)
                    if not end:
                        T.tensor(pe, step + 1, 1, nxt, arrived)
                        gate(step + 1, nxt)
                        T.tensor(pe, step + 1, 2, nxt, arrived)
                    T.ready(pe, step, 2)
                    pe.wait_ge(act_lo, step + 1)
                    mm = T.accumulate(pe, f.a_hi, f.a_lo, slot(j), end)
                    if end:
                        mm.then_inc(summed, 1)

            pe.sem_inc(T.turned, T_CREDIT)
            T.zero_sums(pe)
            for w in range(3):
                T.tensor(pe, 0, w, 0, landed(0, 0))
            gate(0, 0)
            with pe.Fori(0, PAIRS) as q:
                pair(q)
            pair(SHARED, last=True)


class Tensors:
    pass


def program(nc, x, ctx_1024, mask, Wq, Wk, Wv, Wo, in_proj_w, conv_w, conv_b, A_log, dt_bias, D, norm_w,
            out_proj_w, gate_w, w1, w2, shared_w1, shared_w2, out):
    with ExitStack() as whole:
        def sem(name):
            return whole.enter_context(nc.semaphore(name))

        def maker(stack, prefix):
            def sb(name, shape, dt=F32):
                return stack.enter_context(nc.sbuf_tensor(prefix + name, shape, dt))
            return sb

        t = Tensors()
        sb = maker(whole, "t_")
        t.x_res = sb("x_res", [P, BATCH, DM])
        t.xn_hi = sb("xn_hi", [P, KD, TOK], F32R)
        t.xn_lo = sb("xn_lo", [P, KD, TOK], F32R)
        t.ident = sb("ident", [P, P])
        t.ones = sb("ones", [P, P])
        t.tri = sb("tri", [P, P])
        t.after = sb("after", [P, P], F32R)
        t.zeros = sb("zeros", [P, P], F32R)
        t.eps = sb("eps", [P, 1])
        t.stats = sb("stats", [P, BATCH, 2, 6])
        t.meanvar = sb("meanvar", [P, BATCH, 2])
        t.std = sb("std", [P, BATCH])
        t.rstd = sb("rstd", [P, BATCH])
        t.bank = [whole.enter_context(nc.psum_tensor(f"bank{n}", [P, HALF], F32)) for n in range(8)]

        made = sem("masks_made")
        with nc.sbuf_tensor("after_f", [P, P], F32) as after_f, nc.Block() as block:
            @block.gpsimd
            def _(pool):
                pool.memset(t.ident[:, :], 0.0).then_inc(made, 1)
                pool.memset(t.ones[:, :], 1.0).then_inc(made, 1)
                pool.memset(t.tri[:, :], 1.0).then_inc(made, 1)
                pool.memset(after_f[:, :], 1.0).then_inc(made, 1)
                pool.memset(t.zeros[:, :].bitcast(F32), 0.0).then_inc(made, 1)
                pool.wait_ge(made, 5)
                pool.affine_select(out=t.ident[:, :], in_=t.ident[:, :], compare_op=ALU.not_equal, fill=1.0, base=0,
                                   pattern=[[-1, P]], channel_multiplier=1)
                pool.affine_select(out=t.tri[:, :], in_=t.tri[:, :], compare_op=ALU.is_ge, fill=0.0, base=0,
                                   pattern=[[1, P]], channel_multiplier=-1)
                pool.affine_select(out=after_f[:, :], in_=after_f[:, :], compare_op=ALU.is_gt, fill=0.0, base=0,
                                   pattern=[[-1, P]], channel_multiplier=1).then_inc(made, 1)
                pool.wait_ge(made, 6)
                pool.tensor_copy(t.after[:, :], after_f[:, :])

        def layernorm(**kw):
            with ExitStack() as stack:
                t.xn = stack.enter_context(nc.sbuf_tensor(f"ln{len(normed)}_xn", [P, BATCH, DM], F32))
                layernorm_block(nc, ln_sems, len(normed), t, **kw)
            normed.append(1)
        normed = []
        ln_sems = [sem("ln_" + x) for x in ("x_in", "chain", "var", "std", "xn", "turned", "hi", "lo")]

        layernorm(load_x=x)
        with ExitStack() as stack:
            a = Tensors()
            sb = maker(stack, "a_")
            a.ctx_hi = sb("ctx_hi", [P, KC, CTX], F32R)
            a.ctx_lo = sb("ctx_lo", [P, KC, CTX], F32R)
            a.k_hi = sb("k_hi", [P, CTX], F32R)
            a.k_lo = sb("k_lo", [P, CTX], F32R)
            a.v_hi = sb("v_hi", [P, CTX // P, HD], F32R)
            a.v_lo = sb("v_lo", [P, CTX // P, HD], F32R)
            a.v_stage = sb("v_stage", [P, 2, HALF])
            a.q_hi = sb("q_hi", [P, 2 * SEQ], F32R)
            a.q_lo = sb("q_lo", [P, 2 * SEQ], F32R)
            a.p = sb("p", [P, 2, CTX])
            a.pt_hi = sb("pt_hi", [P, 3, HALF], F32R)
            a.pt_lo = sb("pt_lo", [P, 3, HALF], F32R)
            a.w_nat = sb("w_nat", [P, 2 * DM])
            a.w_hi = sb("w_hi", [P, 2 * DM], F32R)
            a.w_lo = sb("w_lo", [P, 2 * DM], F32R)
            a.kv_nat = sb("kv_nat", [P, 2, KC, HD])
            a.kv_hi = sb("kv_hi", [P, 2, KC, HD], F32R)
            a.kv_lo = sb("kv_lo", [P, 2, KC, HD], F32R)
            a.mask_raw = sb("mask_raw", [P, CTX], U8)
            a.mask_bias = sb("mask_bias", [P, CTX], mybir.dt.bfloat16)
            a.any_valid = sb("any_valid", [P, BATCH])
            a.mark = sb("mark", [P, 8])
            a.chunkmax = sb("chunkmax", [P, 8])
            a.rowmax = sb("rowmax", [P, 2])
            a.negmax = sb("negmax", [P, 2])
            a.psum = sb("psum", [P, 2])
            a.rinv = sb("rinv", [P, 2])
            a.diag = sb("diag", [P, 2 * SEQ])
            a.rb = sb("rb", [P, 2 * SEQ])
            a.ot = sb("ot", [P, 2 * SEQ])
            a.ot_hi = sb("ot_hi", [P, 2 * SEQ], F32R)
            a.ot_lo = sb("ot_lo", [P, 2 * SEQ], F32R)
            attention_block(nc, sem, ctx_1024, mask, Wq, Wk, Wv, Wo, t, a)

        layernorm()
        with ExitStack() as stack:
            m = Tensors()
            sb = maker(stack, "m_")
            m.nat = sb("nat", [P, 2, 3, DM])
            m.w_hi = sb("w_hi", [P, 2, 3, DM], F32R)
            m.w_lo = sb("w_lo", [P, 2, 3, DM], F32R)
            m.convw = sb("convw", [P, XB + 2, 4])
            m.convb = sb("convb", [P, XB + 2])
            m.normw = sb("normw", [P, XB])
            m.dcol = sb("dcol", [P, XB])
            m.dtb = sb("dtb", [P, SSM_H])
            m.alog = sb("alog", [P, SSM_H])
            m.ea = sb("ea", [P, SSM_H])
            m.zdt = sb("zdt", [P, BATCH, SSM_H])
            m.nabs = sb("nabs", [P, BATCH, SSM_H])
            m.e_dt = sb("e_dt", [P, BATCH, SSM_H])
            m.w_dt = sb("w_dt", [P, BATCH, SSM_H])
            m.ln_dt = sb("ln_dt", [P, BATCH, SSM_H])
            m.d_dt = sb("d_dt", [P, BATCH, SSM_H])
            m.is0 = sb("is0", [P, BATCH, SSM_H])
            m.dth = sb("dth", [P, BATCH, SSM_H])
            m.a = sb("a", [P, BATCH, SSM_H])
            m.a_lo = sb("a_lo", [P, BATCH, SSM_H])
            m.a_hi = sb("a_hi", [P, BATCH, SSM_H], F32R)
            m.xpad = sb("xpad", [P, BATCH, SEQ + 3])
            m.z = sb("z", [P, TOK])
            m.th = sb("th", [P, TOK])
            m.xs = sb("xs", [P, TOK])
            m.thg = sb("thg", [P, TOK])
            m.sg = sb("sg", [P, TOK])
            m.y = sb("y", [P, TOK])
            m.ynw = sb("ynw", [P, TOK])
            m.yg = sb("yg", [P, TOK])
            m.sumsq = sb("sumsq", [P, TOK])
            m.dtT = sb("dtT", [SSM_H, TOK])
            m.bc = sb("bc", [P, 2, TOK])
            m.gm = sb("gm", [P, BATCH, SEQ])
            m.xdt = sb("xdt", [P, BATCH, 2, P])
            m.atri_hi = sb("atri_hi", [P, HALF], F32R)
            m.atri_lo = sb("atri_lo", [P, HALF], F32R)
            m.e = sb("e", [P, HALF])
            m.mt = sb("mt", [P, HALF])
            m.yn_hi = sb("yn_hi", [P, TOK], F32R)
            m.yn_lo = sb("yn_lo", [P, TOK], F32R)
            m.var = sb("var", [P, BATCH])
            m.std = sb("std", [P, BATCH])
            m.rstd = sb("rstd", [P, BATCH])
            mixer_head_block(nc, sem, in_proj_w, conv_w, conv_b, A_log, dt_bias, D, norm_w, t, m)
            mixer_block(nc, sem, in_proj_w, out_proj_w, t, m)

        layernorm()
        with ExitStack() as stack:
            comb = stack.enter_context(nc.sbuf_tensor("comb", [P, 3 * PAIRS + 3, TOK], F32))
            with ExitStack() as inner:
                r = Tensors()
                r.comb = comb
                sb = maker(inner, "r_")
                r.gw = sb("gw", [EXPERTS, DM])
                r.gw_hi = sb("gw_hi", [P, KD * EXPERTS], F32R)
                r.gw_lo = sb("gw_lo", [P, KD * EXPERTS], F32R)
                r.logit = sb("logit", [P, BATCH, EXPERTS])
                r.prob = sb("prob", [P, BATCH, EXPERTS])
                r.weight = sb("weight", [P, BATCH, EXPERTS])
                r.negmax = sb("negmax", [P, BATCH])
                r.psum = sb("psum", [P, BATCH])
                r.ltri = sb("ltri", [P, EXPERTS, EXPERTS])
                r.eq = sb("eq", [P, EXPERTS, EXPERTS])
                r.gt = sb("gt", [P, EXPERTS, EXPERTS])
                r.logitT = sb("logitT", [EXPERTS, TOK])
                r.rank = sb("rank", [P, EXPERTS])
                r.sel = sb("sel", [EXPERTS, 3 * PAIRS, P])
                r.combT = sb("combT", [EXPERTS, TOK])
                router_block(nc, sem, gate_w, t, r)
            f = Tensors()
            sb = maker(stack, "f_")
            f.nat = sb("nat", [P, 3, 3, DM])
            f.w_hi = sb("w_hi", [P, 3, 3, DM], F32R)
            f.w_lo = sb("w_lo", [P, 3, 3, DM], F32R)
            f.sg = sb("sg", [P, TOK])
            f.sgc = sb("sgc", [P, TOK])
            f.a = sb("a", [P, TOK])
            f.cw = sb("cw", [P, 3, TOK])
            f.a_hi = sb("a_hi", [P, TOK], F32R)
            f.a_lo = sb("a_lo", [P, TOK], F32R)
            ffn_block(nc, sem, w1, w2, shared_w1, shared_w2, out, t, f, comb)


_INS = ["x", "ctx_1024", "mask_BxS2_bf1", "L0_xattn_Wq", "L0_xattn_Wk", "L0_xattn_Wv", "L0_xattn_Wo",
        "L0_attn_in_proj_w", "L0_attn_conv_w", "L0_attn_conv_b", "L0_attn_A_log", "L0_attn_dt_bias", "L0_attn_D",
        "L0_attn_norm_w", "L0_attn_out_proj_w", "L0_ffn_gate_w", "L0_ffn_w1", "L0_ffn_w2", "L0_ffn_shared_w1",
        "L0_ffn_shared_w2"]


def kernel(**inputs):
    import numpy as np
    import concourse.bacc as bacc
    from concourse.bass_utils import run_bass_kernel_spmd

    nc = bacc.Bacc("TRN2", target_bir_lowering=False, num_devices=1)
    arrays, args = {}, []
    for name in _INS:
        v = np.ascontiguousarray(inputs[name])
        if v.dtype == np.bool_:
            v = v.view(np.uint8)
        arrays[f"in_{name}"] = v
        args.append(nc.dram_tensor(f"in_{name}", v.shape, mybir.dt.from_np(v.dtype), kind="ExternalInput").ap())
    args.append(nc.dram_tensor("out", (BATCH, SEQ, DM), F32, kind="ExternalOutput").ap())
    program(nc, *args)
    r = run_bass_kernel_spmd(nc, [arrays], core_ids=[0])
    return r.results[0]["out"]
```

```python
from contextlib import ExitStack

import concourse.bass as bass
from concourse import mybir

ALU = mybir.AluOpType
ACT = mybir.ActivationFunctionType
AX = mybir.AxisListType
F32 = mybir.dt.float32
F32R = mybir.dt.float32r
U8 = mybir.dt.uint8

P = 128
BATCH, SEQ, DM = 2, 128, 1024
KD = DM // P
TOK = BATCH * SEQ
CTX, DC = 2048, 512
KC = DC // P
HD = 128
KVH = 8
SCALE = 1.0 / float(HD) ** 0.5
MASKED = -1.0e30
LOWEST = -3.0e38
INTER, NST, SSM_H, HP = 4096, 128, 64, 64
XB = INTER // P
EXPERTS, TOPK, EI = 16, 6, 704
PAIR = 2 * EI
JB = PAIR // P
PAIRS = EXPERTS // 2
Q = 32
QW = PAIR // 4
EPS = 1e-5
QUAD_ROUNDS = (2,)
HALF = 512


class Chain:

    def __init__(self, eng, sem, base=0):
        self.eng, self.sem, self.base, self.n = eng, sem, base, 0

    def link(self, ins):
        self.n += 1
        ins.then_inc(self.sem, 1)
        self.eng.wait_ge(self.sem, self.base + self.n)


def bc(ap, dim, n):
    shape = list(ap.shape)
    shape[dim] = n
    return ap.broadcast_to(shape)


def split3(pe, out, pairs, first, last):
    n = len(pairs)
    for i, ((sh, sl), (mh, ml)) in enumerate(pairs):
        pe.matmul(out, sh, mh, start=first and i == 0, stop=False)
        pe.matmul(out, sh, ml, start=False, stop=False)
        mm = pe.matmul(out, sl, mh, start=False, stop=last and i == n - 1)
    return mm


def by_quad(row):
    return row.rearrange("p (a k h) -> p a k h", a=4, k=KD)


def blocks_by_quad(row):
    return row.rearrange("p (k a h) -> p a k h", a=4, k=KD)


def layernorm_block(nc, sems, round_, t, quads, load_x=None):
    x_in, chain, var_ready, std_ready, xn_ready, turned, hi_written, lo_written = sems
    two, four = 2 * round_, 4 * round_
    with nc.Block() as block:
        @block.sync
        def _(sp):
            if load_x is not None:
                for b in range(BATCH):
                    sp.dma_start(t.x_res[:, b, :], load_x[b]).then_inc(x_in, 16)

        @block.vector
        def _(dve):
            c = Chain(dve, chain, 5 * round_)
            if load_x is not None:
                dve.wait_ge(x_in, 16 * BATCH)
            c.link(dve.memset(t.eps[:, :], EPS))
            for b in range(BATCH):
                for h in range(2):
                    ins = dve.bn_stats(t.stats[:, b, h, :], t.x_res[:, b, h * HALF:(h + 1) * HALF])
                c.link(ins)
                dve.bn_aggr(t.meanvar[:, b, :], t.stats[:, b, :, :]).then_inc(var_ready, 1)
            for b in range(BATCH):
                dve.wait_ge(std_ready, two + b + 1)
                c.link(dve.reciprocal(t.rstd[:, b:b + 1], t.std[:, b:b + 1]))
                rows, to = (by_quad(t.x_res[:, b, :]), blocks_by_quad(t.xn[:, b, :])) if quads else (t.x_res[:, b, :], t.xn[:, b, :])
                dve.tensor_scalar(to, rows, t.meanvar[:, b, 0:1],
                                  t.rstd[:, b:b + 1], ALU.subtract, ALU.mult).then_inc(xn_ready, 1)
            for b in range(BATCH):
                for g in range(2):
                    n = 2 * b + g
                    dve.wait_ge(hi_written, four + n + 1)
                    bank = t.bank[n][:, :].rearrange("p (k s) -> p k s", k=4)
                    at = (slice(None), slice(4 * g, 4 * g + 4), slice(b * SEQ, (b + 1) * SEQ))
                    dve.tensor_tensor(t.xn_lo[at], bank, t.xn_hi[at].bitcast(F32),
                                      ALU.subtract).then_inc(lo_written, 1)

        @block.scalar
        def _(act):
            for b in range(BATCH):
                act.wait_ge(var_ready, two + b + 1)
                act.activation(t.std[:, b:b + 1], t.meanvar[:, b, 1:2], ACT.Sqrt,
                               bias=t.eps[:, 0:1]).then_inc(std_ready, 1)
            for b in range(BATCH):
                for g in range(2):
                    n = 2 * b + g
                    act.wait_ge(turned, four + n + 1)
                    bank = t.bank[n][:, :].rearrange("p (k s) -> p k s", k=4)
                    act.activation(t.xn_hi[:, 4 * g:4 * g + 4, b * SEQ:(b + 1) * SEQ], bank,
                                   ACT.Copy).then_inc(hi_written, 1)

        @block.tensor
        def _(pe):
            for b in range(BATCH):
                pe.wait_ge(xn_ready, two + b + 1)
                for g in range(2):
                    for k in range(4):
                        at = (4 * g + k) * P
                        mm = pe.transpose(t.bank[2 * b + g][:, k * P:(k + 1) * P],
                                          t.xn[:, b, at:at + P], t.ident[:, :])
                    mm.then_inc(turned, 1)


def attention_block(nc, sem, ctx_in, mask, Wq, Wk, Wv, Wo, t, a):
    LOOP = KVH - 1
    ctx_loaded = [sem("ctx_loaded0"), sem("ctx_loaded1")]
    ctx_turned, ctx_hi, ctx_lo = (sem(f"ctx_{x}") for x in ("turned", "hi", "lo"))
    mask_loaded, mask_ready = sem("mask_loaded"), sem("mask_ready")
    kv_loaded, kv_hi, kv_lo = sem("kv_loaded"), sem("kv_hi"), sem("kv_lo")
    wq_loaded, wq_hi, wq_lo = sem("wq_loaded"), sem("wq_hi"), sem("wq_lo")
    wo_loaded, wo_hi, wo_lo = sem("wo_loaded"), sem("wo_hi"), sem("wo_lo")
    k_filled, k_hi, k_lo = sem("k_filled"), sem("k_hi"), sem("k_lo")
    q_filled, q_hi, q_lo = sem("q_filled"), sem("q_hi"), sem("q_lo")
    v_filled, v_raw, vt_filled, vt_hi, vt_lo = (sem(x) for x in ("v_filled", "v_raw", "vt_filled", "vt_hi", "vt_lo"))
    scores_filled, scores_read, negmax_ready, exp_done = (
        sem(x) for x in ("scores_filled", "scores_read", "negmax_ready", "exp_done"))
    diag_ready, rb_filled, rb_read = sem("diag_ready"), sem("rb_filled"), sem("rb_read")
    pt_filled, pt_hi, pt_lo = sem("pt_filled"), sem("pt_hi"), sem("pt_lo")
    pv_filled, ot_ready, ot_hi, ot_lo = sem("pv_filled"), sem("ot_ready"), sem("ot_hi"), sem("ot_lo")
    out_filled, out_read, zeroed = sem("out_filled"), sem("out_read"), sem("att_zeroed")
    chain, max_done, rinv_done = sem("att_chain"), sem("max_done"), sem("rinv_done")
    S = [t.bank[3], t.bank[4]]
    J = [t.bank[5], t.bank[6]]
    PTB = [S[0], S[1], J[1]]
    R = t.bank[7]
    PVB = t.bank[2]
    CH = CTX // HALF
    SB = CTX // P
    GR = SB // 2

    with nc.Block() as block:
        @block.sync
        def _(sp):
            def load_kv(n, g):
                sp.wait_ge(kv_lo, n + 1)
                for i, w in enumerate((Wk, Wv)):
                    src = w.rearrange("(k p) n -> p k n", p=P)[:, :, bass.ds(g * HD, HD)]
                    sp.dma_start(a.kv_nat[:, i, :, :], src).then_inc(kv_loaded, 16)

            def load_wq(n, g, first=False):
                if not first:
                    sp.wait_ge(wq_lo, n + 1)
                    sp.wait_ge(wo_lo, n + 1)
                src = Wq.rearrange("(k p) n -> p k n", p=P)[:, :, bass.ds(g * 2 * HD, 2 * HD)]
                sp.dma_start(a.w_nat[:, :].rearrange("p (k n) -> p k n", k=KD), src).then_inc(wq_loaded, 16)

            def load_wo(n, g, last=False):
                if last:
                    sp.wait_ge(wo_lo, n + 2)
                else:
                    sp.wait_ge(wq_lo, n + 3)
                src = Wo.rearrange("(m p) n -> p m n", p=P)[:, bass.ds(g * 2, 2), :]
                sp.dma_start(a.w_nat[:, :].rearrange("p (j n) -> p j n", j=2), src).then_inc(wo_loaded, 16)

            for b in range(BATCH):
                n0 = KVH * b
                if b:
                    sp.wait_ge(mask_ready, 1)
                sp.dma_start(a.mask_raw[:, :], bc(mask[b:b + 1, :], 0, P)).then_inc(mask_loaded, 16)
                for i in range(SB // 2):
                    m = 8 * b + i
                    if i >= 2:
                        sp.wait_ge(ctx_turned, 2 * (m - 2) + 2)
                    elif b:
                        sp.wait_ge(wo_lo, n0 + 2)
                    dst = a.w_nat[:, (i % 2) * DM:(i % 2 + 1) * DM].rearrange("p (r c) -> p r c", r=2)
                    src = ctx_in[b, i * 2 * P:(i + 1) * 2 * P, :].rearrange("(r p) c -> p r c", p=P)
                    sp.dma_start(dst, src).then_inc(ctx_loaded[i % 2], 16)
                load_kv(n0, 0)
                sp.wait_ge(ctx_turned, SB * (b + 1))
                load_wq(n0, 0, first=True)
                with sp.Fori(0, LOOP) as g:
                    load_kv(g + (n0 + 1), g + 1)
                    load_wq(g + (n0 + 1), g + 1)
                    load_wo(g + n0, g)
                load_wo(n0 + LOOP, LOOP, last=True)

        @block.gpsimd
        def _(pool):
            def lo_of(lo, nat, hi, sem_done):
                pool.tensor_tensor(lo, nat, hi.bitcast(F32), ALU.subtract).then_inc(sem_done, 1)

            def split_kv(n):
                pool.wait_ge(kv_hi, n + 2)
                lo_of(a.kv_lo[:, :, :, :], a.kv_nat[:, :, :, :], a.kv_hi[:, :, :, :], kv_lo)

            def split_wq(n):
                pool.wait_ge(wq_hi, n + 2)
                lo_of(a.w_lo[:, :], a.w_nat[:, :], a.w_hi[:, :], wq_lo)

            def split_wo(n):
                pool.wait_ge(wo_hi, n + 2)
                lo_of(a.w_lo[:, :], a.w_nat[:, :], a.w_hi[:, :], wo_lo)

            pool.sem_inc(kv_lo, 1)
            pool.sem_inc(wq_lo, 1)
            pool.sem_inc(wo_lo, 2)
            for b in range(BATCH):
                n0 = KVH * b
                split_kv(n0)
                split_wq(n0)
                with pool.Fori(0, LOOP) as g:
                    split_kv(g + n0 + 1)
                    split_wq(g + n0 + 1)
                    split_wo(g + n0)
                split_wo(n0 + LOOP)

        @block.scalar
        def _(act):
            def split_kv(n):
                act.wait_ge(kv_loaded, 32 * n + 32)
                act.wait_ge(v_filled, 4 * n + 1)
                act.activation(a.kv_hi[:, :, :, :], a.kv_nat[:, :, :, :], ACT.Copy).then_inc(kv_hi, 1)

            def split_wq(n, first=False):
                act.wait_ge(wq_loaded, 16 * n + 16)
                act.wait_ge(out_filled, n + 1 if first else n)
                if not first:
                    act.wait_ge(q_filled, n)
                act.activation(a.w_hi[:, :], a.w_nat[:, :], ACT.Copy).then_inc(wq_hi, 1)

            def split_wo(n, last=False):
                act.wait_ge(wo_loaded, 16 * n + 16)
                if last:
                    act.wait_ge(out_filled, n + 1)
                else:
                    act.wait_ge(q_filled, n + 2)
                act.activation(a.w_hi[:, :], a.w_nat[:, :], ACT.Copy).then_inc(wo_hi, 1)

            def hi_k(n, chunks=range(CH)):
                for c in chunks:
                    act.wait_ge(k_filled, CH * n + c + 1)
                    act.activation(a.k_hi[:, c * HALF:(c + 1) * HALF], J[c % 2][:, :], ACT.Copy).then_inc(k_hi, 1)

            def hi_q(n):
                act.wait_ge(q_filled, n + 1)
                act.activation(a.q_hi[:, :], J[0][:, 0:2 * HD], ACT.Copy).then_inc(q_hi, 1)

            def raw_v(n, c):
                act.wait_ge(v_filled, CH * n + c + 2)
                act.wait_ge(vt_filled, CH * n + c + 1)
                act.activation(a.v_stage[:, c % 2, :], J[(c + 1) % 2][:, :], ACT.Copy).then_inc(v_raw, 1)

            def hi_v(n, c):
                act.wait_ge(vt_filled, CH * n + c + 3)
                act.activation(a.v_hi[:, 4 * c:4 * c + 4, :],
                               R[:, :].rearrange("p (r d) -> p r d", r=4), ACT.Copy).then_inc(vt_hi, 1)

            def v_steps(n):
                raw_v(n, 0)
                for c in range(1, CH):
                    raw_v(n, c)
                    hi_v(n, c - 1)
                hi_v(n, CH - 1)

            def softmax(n, j):
                act.wait_ge(negmax_ready, 2 * n + (j + 1))
                act.activation(a.p[:, j, :], a.p[:, j, :], ACT.Exp, bias=a.negmax[:, j:j + 1],
                               scale=SCALE, accum_out=a.psum[:, j:j + 1]).then_inc(exp_done, 1)

            def weigh_steps(n, last=False):
                for r in range(GR):
                    act.wait_ge(pt_filled, GR * n + r + 1)
                    act.activation(a.pt_hi[:, r % 3, :], PTB[r % 3][:, :], ACT.Copy).then_inc(pt_hi, 1)
                act.wait_ge(rb_filled, n + 1)
                act.activation(a.rb[:, :], R[:, 0:2 * SEQ], ACT.Copy).then_inc(rb_read, 1)
                split_wo(n, last)
                act.wait_ge(ot_ready, n + 1)
                act.activation(a.ot_hi[:, :], a.ot[:, :], ACT.Copy).then_inc(ot_hi, 1)

            act.sem_inc(kv_hi, 1)
            act.sem_inc(wq_hi, 1)
            act.sem_inc(wo_hi, 1)
            act.sem_inc(v_raw, 1)
            for b in range(BATCH):
                n0 = KVH * b
                for i in range(SB):
                    u = SB * b + i
                    act.wait_ge(ctx_turned, u + 1)
                    act.activation(a.ctx_hi[:, :, i * P:(i + 1) * P],
                                   t.bank[2 + i % 4][:, :].rearrange("p (c s) -> p c s", c=KC),
                                   ACT.Copy).then_inc(ctx_hi, 1)
                split_kv(n0)
                split_wq(n0, first=True)
                hi_k(n0)
                hi_q(n0)
                v_steps(n0)
                with act.Fori(0, LOOP) as g:
                    n = g + n0
                    split_kv(n + 1)
                    split_wq(n + 1)
                    softmax(n, 0)
                    hi_k(n + 1, range(1))
                    softmax(n, 1)
                    hi_k(n + 1, range(1, CH))
                    hi_q(n + 1)
                    weigh_steps(n)
                    v_steps(n + 1)
                softmax(n0 + LOOP, 0)
                softmax(n0 + LOOP, 1)
                weigh_steps(n0 + LOOP, last=True)

        @block.vector
        def _(dve):
            c = Chain(dve, chain)
            dve.sem_inc(pt_lo, 1)

            def lo_k(n, chunks=range(CH)):
                for ch in chunks:
                    dve.wait_ge(k_hi, CH * n + ch + 1)
                    at = slice(ch * HALF, (ch + 1) * HALF)
                    dve.tensor_tensor(a.k_lo[:, at], J[ch % 2][:, :], a.k_hi[:, at].bitcast(F32),
                                      ALU.subtract).then_inc(k_lo, 1)

            def lo_q(n):
                dve.wait_ge(q_hi, n + 1)
                dve.tensor_tensor(a.q_lo[:, :], J[0][:, 0:2 * HD], a.q_hi[:, :].bitcast(F32),
                                  ALU.subtract).then_inc(q_lo, 1)

            def lo_v(n):
                for ch in range(CH):
                    dve.wait_ge(vt_hi, CH * n + ch + 1)
                    at = (slice(None), slice(4 * ch, 4 * ch + 4), slice(None))
                    dve.tensor_tensor(a.v_lo[at], R[:, :].rearrange("p (r d) -> p r d", r=4),
                                      a.v_hi[at].bitcast(F32), ALU.subtract).then_inc(vt_lo, 1)

            def scores(n):
                for j in range(2):
                    for ch in range(CH):
                        u = j * CH + ch
                        dve.wait_ge(scores_filled, 2 * CH * n + u + 1)
                        dve.memset(a.mark[:, u:u + 1], 0.0)
                        at = slice(ch * HALF, (ch + 1) * HALF)
                        dve.tensor_tensor_reduce(out=a.p[:, j, at], in0=S[u % 2][:, :], in1=a.mask_bias[:, at],
                                                 scale=1.0, scalar=LOWEST, op0=ALU.add, op1=ALU.max,
                                                 accum_out=a.chunkmax[:, u:u + 1]).then_inc(scores_read, 1)
                    dve.wait_ge(scores_read, 2 * CH * n + (j + 1) * CH)
                    dve.tensor_reduce(a.rowmax[:, j:j + 1], a.chunkmax[:, j * CH:(j + 1) * CH], AX.X,
                                      ALU.max).then_inc(max_done, 1)
                    dve.wait_ge(max_done, 2 * n + (j + 1))
                    dve.tensor_scalar(a.negmax[:, j:j + 1], a.rowmax[:, j:j + 1], -SCALE, None,
                                      ALU.mult).then_inc(negmax_ready, 1)

            def inverse_sum(n, b):
                dve.wait_ge(exp_done, 2 * n + 2)
                dve.reciprocal(a.rinv[:, :], a.psum[:, :]).then_inc(rinv_done, 1)
                dve.wait_ge(rinv_done, 2 * n + 1)
                dve.tensor_scalar(a.rinv[:, :], a.rinv[:, :], a.any_valid[:, b:b + 1], None,
                                  ALU.mult).then_inc(rinv_done, 1)
                dve.wait_ge(rinv_done, 2 * n + 2)
                for j in range(2):
                    dve.tensor_scalar(a.diag[:, j * SEQ:(j + 1) * SEQ], t.ident[:, :], a.rinv[:, j:j + 1],
                                      None, ALU.mult).then_inc(diag_ready, 1)

            def pv_steps(n):
                for r in range(GR):
                    dve.wait_ge(pt_hi, GR * n + r + 1)
                    dve.tensor_tensor(a.pt_lo[:, r % 3, :], PTB[r % 3][:, :],
                                      a.pt_hi[:, r % 3, :].bitcast(F32), ALU.subtract).then_inc(pt_lo, 1)
                dve.wait_ge(pv_filled, n + 1)
                dve.wait_ge(rb_read, n + 1)
                dve.tensor_tensor(a.ot[:, :], PVB[:, 0:2 * SEQ], a.rb[:, :], ALU.mult).then_inc(ot_ready, 1)
                dve.wait_ge(ot_hi, n + 1)
                dve.tensor_tensor(a.ot_lo[:, :], a.ot[:, :], a.ot_hi[:, :].bitcast(F32),
                                  ALU.subtract).then_inc(ot_lo, 1)

            for b in range(BATCH):
                n0 = KVH * b
                dve.wait_ge(mask_loaded, 16 * (b + 1))
                dve.tensor_copy(a.mask_bias[:, :], a.mask_raw[:, :]).then_inc(mask_ready, 1)
                dve.wait_ge(mask_ready, b + 1)
                c.link(dve.tensor_reduce(a.any_valid[:, b:b + 1], a.mask_bias[:, :], AX.X, ALU.max))
                c.link(dve.tensor_scalar(a.mask_bias[:, :], a.mask_bias[:, :], 1.0, -MASKED,
                                         ALU.subtract, ALU.mult))
                for i in range(SB):
                    dve.wait_ge(ctx_hi, SB * b + i + 1)
                    at = (slice(None), slice(None), slice(i * P, (i + 1) * P))
                    dve.tensor_tensor(a.ctx_lo[at], t.bank[2 + i % 4][:, :].rearrange("p (c s) -> p c s", c=KC),
                                      a.ctx_hi[at].bitcast(F32), ALU.subtract).then_inc(ctx_lo, 1)
                lo_k(n0)
                lo_q(n0)
                lo_v(n0)
                with dve.Fori(0, LOOP) as g:
                    n = g + n0
                    scores(n)
                    lo_k(n + 1, range(2))
                    inverse_sum(n, b)
                    lo_k(n + 1, range(2, CH))
                    lo_q(n + 1)
                    pv_steps(n)
                    lo_v(n + 1)
                scores(n0 + LOOP)
                inverse_sum(n0 + LOOP, b)
                pv_steps(n0 + LOOP)
                dve.wait_ge(out_filled, KVH * (b + 1) + 1)
                for h in range(2):
                    at = slice(h * HALF, (h + 1) * HALF)
                    dve.tensor_tensor(t.x_res[:, b, at], t.bank[h][:, :], t.x_res[:, b, at],
                                      ALU.add).then_inc(out_read, 1)

        @block.tensor
        def _(pe):
            def project_k(n):
                pe.wait_ge(kv_lo, n + 2)
                for c in range(CH):
                    if c < 2:
                        pe.wait_ge(v_raw, CH * n + 1)
                    else:
                        pe.wait_ge(k_lo, CH * n + (c - 1))
                    at = slice(c * HALF, (c + 1) * HALF)
                    split3(pe, J[c % 2][:, :], [((a.kv_hi[:, 0, k, :], a.kv_lo[:, 0, k, :]),
                                                 (a.ctx_hi[:, k, at], a.ctx_lo[:, k, at])) for k in range(KC)],
                           True, True).then_inc(k_filled, 1)

            def project_q(n, b):
                pe.wait_ge(wq_lo, n + 2)
                pe.wait_ge(k_lo, CH * n + 4)
                at = slice(b * SEQ, (b + 1) * SEQ)
                for j in range(2):
                    ws = [slice(k * 2 * HD + j * HD, k * 2 * HD + (j + 1) * HD) for k in range(KD)]
                    mm = split3(pe, J[0][:, j * SEQ:(j + 1) * SEQ],
                                [((a.w_hi[:, ws[k]], a.w_lo[:, ws[k]]),
                                  (t.xn_hi[:, k, at], t.xn_lo[:, k, at])) for k in range(KD)], True, True)
                mm.then_inc(q_filled, 1)

            def project_v(n, first=False, out_before_last_turn=None):
                def chunk(c):
                    if c < 2:
                        pe.wait_ge(q_lo, n + 1)
                    else:
                        pe.wait_ge(v_raw, CH * n + c)
                    at = slice(c * HALF, (c + 1) * HALF)
                    split3(pe, J[(c + 1) % 2][:, :], [((a.kv_hi[:, 1, k, :], a.kv_lo[:, 1, k, :]),
                                                       (a.ctx_hi[:, k, at], a.ctx_lo[:, k, at])) for k in range(KC)],
                           True, True).then_inc(v_filled, 1)

                def turn(c):
                    pe.wait_ge(v_raw, CH * n + c + 2)
                    if c > 0:
                        pe.wait_ge(vt_lo, CH * n + c)
                    elif not first:
                        pe.wait_ge(rb_read, n)
                    for r in range(4):
                        mm = pe.transpose(R[:, r * P:(r + 1) * P], a.v_stage[:, c % 2, r * P:(r + 1) * P],
                                          t.ident[:, :])
                    mm.then_inc(vt_filled, 1)
                chunk(0)
                for c in range(1, CH):
                    chunk(c)
                    turn(c - 1)
                if out_before_last_turn is not None:
                    project_out(out_before_last_turn, False)
                turn(CH - 1)

            def scores(n):
                pe.wait_ge(k_lo, CH * n + CH)
                pe.wait_ge(q_lo, n + 1)
                for j in range(2):
                    for c in range(CH):
                        u = j * CH + c
                        if u < 2:
                            pe.wait_ge(pt_lo, GR * n + 1)
                        else:
                            pe.wait_ge(scores_read, 2 * CH * n + u - 1)
                        qs, at = slice(j * SEQ, (j + 1) * SEQ), slice(c * HALF, (c + 1) * HALF)
                        split3(pe, S[u % 2][:, :], [((a.q_hi[:, qs], a.q_lo[:, qs]),
                                                     (a.k_hi[:, at], a.k_lo[:, at]))],
                               True, True).then_inc(scores_filled, 1)

            def broadcast_inverse(n):
                pe.wait_ge(diag_ready, 2 * n + 2)
                pe.wait_ge(vt_lo, CH * n + CH)
                pe.matmul(R[:, 0:2 * SEQ], t.ones[:, :], a.diag[:, :], start=True, stop=True).then_inc(rb_filled, 1)

            def weigh_values(n):
                def turn(r):
                    if r >= 3:
                        pe.wait_ge(pt_lo, GR * n + r - 1)
                    for q in range(2):
                        for j in range(2):
                            s = (2 * r + q) * P
                            mm = pe.transpose(PTB[r % 3][:, (2 * q + j) * P:(2 * q + j + 1) * P],
                                              a.p[:, j, s:s + P], t.ident[:, :])
                    mm.then_inc(pt_filled, 1)

                def weigh(r):
                    pe.wait_ge(pt_lo, GR * n + r + 2)
                    pairs = [((a.v_hi[:, 2 * r + q, :], a.v_lo[:, 2 * r + q, :]),
                              (a.pt_hi[:, r % 3, q * 2 * SEQ:(q + 1) * 2 * SEQ],
                               a.pt_lo[:, r % 3, q * 2 * SEQ:(q + 1) * 2 * SEQ])) for q in range(2)]
                    return split3(pe, PVB[:, 0:2 * SEQ], pairs, r == 0, r == GR - 1)
                pe.wait_ge(exp_done, 2 * n + 2)
                for r in range(3):
                    turn(r)
                for r in range(GR):
                    if r == 5:
                        broadcast_inverse(n)
                    mm = weigh(r)
                    if r + 3 < GR:
                        turn(r + 3)
                mm.then_inc(pv_filled, 1)

            def project_out(n, last):
                pe.wait_ge(wo_lo, n + 3)
                pe.wait_ge(ot_lo, n + 1)
                for j in range(2):
                    at = slice(j * SEQ, (j + 1) * SEQ)
                    for h in range(2):
                        w = slice(j * DM + h * HALF, j * DM + (h + 1) * HALF)
                        mm = split3(pe, t.bank[h][:, :], [((a.ot_hi[:, at], a.ot_lo[:, at]),
                                                           (a.w_hi[:, w], a.w_lo[:, w]))],
                                    False, last and j == 1)
                mm.then_inc(out_filled, 1)

            pe.sem_inc(out_filled, 1)
            pe.sem_inc(v_filled, 1)
            pe.sem_inc(vt_filled, 2)
            for b in range(BATCH):
                n0 = KVH * b
                if b:
                    pe.wait_ge(out_read, 2 * b)
                for h in range(2):
                    pe.matmul(t.bank[h][:, :], t.zeros[:, :], t.xn_hi[:, 0:2, :], start=True, stop=False)
                for i in range(SB):
                    u = SB * b + i
                    pe.wait_ge(ctx_loaded[i // 2 % 2], 16 * (SB // 4 * b + i // 4 + 1))
                    if i >= 4:
                        pe.wait_ge(ctx_lo, u - 3)
                    elif b:
                        pe.wait_ge(ot_lo, n0)
                        pe.wait_ge(pt_lo, GR * n0 + 1)
                    half = a.w_nat[:, (i // 2 % 2) * DM + (i % 2) * DC:(i // 2 % 2) * DM + (i % 2 + 1) * DC]
                    for c in range(KC):
                        mm = pe.transpose(t.bank[2 + i % 4][:, c * P:(c + 1) * P], half[:, c * P:(c + 1) * P],
                                          t.ident[:, :])
                    mm.then_inc(ctx_turned, 1)
                pe.wait_ge(ctx_lo, SB * (b + 1))
                project_k(n0)
                project_q(n0, b)
                project_v(n0, first=b == 0)
                with pe.Fori(0, LOOP) as g:
                    n = g + n0
                    scores(n)
                    project_k(n + 1)
                    project_q(n + 1, b)
                    weigh_values(n)
                    project_v(n + 1, out_before_last_turn=n)
                scores(n0 + LOOP)
                weigh_values(n0 + LOOP)
                project_out(n0 + LOOP, True)


T_CREDIT, LO_CREDIT = 12, 2


class Turn:

    def __init__(self, sem, t, f, name, slots):
        self.t, self.f = t, f
        self.turned, self.hi, self.lo = sem(name + "_turned"), sem(name + "_hi"), sem(name + "_lo")
        self.loaded = [[sem(f"{name}_loaded{w}_{s}") for s in range(slots)] for w in range(3)]

    def tensor(self, pe, m, w, s, loaded):
        pe.wait_ge(self.loaded[w][s], loaded)
        for half in range(2):
            pe.wait_ge(self.lo, 6 * m + (2 * w + half + 1))
            for r in range(4):
                mm = pe.transpose(self.t.bank[4 + half][:, r * P:(r + 1) * P],
                                  self.f.nat[:, s, w, (4 * half + r) * P:(4 * half + r + 1) * P],
                                  self.t.ident[:, :])
            mm.then_inc(self.turned, 1)

    def scalar(self, act, m, w, s):
        for half in range(2):
            act.wait_ge(self.turned, 6 * m + (2 * w + half + 1 + T_CREDIT))
            act.activation(self.f.w_hi[:, s, w, half * HALF:(half + 1) * HALF],
                           self.t.bank[4 + half][:, :], ACT.Copy).then_inc(self.hi, 1)

    def vector(self, dve, m, w, s):
        for half in range(2):
            at = (slice(None), s, w, slice(half * HALF, (half + 1) * HALF))
            dve.wait_ge(self.hi, 6 * m + (2 * w + half + 1))
            dve.tensor_tensor(self.f.w_lo[at], self.t.bank[4 + half][:, :],
                              self.f.w_hi[at].bitcast(F32), ALU.subtract).then_inc(self.lo, 1)

    def stage_free(self, sp, m):
        sp.wait_ge(self.turned, 6 * m + 6)

    def ready(self, pe, m, w):
        pe.wait_ge(self.lo, 6 * m + (2 * w + 2 + LO_CREDIT))


def project(pe, t, f, out, w, s):
    ks = [slice(k * P, (k + 1) * P) for k in range(KD)]
    return split3(pe, out, [((f.w_hi[:, s, w, ks[k]], f.w_lo[:, s, w, ks[k]]),
                             (t.xn_hi[:, k, :], t.xn_lo[:, k, :])) for k in range(KD)], True, True)


def accumulate(pe, t, f, hi, lo, s, last):
    for b in range(BATCH):
        rows = slice(b * SEQ, (b + 1) * SEQ)
        for h in range(2):
            at = slice(h * HALF, (h + 1) * HALF)
            mm = split3(pe, t.bank[2 * b + h][:, :],
                        [((hi[:, rows], lo[:, rows]), (f.w_hi[:, s, 2, at], f.w_lo[:, s, 2, at]))], False, last)
    return mm


def zero_sums(pe, t):
    for n in range(4):
        pe.matmul(t.bank[n][:, :], t.zeros[:, :], t.xn_hi[:, 0:2, :], start=True, stop=False)


def mixer_head_block(nc, sem, in_proj, conv_w, conv_b, A_log, dt_bias, D, norm_w, t, m):
    nat, wh, wl = m.nat, m.w_hi, m.w_lo
    tiles, consts = [sem(f"head_tile{w}") for w in range(3)], sem("head_consts")
    turned, hi_w, lo_w = sem("head_turned"), sem("head_hi"), sem("head_lo")
    projected, copied, conved, tanhed, bc_ready = (sem(f"head_{x}") for x in ("proj", "copied", "conved", "tanhed", "bc"))
    g_filled, zdt_ready, exp_dt, w_ready, ln_dt, a_ready, padded, m_zeroed = (
        sem(f"head_{x}") for x in ("g", "zdt", "expdt", "w", "lndt", "a", "padded", "mzero"))
    chain, dtT_ready = sem("head_chain"), sem("head_dtT")
    BANKS = [0, 1, 2, 3, 4]
    with nc.Block() as block:
        @block.sync
        def _(sp):
            r0 = 2 * INTER
            for w, (r, n) in enumerate(((r0, P), (r0 + P, P), (r0 + 2 * P, SSM_H))):
                sp.dma_start(nat[0:n, 0, w, :], in_proj[r:r + n, :]).then_inc(tiles[w], 16)
            sp.dma_start(m.convw[:, :, :], conv_w.rearrange("(i p) o k -> p i (o k)", p=P)).then_inc(consts, 16)
            sp.dma_start(m.convb[:, :], conv_b.rearrange("(i p) -> p i", p=P), allow_slow_non_contiguous=True).then_inc(consts, 16)
            sp.dma_start(m.normw[:, :], norm_w.rearrange("(i p) -> p i", p=P), allow_slow_non_contiguous=True).then_inc(consts, 16)
            for j in range(2):
                src = bc(D.rearrange("(a i two) -> a two i", a=1, two=2)[:, j, :], 0, HP)
                sp.dma_start(m.dcol[j * HP:(j + 1) * HP, :], src, allow_slow_non_contiguous=True).then_inc(consts, 16)
            sp.dma_start(m.dtb[:, :], bc(dt_bias.rearrange("(a h) -> a h", a=1), 0, P)).then_inc(consts, 16)
            sp.dma_start(m.alog[:, :], bc(A_log.rearrange("(a h) -> a h", a=1), 0, P)).then_inc(consts, 16)

        @block.gpsimd
        def _(pool):
            pool.memset(m.xpad[:, :, :], 0.0).then_inc(padded, 1)
            pool.memset(m.xdt[:, :, :, :], 0.0).then_inc(m_zeroed, 1)
            pool.memset(m.sumsq[:, :], 0.0).then_inc(m_zeroed, 1)
            pool.wait_ge(m_zeroed, 2)

        @block.scalar
        def _(act):
            for q in range(5):
                act.wait_ge(turned, q + 1)
                w, half = q // 2, q % 2
                act.activation(wh[:, 0, w, half * HALF:(half + 1) * HALF], t.bank[q][:, :],
                               ACT.Copy).then_inc(hi_w, 1)
            act.wait_ge(padded, 1)
            for n in range(2):
                act.wait_ge(projected, n + 1)
                if n:
                    act.wait_ge(conved, 1)
                act.activation(m.xpad[:, :, 3:3 + SEQ], t.bank[5 + n][:, 0:TOK].rearrange("p (b s) -> p b s", b=BATCH),
                               ACT.Copy).then_inc(copied, 1)
                act.wait_ge(conved, n + 1)
                if n:
                    act.wait_ge(bc_ready, 1)
                act.activation(m.th[:, :], m.z[:, :], ACT.Tanh, scale=0.5).then_inc(tanhed, 1)
            act.wait_ge(zdt_ready, 1)
            act.activation(m.e_dt[:, :, :], m.nabs[:, :, :], ACT.Exp).then_inc(exp_dt, 1)
            act.activation(m.ea[:, :], m.alog[:, :], ACT.Exp).then_inc(exp_dt, 1)
            act.wait_ge(w_ready, 1)
            act.activation(m.ln_dt[:, :, :], m.w_dt[:, :, :], ACT.Ln).then_inc(ln_dt, 1)
            act.wait_ge(a_ready, 1)
            act.activation(m.a_hi[:, :, :], m.a[:, :, :], ACT.Copy).then_inc(ln_dt, 1)

        @block.vector
        def _(dve):
            c = Chain(dve, chain)
            for q in range(5):
                dve.wait_ge(hi_w, q + 1)
                w, half = q // 2, q % 2
                at = (slice(None), 0, w, slice(half * HALF, (half + 1) * HALF))
                dve.tensor_tensor(wl[at], t.bank[q][:, :], wh[at].bitcast(F32), ALU.subtract).then_inc(lo_w, 1)
            dve.wait_ge(projected, 3)
            dve.tensor_copy(m.dtT[:, :], t.bank[7][0:SSM_H, 0:TOK]).then_inc(dtT_ready, 1)
            dve.wait_ge(consts, 16 * 7)
            for n in range(2):
                dve.wait_ge(copied, n + 1)
                if n:
                    dve.wait_ge(bc_ready, 1)
                conv(dve, c, m, XB + n, conved)
                dve.wait_ge(tanhed, n + 1)
                dve.scalar_tensor_tensor(m.bc[:, n, :], m.th[:, :], 1.0, m.z[:, :], ALU.add,
                                         ALU.mult).then_inc(bc_ready, 1)
            dve.wait_ge(projected, 4)
            c.link(dve.tensor_tensor(m.zdt[:, :, :], t.bank[1][:, 0:2 * SSM_H].rearrange("p (b h) -> p b h", b=BATCH),
                                     bc(m.dtb[:, :].rearrange("p (a h) -> p a h", a=1), 1, BATCH), ALU.add))
            dve.scalar_tensor_tensor(m.nabs[:, :, :], m.zdt[:, :, :], -1.0, m.zdt[:, :, :], ALU.mult, ALU.min).then_inc(zdt_ready, 1)
            dve.wait_ge(exp_dt, 1)
            dve.tensor_scalar(m.w_dt[:, :, :], m.e_dt[:, :, :], 1.0, None, ALU.add).then_inc(w_ready, 1)
            dve.wait_ge(w_ready, 1)
            c.link(dve.tensor_scalar(m.d_dt[:, :, :], m.w_dt[:, :, :], 1.0, None, ALU.subtract))
            c.link(dve.tensor_scalar(m.is0[:, :, :], m.d_dt[:, :, :], 0.0, None, ALU.is_equal))
            c.link(dve.tensor_tensor(m.d_dt[:, :, :], m.d_dt[:, :, :], m.is0[:, :, :], ALU.add))
            c.link(dve.reciprocal(m.d_dt[:, :, :], m.d_dt[:, :, :]))
            c.link(dve.tensor_tensor(m.d_dt[:, :, :], m.d_dt[:, :, :], m.e_dt[:, :, :], ALU.mult))
            c.link(dve.tensor_tensor(m.is0[:, :, :], m.is0[:, :, :], m.e_dt[:, :, :], ALU.mult))
            dve.wait_ge(ln_dt, 1)
            c.link(dve.tensor_tensor(m.d_dt[:, :, :], m.d_dt[:, :, :], m.ln_dt[:, :, :], ALU.mult))
            c.link(dve.tensor_tensor(m.d_dt[:, :, :], m.d_dt[:, :, :], m.is0[:, :, :], ALU.add))
            c.link(dve.scalar_tensor_tensor(m.zdt[:, :, :], m.zdt[:, :, :], 0.0, m.d_dt[:, :, :], ALU.max, ALU.add))
            dve.tensor_scalar(m.dth[:, :, :], m.zdt[:, :, :], 0.5, None, ALU.mult)
            dve.wait_ge(exp_dt, 2)
            dve.scalar_tensor_tensor(m.a[:, :, :], m.zdt[:, :, :], -1.0,
                                     bc(m.ea[:, :].rearrange("p (a h) -> p a h", a=1), 1, BATCH),
                                     ALU.mult, ALU.mult).then_inc(a_ready, 1)
            dve.wait_ge(ln_dt, 2)
            dve.tensor_tensor(m.a_lo[:, :, :], m.a[:, :, :], m.a_hi[:, :, :].bitcast(F32), ALU.subtract)
            dve.tensor_scalar(m.dcol[:, :], m.dcol[:, :], 0.5, None, ALU.mult)
            c.link(dve.tensor_scalar(m.normw[:, :], m.normw[:, :], 0.5, None, ALU.mult))
            dve.wait_ge(g_filled, 1)
            c.link(dve.scalar_tensor_tensor(m.gm[:, :, :], t.bank[0][:, 0:TOK].rearrange("p (b s) -> p b s", b=BATCH),
                                            0.25, bc(t.tri[:, :].rearrange("p (a l) -> p a l", a=1), 1, BATCH),
                                            ALU.mult, ALU.mult))

        @block.tensor
        def _(pe):
            for w in range(3):
                n = SSM_H if w == 2 else P
                pe.wait_ge(tiles[w], 16)
                for half in range(1 if w == 2 else 2):
                    blocks = KD if w == 2 else 4
                    for r in range(blocks):
                        k = 4 * half + r
                        mm = pe.transpose(t.bank[2 * w + half][:, r * n:(r + 1) * n],
                                          nat[0:n, 0, w, k * P:(k + 1) * P], t.ident[0:n, 0:n])
                    mm.then_inc(turned, 1)
            for w in range(2):
                pe.wait_ge(lo_w, 2 * w + 2)
                ks = [slice(k * P, (k + 1) * P) for k in range(KD)]
                split3(pe, t.bank[5 + w][:, 0:TOK], [((wh[:, 0, w, ks[k]], wl[:, 0, w, ks[k]]),
                                                       (t.xn_hi[:, k, :], t.xn_lo[:, k, :])) for k in range(KD)],
                       True, True).then_inc(projected, 1)
            pe.wait_ge(lo_w, 5)
            hs = [slice(k * SSM_H, (k + 1) * SSM_H) for k in range(KD)]
            split3(pe, t.bank[7][0:SSM_H, 0:TOK],
                   [((wh[:, 0, 2, hs[k]], wl[:, 0, 2, hs[k]]), (t.xn_hi[:, k, :], t.xn_lo[:, k, :]))
                    for k in range(KD)], True, True).then_inc(projected, 1)
            pe.wait_ge(dtT_ready, 1)
            for b in range(BATCH):
                mm = pe.transpose(t.bank[1][:, b * SSM_H:(b + 1) * SSM_H], m.dtT[:, b * SEQ:(b + 1) * SEQ],
                                  t.ident[0:SSM_H, 0:SSM_H])
            mm.then_inc(projected, 1)
            pe.wait_ge(bc_ready, 2)
            for b in range(BATCH):
                at = slice(b * SEQ, (b + 1) * SEQ)
                mm = pe.matmul(t.bank[0][:, at], m.bc[:, 0, at], m.bc[:, 1, at], start=True, stop=True)
            mm.then_inc(g_filled, 1)


def conv(dve, c, m, i, done):
    z = m.z[:, :].rearrange("p (b s) -> p b s", b=BATCH)

    def col(k):
        return m.convw[:, bass.ds(i, 1), k:k + 1].rearrange("p a k -> p (a k)")
    c.link(dve.tensor_scalar(z, m.xpad[:, :, 0:SEQ], col(0), m.convb[:, bass.ds(i, 1)], ALU.mult, ALU.add))
    for k in range(1, 4):
        ins = dve.scalar_tensor_tensor(z, m.xpad[:, :, k:k + SEQ], col(k), z, ALU.mult, ALU.add)
        if k < 3:
            c.link(ins)
        else:
            ins.then_inc(done, 1)


def mixer_block(nc, sem, in_proj, out_proj, t, m):
    T = Turn(sem, t, m, "mix", 2)
    XBK, GBK = t.bank[6], t.bank[7]
    x_filled, x_copied, conved, tanh_x, xs_ready = (sem("mix_" + x) for x in ("x", "xcopied", "conved", "tanhx", "xs"))
    xt_filled, xdt_ready, atri_ready, s_filled, exp_done, m_ready = (
        sem("mix_" + x) for x in ("xt", "xdt", "atri", "s", "exp", "m"))
    gate_filled, tanh_g, sg_ready, y_filled, y_ready, ynw_ready, sq_done = (
        sem("mix_" + x) for x in ("gate", "tanhg", "sg", "y", "yready", "ynw", "sq"))
    yn_hi, yn_lo, mixed, sum_filled, var_ready, std_ready, rstd_ready = (
        sem("mix_" + x) for x in ("ynhi", "ynlo", "mixed", "sum", "var", "std", "rstd"))
    dchain, pchain, pready = sem("mix_dchain"), sem("mix_pchain"), sem("mix_pool")
    STEPS = XB
    W = 2

    with nc.Block() as block:
        @block.sync
        def _(sp):
            def load(i, s):
                T.stage_free(sp, i)
                for w, base in ((0, INTER), (1, 0)):
                    sp.dma_start(m.nat[:, s, w, :], in_proj[bass.ds(i * P + base, P), :]).then_inc(T.loaded[w][s], 16)
                src = out_proj.rearrange("(h p) i -> p h i", p=P)[:, :, bass.ds(i * P, P)]
                sp.dma_start(m.nat[:, s, 2, :].rearrange("p (h i) -> p h i", h=KD), src).then_inc(T.loaded[2][s], 16)
            with sp.Fori(0, STEPS // W) as r:
                for u in range(W):
                    load(r * W + u, u)

        @block.gpsimd
        def _(pool):
            def scan_weights(i):
                tri = bc(bc(t.tri[:, :].rearrange("p (x y l) -> p x y l", x=1, y=1), 1, BATCH), 2, 2)
                for dst, src in ((m.atri_hi, m.a_hi[:, :, :].bitcast(F32)), (m.atri_lo, m.a_lo[:, :, :])):
                    col = bc(src[:, :, bass.ds(i * 2, 2)].rearrange("p b (j l) -> p b j l", l=1), 3, SEQ)
                    ins = pool.tensor_tensor(dst[:, :].rearrange("p (b j l) -> p b j l", b=BATCH, j=2), tri, col, ALU.mult)
                ins.then_inc(atri_ready, 1)

            def step(i, last=False):
                pool.wait_ge(exp_done, i + 1)
                ev = m.e[:, :].rearrange("p (b j l) -> p b j l", b=BATCH, j=2)
                gm = bc(m.gm[:, :, :].rearrange("p b (x l) -> p b x l", x=1), 2, 2)
                pool.tensor_tensor(m.mt[:, :].rearrange("p (b j l) -> p b j l", b=BATCH, j=2), ev, gm,
                                   ALU.mult).then_inc(m_ready, 1)
                if not last:
                    scan_weights(i + 1)
                pool.wait_ge(y_ready, i + 1)
                c = Chain(pool, pchain, 2 * i)
                c.link(pool.tensor_tensor(m.yg[:, :], m.y[:, :], m.sg[:, :], ALU.mult))
                c.link(pool.tensor_tensor(m.yg[:, :], m.yg[:, :], m.yg[:, :], ALU.mult))
                pool.tensor_tensor(m.sumsq[:, :], m.sumsq[:, :], m.yg[:, :], ALU.add).then_inc(sq_done, 1)

            pool.sem_inc(sq_done, 1)
            scan_weights(0)
            with pool.Fori(0, STEPS // W - 1) as r:
                for u in range(W):
                    step(r * W + u)
            for i in range(STEPS - W, STEPS):
                step(i, i == STEPS - 1)

        @block.scalar
        def _(act):
            def copy_x(i):
                act.wait_ge(x_filled, i + 1)
                act.wait_ge(conved, i + 1)
                act.activation(m.xpad[:, :, 3:3 + SEQ], XBK[:, 0:TOK].rearrange("p (b s) -> p b s", b=BATCH),
                               ACT.Copy).then_inc(x_copied, 1)

            def tanh_of_x(i):
                act.wait_ge(conved, i + 2)
                act.activation(m.th[:, :], m.z[:, :], ACT.Tanh, scale=0.5).then_inc(tanh_x, 1)

            def step(i, u, last=False):
                act.wait_ge(s_filled, i + 1)
                act.activation(m.e[:, :], GBK[:, :], ACT.Exp).then_inc(exp_done, 1)
                if not last:
                    T.scalar(act, i + 1, 0, 1 - u)
                act.wait_ge(gate_filled, i + 1)
                act.activation(m.thg[:, :], GBK[:, 0:TOK], ACT.Tanh, scale=0.5).then_inc(tanh_g, 1)
                if not last:
                    T.scalar(act, i + 1, 1, 1 - u)
                act.wait_ge(ynw_ready, i + 1)
                act.activation(m.yn_hi[:, :], m.ynw[:, :], ACT.Copy).then_inc(yn_hi, 1)
                if not last:
                    copy_x(i + 1)
                    tanh_of_x(i + 1)
                    T.scalar(act, i + 1, 2, 1 - u)

            for w in range(3):
                T.scalar(act, 0, w, 0)
            copy_x(0)
            tanh_of_x(0)
            with act.Fori(0, STEPS // W - 1) as r:
                for u in range(W):
                    step(r * W + u, u)
            for i in range(STEPS - W, STEPS):
                step(i, i % W, i == STEPS - 1)
            act.wait_ge(var_ready, 1)
            act.activation(m.std[:, :], m.var[:, :], ACT.Sqrt, bias=t.eps[:, 0:1]).then_inc(std_ready, 1)

        @block.vector
        def _(dve):
            def make_x(i):
                dve.wait_ge(tanh_x, i + 1)
                dve.scalar_tensor_tensor(m.xs[:, :], m.th[:, :], 1.0, m.z[:, :], ALU.add,
                                         ALU.mult).then_inc(xs_ready, 1)

            def convolve(i):
                dve.wait_ge(x_copied, i + 1)
                conv(dve, Chain(dve, dchain, 3 * i), m, i, conved)

            def step(i, u, last=False):
                dve.wait_ge(xt_filled, i + 1)
                for j in range(2):
                    at = slice(j * HP, (j + 1) * HP)
                    ins = dve.tensor_tensor(
                        m.xdt[:, :, j, at],
                        XBK[:, 0:TOK].rearrange("p (b c) -> p b c", b=BATCH)[:, :, at],
                        bc(m.dth[:, :, bass.ds(i * 2 + j, 1)], 2, HP), ALU.mult)
                ins.then_inc(xdt_ready, 1)
                if not last:
                    T.vector(dve, i + 1, 0, 1 - u)
                dve.wait_ge(tanh_g, i + 1)
                dve.wait_ge(sq_done, i + 1)
                dve.scalar_tensor_tensor(m.sg[:, :], m.thg[:, :], 1.0, GBK[:, 0:TOK], ALU.add,
                                         ALU.mult).then_inc(sg_ready, 1)
                dve.wait_ge(y_filled, i + 1)
                dve.scalar_tensor_tensor(m.y[:, :], m.xs[:, :], m.dcol[:, bass.ds(i, 1)], XBK[:, 0:TOK], ALU.mult,
                                         ALU.add).then_inc(y_ready, 1)
                dve.wait_ge(y_ready, i + 1)
                dve.scalar_tensor_tensor(m.ynw[:, :], m.y[:, :], m.normw[:, bass.ds(i, 1)], m.sg[:, :], ALU.mult,
                                         ALU.mult).then_inc(ynw_ready, 1)
                if not last:
                    T.vector(dve, i + 1, 1, 1 - u)
                dve.wait_ge(yn_hi, i + 1)
                dve.tensor_tensor(m.yn_lo[:, :], m.ynw[:, :], m.yn_hi[:, :].bitcast(F32),
                                  ALU.subtract).then_inc(yn_lo, 1)
                if not last:
                    convolve(i + 1)
                    make_x(i + 1)
                    T.vector(dve, i + 1, 2, 1 - u)

            dve.sem_inc(T.lo, LO_CREDIT)
            dve.sem_inc(conved, 1)
            dve.sem_inc(sg_ready, 1)
            for w in range(3):
                T.vector(dve, 0, w, 0)
            convolve(0)
            make_x(0)
            with dve.Fori(0, STEPS // W - 1) as r:
                for u in range(W):
                    step(r * W + u, u)
            for i in range(STEPS - W, STEPS):
                step(i, i % W, i == STEPS - 1)
            dve.wait_ge(sum_filled, 1)
            dve.tensor_scalar(m.var[:, :], XBK[:, 0:BATCH], 0.25 / INTER, None, ALU.mult).then_inc(var_ready, 1)
            dve.wait_ge(std_ready, 1)
            dve.reciprocal(m.rstd[:, :], m.std[:, :]).then_inc(rstd_ready, 1)
            dve.wait_ge(rstd_ready, 1)
            dve.wait_ge(mixed, 1)
            for b in range(BATCH):
                for h in range(2):
                    at = slice(h * HALF, (h + 1) * HALF)
                    dve.scalar_tensor_tensor(t.x_res[:, b, at], t.bank[2 * b + h][:, :], m.rstd[:, b:b + 1],
                                             t.x_res[:, b, at], ALU.mult, ALU.add)

        @block.tensor
        def _(pe):
            def project_x(i, s):
                T.ready(pe, i, 0)
                project(pe, t, m, XBK[:, 0:TOK], 0, s).then_inc(x_filled, 1)

            def step(r, u, last=False):
                i = r * W + u
                landed = 16 * r + 16 * (1 + u)
                pe.wait_ge(xs_ready, i + 1)
                for b in range(BATCH):
                    mm = pe.transpose(XBK[:, b * P:(b + 1) * P], m.xs[:, b * SEQ:(b + 1) * SEQ], t.ident[:, :])
                mm.then_inc(xt_filled, 1)
                pe.wait_ge(atri_ready, i + 1)
                pe.wait_ge(sg_ready, i + 1)
                pe.matmul(GBK[:, :], t.after[:, :], m.atri_hi[:, :], start=True, stop=False)
                pe.matmul(GBK[:, :], t.after[:, :], m.atri_lo[:, :], start=False, stop=True).then_inc(s_filled, 1)
                if not last:
                    T.tensor(pe, i + 1, 0, 1 - u, landed)
                T.ready(pe, i, 1)
                pe.wait_ge(exp_done, i + 1)
                project(pe, t, m, GBK[:, 0:TOK], 1, u).then_inc(gate_filled, 1)
                pe.wait_ge(xdt_ready, i + 1)
                pe.wait_ge(m_ready, i + 1)
                for b in range(BATCH):
                    for j in range(2):
                        at = (2 * b + j) * SEQ
                        mm = pe.matmul(XBK[:, b * SEQ:(b + 1) * SEQ], m.xdt[:, b, j, :], m.mt[:, at:at + SEQ],
                                       start=j == 0, stop=j == 1)
                mm.then_inc(y_filled, 1)
                if not last:
                    T.tensor(pe, i + 1, 1, 1 - u, landed)
                    pe.wait_ge(y_ready, i + 1)
                    project_x(i + 1, 1 - u)
                    T.tensor(pe, i + 1, 2, 1 - u, landed)
                T.ready(pe, i, 2)
                pe.wait_ge(yn_lo, i + 1)
                mm = accumulate(pe, t, m, m.yn_hi, m.yn_lo, u, last)
                if last:
                    mm.then_inc(mixed, 1)

            pe.sem_inc(T.turned, T_CREDIT)
            zero_sums(pe, t)
            for w in range(3):
                T.tensor(pe, 0, w, 0, 16)
            project_x(0, 0)
            with pe.Fori(0, STEPS // W - 1) as r:
                for u in range(W):
                    step(r, u)
            for i in range(STEPS - W, STEPS):
                step(i // W, i % W, i == STEPS - 1)
            pe.wait_ge(sq_done, STEPS + 1)
            for b in range(BATCH):
                mm = pe.matmul(XBK[:, b:b + 1], m.sumsq[:, b * SEQ:(b + 1) * SEQ], t.ones[:, 0:1],
                               start=True, stop=True)
            mm.then_inc(sum_filled, 1)


def router_block(nc, sem, gate_w, t, r):
    loaded, turned, gw_hi, gw_lo = (sem("rt_" + x) for x in ("loaded", "turned", "hi", "lo"))
    logits_filled, max_ready, exp_done, comb_ready, comb_turned, combT_ready, spread, spread_read = (
        sem("rt_" + x) for x in ("logits", "max", "exp", "comb", "cturned", "cT", "spread", "sread"))
    logitT_ready = sem("rt_logitT")
    sel_steps, ltri_ready, chain = sem("rt_sel"), sem("rt_ltri"), sem("rt_chain")
    TILES = PAIRS
    with nc.Block() as block:
        @block.sync
        def _(sp):
            for a in range(4):
                sp.dma_start(blocks_by_quad(r.gw[:, :])[:, a], by_quad(gate_w)[:, a]).then_inc(loaded, 16)

        @block.gpsimd
        def _(pool):
            pool.memset(r.sel[:, :, :], 0.0).then_inc(sel_steps, 1)
            pool.memset(r.ltri[:, :, :], 1.0).then_inc(sel_steps, 1)
            pool.memset(r.comb[:, TILES:TILES + 1, :], 1.0).then_inc(sel_steps, 1)
            pool.wait_ge(sel_steps, 3)
            pool.affine_select(out=r.ltri[:, :, :], in_=r.ltri[:, :, :], compare_op=ALU.is_gt, fill=0.0, base=0,
                               pattern=[[1, EXPERTS], [-1, EXPERTS]], channel_multiplier=0).then_inc(ltri_ready, 1)
            for half in range(2):
                view = r.sel[:, :, half * HP:(half + 1) * HP]
                pool.affine_select(out=view, in_=view, compare_op=ALU.not_equal, fill=1.0, base=-half,
                                   pattern=[[-2, PAIRS], [0, HP]], channel_multiplier=1).then_inc(sel_steps, 1)

        @block.scalar
        def _(act):
            act.wait_ge(turned, 1)
            act.activation(r.gw_hi[:, :], t.bank[0][:, 0:KD * EXPERTS], ACT.Copy).then_inc(gw_hi, 1)
            for b in range(BATCH):
                act.wait_ge(max_ready, 1)
                act.activation(r.prob[:, b, :], r.logit[:, b, :], ACT.Exp, bias=r.negmax[:, b:b + 1],
                               accum_out=r.psum[:, b:b + 1]).then_inc(exp_done, 1)
            act.wait_ge(comb_turned, 1)
            act.activation(r.combT[:, :], t.bank[7][0:EXPERTS, 0:TOK], ACT.Copy).then_inc(combT_ready, 1)
            for n in range(TILES // 2):
                act.wait_ge(spread, n + 1)
                act.activation(r.comb[:, 2 * n:2 * n + 2, :], t.bank[n % 4 + 3][:, :].rearrange("p (a s) -> p a s", a=2),
                               ACT.Copy).then_inc(spread_read, 1)

        @block.vector
        def _(dve):
            c = Chain(dve, chain)
            dve.wait_ge(gw_hi, 1)
            dve.tensor_tensor(r.gw_lo[:, :], t.bank[0][:, 0:KD * EXPERTS], r.gw_hi[:, :].bitcast(F32),
                              ALU.subtract).then_inc(gw_lo, 1)
            dve.wait_ge(logits_filled, 1)
            dve.tensor_copy(r.logitT[:, :], t.bank[1][0:EXPERTS, 0:TOK]).then_inc(logitT_ready, 1)
            dve.wait_ge(logits_filled, 2)
            c.link(dve.tensor_copy(r.logit[:, :, :], t.bank[2][:, 0:BATCH * EXPERTS].rearrange("p (b e) -> p b e", b=BATCH)))
            c.link(dve.tensor_reduce(r.negmax[:, :], r.logit[:, :, :], AX.X, ALU.max))
            dve.tensor_scalar(r.negmax[:, :], r.negmax[:, :], -1.0, None, ALU.mult).then_inc(max_ready, 1)
            dve.wait_ge(exp_done, 2)
            c.link(dve.reciprocal(r.psum[:, :], r.psum[:, :]))
            dve.wait_ge(ltri_ready, 1)
            for b in range(BATCH):
                c.link(dve.tensor_scalar(r.prob[:, b, :], r.prob[:, b, :], r.psum[:, b:b + 1], None, ALU.mult))
                pj = bc(r.prob[:, b, :].rearrange("p (a j) -> p a j", a=1), 1, EXPERTS)
                pe_ = bc(r.prob[:, b, :].rearrange("p (e a) -> p e a", a=1), 2, EXPERTS)
                c.link(dve.tensor_tensor(r.eq[:, :, :], pj, pe_, ALU.is_equal))
                c.link(dve.tensor_tensor(r.eq[:, :, :], r.eq[:, :, :], r.ltri[:, :, :], ALU.mult))
                c.link(dve.tensor_tensor(r.gt[:, :, :], pj, pe_, ALU.is_gt))
                c.link(dve.tensor_tensor(r.gt[:, :, :], r.gt[:, :, :], r.eq[:, :, :], ALU.add))
                c.link(dve.tensor_reduce(r.rank[:, :], r.gt[:, :, :], AX.X, ALU.add))
                dve.scalar_tensor_tensor(r.weight[:, b, :], r.rank[:, :], TOPK - 0.5, r.prob[:, b, :], ALU.is_lt,
                                         ALU.mult).then_inc(comb_ready, 1)

        @block.tensor
        def _(pe):
            pe.wait_ge(loaded, 64)
            for k in range(KD):
                mm = pe.transpose(t.bank[0][:, k * EXPERTS:(k + 1) * EXPERTS], r.gw[:, k * P:(k + 1) * P],
                                  t.ident[0:EXPERTS, 0:EXPERTS])
            mm.then_inc(turned, 1)
            pe.wait_ge(gw_lo, 1)
            out = t.bank[1][0:EXPERTS, 0:TOK]
            for k in range(KD):
                es = slice(k * EXPERTS, (k + 1) * EXPERTS)
                pe.matmul(out, r.gw_hi[:, es], t.xn_hi[:, k, :], start=k == 0, stop=False)
                pe.matmul(out, r.gw_hi[:, es], t.xn_lo[:, k, :], start=False, stop=False)
                pe.matmul(out, r.gw_lo[:, es], t.xn_hi[:, k, :], start=False, stop=False)
                mm = pe.matmul(out, r.gw_lo[:, es], t.xn_lo[:, k, :], start=False, stop=k == KD - 1)
            mm.then_inc(logits_filled, 1)
            pe.wait_ge(logitT_ready, 1)
            for b in range(BATCH):
                mm = pe.transpose(t.bank[2][:, b * EXPERTS:(b + 1) * EXPERTS], r.logitT[:, b * SEQ:(b + 1) * SEQ],
                                  t.ident[0:EXPERTS, 0:EXPERTS])
            mm.then_inc(logits_filled, 1)
            for b in range(BATCH):
                pe.wait_ge(comb_ready, b + 1)
                mm = pe.transpose(t.bank[7][0:EXPERTS, b * SEQ:(b + 1) * SEQ], r.weight[:, b, :], t.ident[:, :])
            mm.then_inc(comb_turned, 1)
            pe.wait_ge(combT_ready, 1)
            pe.wait_ge(sel_steps, 5)
            for n in range(TILES // 2):
                if n >= 4:
                    pe.wait_ge(spread_read, n - 3)
                for v in range(2):
                    mm = pe.matmul(t.bank[n % 4 + 3][:, v * TOK:(v + 1) * TOK], r.sel[:, 2 * n + v, :],
                                   r.combT[:, :], start=True, stop=True)
                mm.then_inc(spread, 1)


def ffn_block(nc, sem, w1, w2, sw1, sw2, out, t, f, comb):
    turned, w_hi_done, lo_dve, lo_pool = (sem("ffn_" + x) for x in ("turned", "hi", "lo_dve", "lo_pool"))
    rows_loaded = [sem(f"ffn_rows{s}") for s in range(3)]
    cols_loaded = [sem(f"ffn_cols{c}") for c in range(3)]
    GBK, UBK = t.bank[6], t.bank[7]
    gate_filled, silu_done, sgc_ready, up_filled, act_ready, act_hi, act_lo, summed, y_ready, stored = (
        sem("ffn_" + x) for x in ("gate", "silu", "sgc", "up", "act", "acthi", "actlo", "summed", "y", "stored"))
    cw_ready = sem("ffn_cw")
    SHARED = PAIRS
    CREDIT = 6

    def slot(j):
        return j % JB % 3

    def uses(s):
        return len([j for j in range(JB) if slot(j) == s])

    def rows_landed(q, j):
        q, j = q + j // JB, j % JB
        return q * (64 * uses(slot(j))) + 64 * (j // 3 + 1)

    with nc.Block() as block:
        @block.sync
        def _(sp):
            def load_rows(step, j, src):
                sp.wait_ge(turned, 3 * step + 2)
                for a in range(4):
                    sp.dma_start(f.nat[a * Q:(a + 1) * Q, slot(j), :, :], src(a)).then_inc(rows_loaded[slot(j)], 16)

            def load_cols(c, src):
                n = min(4, JB - 4 * c) * Q
                for a in range(4):
                    sp.dma_start(f.nat_c[a * Q:(a + 1) * Q, c, :, 0:n], src(a, 4 * c * Q, n)).then_inc(cols_loaded[c], 16)

            def rows_of(q, j):
                def src(a):
                    return w1.rearrange("e (s o) h -> o (e s) h", s=4)[
                        j * Q:(j + 1) * Q, bass.ds(q * 8, 8), a * 2 * P:(a + 1) * 2 * P]
                return src

            def cols_of(q):
                def src(a, col, n):
                    at = a % 2 * QW + col
                    return w2.rearrange("e (b p) i -> p e b i", p=Q)[
                        :, bass.ds(q * 2 + a // 2, 1), :, at:at + n].rearrange("p e b i -> p (e b) i")
                return src

            def shared_rows(j):
                def src(a):
                    return sw1.rearrange("(s o) h -> o s h", s=8)[j * Q:(j + 1) * Q, :, a * 2 * P:(a + 1) * 2 * P]
                return src

            def shared_cols(a, col, n):
                return sw2.rearrange("(b p) i -> p b i", p=Q)[:, :, a * QW + col:a * QW + col + n]

            def pair(q, rows, cols, next_cols):
                for j in range(JB):
                    load_rows(q * JB + j, j, rows(j))
                    if j == 0:
                        load_cols(1, cols)
                    elif j == 4:
                        load_cols(2, cols)
                    elif j == 8 and next_cols is not None:
                        load_cols(0, next_cols)

            load_cols(0, cols_of(0))
            with sp.Fori(0, PAIRS - 1) as q:
                pair(q, lambda j: rows_of(q, j), cols_of(q), cols_of(q + 1))
            pair(PAIRS - 1, lambda j: rows_of(PAIRS - 1, j), cols_of(PAIRS - 1), shared_cols)
            pair(SHARED, shared_rows, shared_cols, None)
            for b in range(BATCH):
                sp.wait_ge(y_ready, 2 * b + 2)
                sp.dma_start(out[b], t.x_res[:, b, :]).then_inc(stored, 16)
            sp.wait_ge(stored, 16 * BATCH)

        @block.gpsimd
        def _(pool):
            def split_up(step, s):
                pool.wait_ge(w_hi_done, 3 * step + 2)
                pool.tensor_tensor(f.w_lo[:, s, 1, :], f.wt[:, 1, :], f.w_hi[:, s, 1, :].bitcast(F32),
                                   ALU.subtract).then_inc(lo_pool, 1)

            def pair(q, last=False):
                pool.tensor_copy(f.cw[:, :], comb[:, bass.ds(q, 1), :].rearrange("p a s -> p (a s)")).then_inc(cw_ready, 1)
                pool.wait_ge(cw_ready, q + 1)
                for j in range(JB):
                    step = q * JB + j
                    pool.wait_ge(silu_done, step + 2)
                    pool.wait_ge(act_ready, step + 1)
                    pool.tensor_tensor(f.sgc[:, :], f.sg[:, :], f.cw[:, :], ALU.mult).then_inc(sgc_ready, 1)
                    if not (last and j == JB - 1):
                        split_up(step + 1, slot(j + 1))
                pool.wait_ge(sgc_ready, q * JB + (JB + 1))
            pool.sem_inc(lo_pool, 1)
            split_up(0, 0)
            with pool.Fori(0, PAIRS) as q:
                pair(q)
            pair(SHARED, last=True)

        @block.scalar
        def _(act):
            def hi(step, w, s):
                act.wait_ge(turned, 3 * step + (w + 1 + CREDIT))
                act.activation(f.w_hi[:, s, w, :], f.wt[:, w, :], ACT.Copy).then_inc(w_hi_done, 1)

            def silu(step):
                act.wait_ge(gate_filled, step + 1)
                act.wait_ge(sgc_ready, step + 1)
                act.activation(f.sg[:, :], GBK[:, 0:TOK], ACT.Silu).then_inc(silu_done, 1)

            def pair(q, last=False):
                for j in range(JB):
                    step, left = q * JB + j, JB - 1 - j if last else JB
                    if left:
                        hi(step + 1, 1, slot(j + 1))
                    act.wait_ge(act_ready, step + 2)
                    act.activation(f.a_hi[:, :], f.a[:, :], ACT.Copy).then_inc(act_hi, 1)
                    if left:
                        hi(step + 1, 2, slot(j + 1))
                        silu(step + 1)
                    if left > 1:
                        hi(step + 2, 0, slot(j + 2))
            act.sem_inc(silu_done, 1)
            act.sem_inc(sgc_ready, 1)
            for w in range(3):
                hi(0, w, 0)
            silu(0)
            hi(1, 0, 1)
            with act.Fori(0, PAIRS) as q:
                pair(q)
            pair(SHARED, last=True)

        @block.vector
        def _(dve):
            def turn_rows(q, j, w, shared=False):
                step = q * JB + j
                if w == 0:
                    dve.wait_ge(lo_dve, 2 * step + 1)
                else:
                    dve.wait_ge(lo_pool, step + 1)
                if w == 0:
                    dve.wait_ge(rows_loaded[slot(j)], rows_landed(q, j))
                for e in range(2):
                    at = 4 * w + 2 * e if shared else 4 * e + 2 * w
                    ins = dve.transpose(
                        f.wt[:, w, :].rearrange("p (k b o) -> p b k o", k=KD, b=4)[:, 2 * e:2 * e + 2],
                        f.nat[:, slot(j), at:at + 2, :].rearrange("p c (k h) -> p c k h", k=KD))
                ins.then_inc(turned, 1)

            def turn_cols(q, j):
                c, jj = j % JB // 4, j % JB % 4
                dve.wait_ge(lo_dve, 2 * (q * JB + j) + 2)
                dve.wait_ge(cols_loaded[c], (q + j // JB) * 64 + 64)
                dve.transpose(f.wt[:, 2, :].rearrange("p (b h) -> p b h", h=Q),
                              f.nat_c[:, c, :, jj * Q:(jj + 1) * Q]).then_inc(turned, 1)

            def lo(step, w, s):
                dve.wait_ge(w_hi_done, 3 * step + (w + 1))
                dve.tensor_tensor(f.w_lo[:, s, w, :], f.wt[:, w, :], f.w_hi[:, s, w, :].bitcast(F32),
                                  ALU.subtract).then_inc(lo_dve, 1)

            def pair(q, last=False, before_last=False):
                for j in range(JB):
                    step, left = q * JB + j, JB - 1 - j if last else JB
                    if left:
                        lo(step + 1, 0, slot(j + 1))
                        turn_rows(q, j + 1, 1, last or before_last and j + 1 >= JB)
                    dve.wait_ge(up_filled, step + 1)
                    dve.wait_ge(sgc_ready, step + 2)
                    dve.tensor_tensor(f.a[:, :], UBK[:, 0:TOK], f.sgc[:, :], ALU.mult).then_inc(act_ready, 1)
                    if left:
                        turn_cols(q, j + 1)
                    dve.wait_ge(act_hi, step + 1)
                    dve.tensor_tensor(f.a_lo[:, :], f.a[:, :], f.a_hi[:, :].bitcast(F32),
                                      ALU.subtract).then_inc(act_lo, 1)
                    if left > 1:
                        turn_rows(q, j + 2, 0, last or before_last and j + 2 >= JB)
                    if left:
                        lo(step + 1, 2, slot(j + 1))
            dve.sem_inc(turned, CREDIT)
            dve.sem_inc(lo_dve, 2)
            dve.sem_inc(act_ready, 1)
            turn_rows(0, 0, 0)
            turn_rows(0, 0, 1)
            lo(0, 0, 0)
            turn_cols(0, 0)
            turn_rows(0, 1, 0)
            lo(0, 2, 0)
            with dve.Fori(0, PAIRS - 1) as q:
                pair(q)
            pair(PAIRS - 1, before_last=True)
            pair(SHARED, last=True)
            dve.wait_ge(summed, 1)
            for b in range(BATCH):
                for h in range(2):
                    at = slice(h * HALF, (h + 1) * HALF)
                    dve.tensor_tensor(t.x_res[:, b, at], t.bank[2 * b + h][:, :], t.x_res[:, b, at],
                                      ALU.add).then_inc(y_ready, 1)

        @block.tensor
        def _(pe):
            def gate(step, s):
                pe.wait_ge(lo_dve, 2 * step + 3)
                pe.wait_ge(silu_done, step + 1)
                project(pe, t, f, GBK[:, 0:TOK], 0, s).then_inc(gate_filled, 1)

            def pair(q, last=False):
                for j in range(JB):
                    step, end = q * JB + j, last and j == JB - 1
                    pe.wait_ge(lo_pool, step + 2)
                    pe.wait_ge(act_ready, step + 1)
                    project(pe, t, f, UBK[:, 0:TOK], 1, slot(j)).then_inc(up_filled, 1)
                    if not end:
                        gate(step + 1, slot(j + 1))
                    pe.wait_ge(lo_dve, 2 * step + 4)
                    pe.wait_ge(act_lo, step + 1)
                    mm = accumulate(pe, t, f, f.a_hi, f.a_lo, slot(j), end)
                    if end:
                        mm.then_inc(summed, 1)

            zero_sums(pe, t)
            gate(0, 0)
            with pe.Fori(0, PAIRS) as q:
                pair(q)
            pair(SHARED, last=True)


class Tensors:
    pass


def program(nc, x, ctx_1024, mask, Wq, Wk, Wv, Wo, in_proj_w, conv_w, conv_b, A_log, dt_bias, D, norm_w,
            out_proj_w, gate_w, w1, w2, shared_w1, shared_w2, out):
    with ExitStack() as whole:
        def sem(name):
            return whole.enter_context(nc.semaphore(name))

        def maker(stack, prefix):
            def sb(name, shape, dt=F32):
                return stack.enter_context(nc.sbuf_tensor(prefix + name, shape, dt))
            return sb

        t = Tensors()
        sb = maker(whole, "t_")
        t.x_res = sb("x_res", [P, BATCH, DM])
        t.xn_hi = sb("xn_hi", [P, KD, TOK], F32R)
        t.xn_lo = sb("xn_lo", [P, KD, TOK], F32R)
        t.ident = sb("ident", [P, P])
        t.ones = sb("ones", [P, P])
        t.tri = sb("tri", [P, P])
        t.after = sb("after", [P, P], F32R)
        t.zeros = sb("zeros", [P, P], F32R)
        t.eps = sb("eps", [P, 1])
        t.stats = sb("stats", [P, BATCH, 2, 6])
        t.meanvar = sb("meanvar", [P, BATCH, 2])
        t.std = sb("std", [P, BATCH])
        t.rstd = sb("rstd", [P, BATCH])
        t.bank = [whole.enter_context(nc.psum_tensor(f"bank{n}", [P, HALF], F32)) for n in range(8)]

        made = sem("masks_made")
        with nc.sbuf_tensor("after_f", [P, P], F32) as after_f, nc.Block() as block:
            @block.gpsimd
            def _(pool):
                pool.memset(t.ident[:, :], 0.0).then_inc(made, 1)
                pool.memset(t.ones[:, :], 1.0).then_inc(made, 1)
                pool.memset(t.tri[:, :], 1.0).then_inc(made, 1)
                pool.memset(after_f[:, :], 1.0).then_inc(made, 1)
                pool.memset(t.zeros[:, :].bitcast(F32), 0.0).then_inc(made, 1)
                pool.wait_ge(made, 5)
                pool.affine_select(out=t.ident[:, :], in_=t.ident[:, :], compare_op=ALU.not_equal, fill=1.0, base=0,
                                   pattern=[[-1, P]], channel_multiplier=1)
                pool.affine_select(out=t.tri[:, :], in_=t.tri[:, :], compare_op=ALU.is_ge, fill=0.0, base=0,
                                   pattern=[[1, P]], channel_multiplier=-1)
                pool.affine_select(out=after_f[:, :], in_=after_f[:, :], compare_op=ALU.is_gt, fill=0.0, base=0,
                                   pattern=[[-1, P]], channel_multiplier=1).then_inc(made, 1)
                pool.wait_ge(made, 6)
                pool.tensor_copy(t.after[:, :], after_f[:, :])

        def layernorm(**kw):
            with ExitStack() as stack:
                t.xn = stack.enter_context(nc.sbuf_tensor(f"ln{len(normed)}_xn", [P, BATCH, DM], F32))
                layernorm_block(nc, ln_sems, len(normed), t, len(normed) in QUAD_ROUNDS, **kw)
            normed.append(1)
        normed = []
        ln_sems = [sem("ln_" + x) for x in ("x_in", "chain", "var", "std", "xn", "turned", "hi", "lo")]

        layernorm(load_x=x)
        with ExitStack() as stack:
            a = Tensors()
            sb = maker(stack, "a_")
            a.ctx_hi = sb("ctx_hi", [P, KC, CTX], F32R)
            a.ctx_lo = sb("ctx_lo", [P, KC, CTX], F32R)
            a.k_hi = sb("k_hi", [P, CTX], F32R)
            a.k_lo = sb("k_lo", [P, CTX], F32R)
            a.v_hi = sb("v_hi", [P, CTX // P, HD], F32R)
            a.v_lo = sb("v_lo", [P, CTX // P, HD], F32R)
            a.v_stage = sb("v_stage", [P, 2, HALF])
            a.q_hi = sb("q_hi", [P, 2 * SEQ], F32R)
            a.q_lo = sb("q_lo", [P, 2 * SEQ], F32R)
            a.p = sb("p", [P, 2, CTX])
            a.pt_hi = sb("pt_hi", [P, 3, HALF], F32R)
            a.pt_lo = sb("pt_lo", [P, 3, HALF], F32R)
            a.w_nat = sb("w_nat", [P, 2 * DM])
            a.w_hi = sb("w_hi", [P, 2 * DM], F32R)
            a.w_lo = sb("w_lo", [P, 2 * DM], F32R)
            a.kv_nat = sb("kv_nat", [P, 2, KC, HD])
            a.kv_hi = sb("kv_hi", [P, 2, KC, HD], F32R)
            a.kv_lo = sb("kv_lo", [P, 2, KC, HD], F32R)
            a.mask_raw = sb("mask_raw", [P, CTX], U8)
            a.mask_bias = sb("mask_bias", [P, CTX], mybir.dt.bfloat16)
            a.any_valid = sb("any_valid", [P, BATCH])
            a.mark = sb("mark", [P, 8])
            a.chunkmax = sb("chunkmax", [P, 8])
            a.rowmax = sb("rowmax", [P, 2])
            a.negmax = sb("negmax", [P, 2])
            a.psum = sb("psum", [P, 2])
            a.rinv = sb("rinv", [P, 2])
            a.diag = sb("diag", [P, 2 * SEQ])
            a.rb = sb("rb", [P, 2 * SEQ])
            a.ot = sb("ot", [P, 2 * SEQ])
            a.ot_hi = sb("ot_hi", [P, 2 * SEQ], F32R)
            a.ot_lo = sb("ot_lo", [P, 2 * SEQ], F32R)
            attention_block(nc, sem, ctx_1024, mask, Wq, Wk, Wv, Wo, t, a)

        layernorm()
        with ExitStack() as stack:
            m = Tensors()
            sb = maker(stack, "m_")
            m.nat = sb("nat", [P, 2, 3, DM])
            m.w_hi = sb("w_hi", [P, 2, 3, DM], F32R)
            m.w_lo = sb("w_lo", [P, 2, 3, DM], F32R)
            m.convw = sb("convw", [P, XB + 2, 4])
            m.convb = sb("convb", [P, XB + 2])
            m.normw = sb("normw", [P, XB])
            m.dcol = sb("dcol", [P, XB])
            m.dtb = sb("dtb", [P, SSM_H])
            m.alog = sb("alog", [P, SSM_H])
            m.ea = sb("ea", [P, SSM_H])
            m.zdt = sb("zdt", [P, BATCH, SSM_H])
            m.nabs = sb("nabs", [P, BATCH, SSM_H])
            m.e_dt = sb("e_dt", [P, BATCH, SSM_H])
            m.w_dt = sb("w_dt", [P, BATCH, SSM_H])
            m.ln_dt = sb("ln_dt", [P, BATCH, SSM_H])
            m.d_dt = sb("d_dt", [P, BATCH, SSM_H])
            m.is0 = sb("is0", [P, BATCH, SSM_H])
            m.dth = sb("dth", [P, BATCH, SSM_H])
            m.a = sb("a", [P, BATCH, SSM_H])
            m.a_lo = sb("a_lo", [P, BATCH, SSM_H])
            m.a_hi = sb("a_hi", [P, BATCH, SSM_H], F32R)
            m.xpad = sb("xpad", [P, BATCH, SEQ + 3])
            m.z = sb("z", [P, TOK])
            m.th = sb("th", [P, TOK])
            m.xs = sb("xs", [P, TOK])
            m.thg = sb("thg", [P, TOK])
            m.sg = sb("sg", [P, TOK])
            m.y = sb("y", [P, TOK])
            m.ynw = sb("ynw", [P, TOK])
            m.yg = sb("yg", [P, TOK])
            m.sumsq = sb("sumsq", [P, TOK])
            m.dtT = sb("dtT", [SSM_H, TOK])
            m.bc = sb("bc", [P, 2, TOK])
            m.gm = sb("gm", [P, BATCH, SEQ])
            m.xdt = sb("xdt", [P, BATCH, 2, P])
            m.atri_hi = sb("atri_hi", [P, HALF], F32R)
            m.atri_lo = sb("atri_lo", [P, HALF], F32R)
            m.e = sb("e", [P, HALF])
            m.mt = sb("mt", [P, HALF])
            m.yn_hi = sb("yn_hi", [P, TOK], F32R)
            m.yn_lo = sb("yn_lo", [P, TOK], F32R)
            m.var = sb("var", [P, BATCH])
            m.std = sb("std", [P, BATCH])
            m.rstd = sb("rstd", [P, BATCH])
            mixer_head_block(nc, sem, in_proj_w, conv_w, conv_b, A_log, dt_bias, D, norm_w, t, m)
            mixer_block(nc, sem, in_proj_w, out_proj_w, t, m)

        layernorm()
        with ExitStack() as stack:
            comb = stack.enter_context(nc.sbuf_tensor("comb", [P, PAIRS + 1, TOK], F32))
            with ExitStack() as inner:
                r = Tensors()
                r.comb = comb
                sb = maker(inner, "r_")
                r.gw = sb("gw", [EXPERTS, DM])
                r.gw_hi = sb("gw_hi", [P, KD * EXPERTS], F32R)
                r.gw_lo = sb("gw_lo", [P, KD * EXPERTS], F32R)
                r.logit = sb("logit", [P, BATCH, EXPERTS])
                r.prob = sb("prob", [P, BATCH, EXPERTS])
                r.weight = sb("weight", [P, BATCH, EXPERTS])
                r.negmax = sb("negmax", [P, BATCH])
                r.psum = sb("psum", [P, BATCH])
                r.ltri = sb("ltri", [P, EXPERTS, EXPERTS])
                r.eq = sb("eq", [P, EXPERTS, EXPERTS])
                r.gt = sb("gt", [P, EXPERTS, EXPERTS])
                r.logitT = sb("logitT", [EXPERTS, TOK])
                r.rank = sb("rank", [P, EXPERTS])
                r.sel = sb("sel", [EXPERTS, PAIRS, P])
                r.combT = sb("combT", [EXPERTS, TOK])
                router_block(nc, sem, gate_w, t, r)
            f = Tensors()
            sb = maker(stack, "f_")
            f.nat = sb("nat", [P, 3, 8, 2 * P])
            f.nat_c = sb("nat_c", [P, 3, DM // Q, 4 * Q])
            f.wt = sb("wt", [P, 3, DM])
            f.w_hi = sb("w_hi", [P, 3, 3, DM], F32R)
            f.w_lo = sb("w_lo", [P, 3, 3, DM], F32R)
            f.sg = sb("sg", [P, TOK])
            f.sgc = sb("sgc", [P, TOK])
            f.a = sb("a", [P, TOK])
            f.cw = sb("cw", [P, TOK])
            f.a_hi = sb("a_hi", [P, TOK], F32R)
            f.a_lo = sb("a_lo", [P, TOK], F32R)
            ffn_block(nc, sem, w1, w2, shared_w1, shared_w2, out, t, f, comb)


_INS = ["x", "ctx_1024", "mask_BxS2_bf1", "L0_xattn_Wq", "L0_xattn_Wk", "L0_xattn_Wv", "L0_xattn_Wo",
        "L0_attn_in_proj_w", "L0_attn_conv_w", "L0_attn_conv_b", "L0_attn_A_log", "L0_attn_dt_bias", "L0_attn_D",
        "L0_attn_norm_w", "L0_attn_out_proj_w", "L0_ffn_gate_w", "L0_ffn_w1", "L0_ffn_w2", "L0_ffn_shared_w1",
        "L0_ffn_shared_w2"]


def kernel(**inputs):
    import numpy as np
    import concourse.bacc as bacc
    from concourse.bass_utils import run_bass_kernel_spmd

    nc = bacc.Bacc("TRN2", target_bir_lowering=False, num_devices=1)
    arrays, args = {}, []
    for name in _INS:
        v = np.ascontiguousarray(inputs[name])
        if v.dtype == np.bool_:
            v = v.view(np.uint8)
        arrays[f"in_{name}"] = v
        args.append(nc.dram_tensor(f"in_{name}", v.shape, mybir.dt.from_np(v.dtype), kind="ExternalInput").ap())
    args.append(nc.dram_tensor("out", (BATCH, SEQ, DM), F32, kind="ExternalOutput").ap())
    program(nc, *args)
    r = run_bass_kernel_spmd(nc, [arrays], core_ids=[0])
    return r.results[0]["out"]
```

```python
from contextlib import ExitStack

import concourse.bass as bass
from concourse import mybir

ALU = mybir.AluOpType
ACT = mybir.ActivationFunctionType
AX = mybir.AxisListType
F32 = mybir.dt.float32
F32R = mybir.dt.float32r
U8 = mybir.dt.uint8

P = 128
BATCH, SEQ, DM = 2, 128, 1024
KD = DM // P
TOK = BATCH * SEQ
CTX, DC = 2048, 512
KC = DC // P
HD = 128
KVH = 8
SCALE = 1.0 / float(HD) ** 0.5
MASKED = -1.0e30
LOWEST = -3.0e38
INTER, NST, SSM_H, HP = 4096, 128, 64, 64
XB = INTER // P
EXPERTS, TOPK, EI = 16, 6, 704
PAIR = 2 * EI
JB = PAIR // P
PAIRS = EXPERTS // 2
Q = 32
QW = PAIR // 4
EPS = 1e-5
QUAD_ROUNDS = (1, 2)
HALF = 512


class Chain:

    def __init__(self, eng, sem, base=0):
        self.eng, self.sem, self.base, self.n = eng, sem, base, 0

    def link(self, ins):
        self.n += 1
        ins.then_inc(self.sem, 1)
        self.eng.wait_ge(self.sem, self.base + self.n)


def bc(ap, dim, n):
    shape = list(ap.shape)
    shape[dim] = n
    return ap.broadcast_to(shape)


def split3(pe, out, pairs, first, last):
    n = len(pairs)
    for i, ((sh, sl), (mh, ml)) in enumerate(pairs):
        pe.matmul(out, sh, mh, start=first and i == 0, stop=False)
        pe.matmul(out, sh, ml, start=False, stop=False)
        mm = pe.matmul(out, sl, mh, start=False, stop=last and i == n - 1)
    return mm


def by_quad(row):
    return row.rearrange("p (a k h) -> p a k h", a=4, k=KD)


def blocks_by_quad(row):
    return row.rearrange("p (k a h) -> p a k h", a=4, k=KD)


def layernorm_block(nc, sems, round_, t, quads, load_x=None, load_ahead=None):
    x_in, chain, var_ready, std_ready, xn_ready, turned, hi_written, lo_written = sems
    two, four = 2 * round_, 4 * round_
    with nc.Block() as block:
        @block.sync
        def _(sp):
            if load_x is not None:
                for b in range(BATCH):
                    sp.dma_start(t.x_res[:, b, :], load_x[b]).then_inc(x_in, 16)
            if load_ahead is not None:
                load_ahead(sp)

        @block.vector
        def _(dve):
            c = Chain(dve, chain, 5 * round_)
            if load_x is not None:
                dve.wait_ge(x_in, 16 * BATCH)
            c.link(dve.memset(t.eps[:, :], EPS))
            for b in range(BATCH):
                for h in range(2):
                    ins = dve.bn_stats(t.stats[:, b, h, :], t.x_res[:, b, h * HALF:(h + 1) * HALF])
                c.link(ins)
                dve.bn_aggr(t.meanvar[:, b, :], t.stats[:, b, :, :]).then_inc(var_ready, 1)
            for b in range(BATCH):
                dve.wait_ge(std_ready, two + b + 1)
                c.link(dve.reciprocal(t.rstd[:, b:b + 1], t.std[:, b:b + 1]))
                rows, to = (by_quad(t.x_res[:, b, :]), blocks_by_quad(t.xn[:, b, :])) if quads else (t.x_res[:, b, :], t.xn[:, b, :])
                dve.tensor_scalar(to, rows, t.meanvar[:, b, 0:1],
                                  t.rstd[:, b:b + 1], ALU.subtract, ALU.mult).then_inc(xn_ready, 1)
            for b in range(BATCH):
                for g in range(2):
                    n = 2 * b + g
                    dve.wait_ge(hi_written, four + n + 1)
                    bank = t.bank[n][:, :].rearrange("p (k s) -> p k s", k=4)
                    at = (slice(None), slice(4 * g, 4 * g + 4), slice(b * SEQ, (b + 1) * SEQ))
                    dve.tensor_tensor(t.xn_lo[at], bank, t.xn_hi[at].bitcast(F32),
                                      ALU.subtract).then_inc(lo_written, 1)

        @block.scalar
        def _(act):
            for b in range(BATCH):
                act.wait_ge(var_ready, two + b + 1)
                act.activation(t.std[:, b:b + 1], t.meanvar[:, b, 1:2], ACT.Sqrt,
                               bias=t.eps[:, 0:1]).then_inc(std_ready, 1)
            for b in range(BATCH):
                for g in range(2):
                    n = 2 * b + g
                    act.wait_ge(turned, four + n + 1)
                    bank = t.bank[n][:, :].rearrange("p (k s) -> p k s", k=4)
                    act.activation(t.xn_hi[:, 4 * g:4 * g + 4, b * SEQ:(b + 1) * SEQ], bank,
                                   ACT.Copy).then_inc(hi_written, 1)

        @block.tensor
        def _(pe):
            for b in range(BATCH):
                pe.wait_ge(xn_ready, two + b + 1)
                for g in range(2):
                    for k in range(4):
                        at = (4 * g + k) * P
                        mm = pe.transpose(t.bank[2 * b + g][:, k * P:(k + 1) * P],
                                          t.xn[:, b, at:at + P], t.ident[:, :])
                    mm.then_inc(turned, 1)


def attention_block(nc, sem, ctx_in, mask, Wq, Wk, Wv, Wo, t, a):
    LOOP = KVH - 1
    ctx_loaded = [sem("ctx_loaded0"), sem("ctx_loaded1")]
    ctx_turned, ctx_hi, ctx_lo = (sem(f"ctx_{x}") for x in ("turned", "hi", "lo"))
    mask_loaded, mask_ready = sem("mask_loaded"), sem("mask_ready")
    kv_loaded, kv_hi, kv_lo = sem("kv_loaded"), sem("kv_hi"), sem("kv_lo")
    wq_loaded, wq_hi, wq_lo = sem("wq_loaded"), sem("wq_hi"), sem("wq_lo")
    wo_loaded, wo_hi, wo_lo = sem("wo_loaded"), sem("wo_hi"), sem("wo_lo")
    k_filled, k_hi, k_lo = sem("k_filled"), sem("k_hi"), sem("k_lo")
    q_filled, q_hi, q_lo = sem("q_filled"), sem("q_hi"), sem("q_lo")
    v_filled, v_raw, vt_filled, vt_hi, vt_lo = (sem(x) for x in ("v_filled", "v_raw", "vt_filled", "vt_hi", "vt_lo"))
    scores_filled, scores_read, negmax_ready, exp_done = (
        sem(x) for x in ("scores_filled", "scores_read", "negmax_ready", "exp_done"))
    diag_ready, rb_filled, rb_read = sem("diag_ready"), sem("rb_filled"), sem("rb_read")
    pt_filled, pt_hi, pt_lo = sem("pt_filled"), sem("pt_hi"), sem("pt_lo")
    pv_filled, ot_ready, ot_hi, ot_lo = sem("pv_filled"), sem("ot_ready"), sem("ot_hi"), sem("ot_lo")
    out_filled, out_read, zeroed = sem("out_filled"), sem("out_read"), sem("att_zeroed")
    chain, max_done, rinv_done = sem("att_chain"), sem("max_done"), sem("rinv_done")
    S = [t.bank[3], t.bank[4]]
    J = [t.bank[5], t.bank[6]]
    SCB = [S[0], S[1], J[1], J[0], S[0], S[1], J[1], S[0]]
    PTB = [S[0], S[1], J[1]]
    R = t.bank[7]
    PVB = t.bank[2]
    CH = CTX // HALF
    SB = CTX // P
    GR = SB // 2
    EARLY = 2

    with nc.Block() as block:
        @block.sync
        def _(sp):
            def load_kv(n, g):
                sp.wait_ge(kv_lo, n + 1)
                for i, w in enumerate((Wk, Wv)):
                    src = w.rearrange("(k p) n -> p k n", p=P)[:, :, bass.ds(g * HD, HD)]
                    sp.dma_start(a.kv_nat[:, i, :, :], src).then_inc(kv_loaded, 16)

            def load_wq(n, g, first=False):
                if not first:
                    sp.wait_ge(wq_lo, n + 1)
                    sp.wait_ge(wo_lo, n + 1)
                src = Wq.rearrange("(k p) n -> p k n", p=P)[:, :, bass.ds(g * 2 * HD, 2 * HD)]
                sp.dma_start(a.w_nat[:, :].rearrange("p (k n) -> p k n", k=KD), src).then_inc(wq_loaded, 16)

            def load_wo(n, g, last=False):
                if last:
                    sp.wait_ge(wo_lo, n + 2)
                else:
                    sp.wait_ge(wq_lo, n + 3)
                src = Wo.rearrange("(m p) n -> p m n", p=P)[:, bass.ds(g * 2, 2), :]
                sp.dma_start(a.w_nat[:, :].rearrange("p (j n) -> p j n", j=2), src).then_inc(wo_loaded, 16)

            for b in range(BATCH):
                n0 = KVH * b
                if b:
                    sp.wait_ge(mask_ready, 1)
                sp.dma_start(a.mask_raw[:, :], bc(mask[b:b + 1, :], 0, P)).then_inc(mask_loaded, 16)
                for i in range(SB // 2):
                    m = 8 * b + i
                    if i >= 2:
                        sp.wait_ge(ctx_turned, 2 * (m - 2) + 2)
                    elif b:
                        sp.wait_ge(wo_lo, n0 + 2)
                    dst = a.w_nat[:, (i % 2) * DM:(i % 2 + 1) * DM].rearrange("p (r c) -> p r c", r=2)
                    src = ctx_in[b, i * 2 * P:(i + 1) * 2 * P, :].rearrange("(r p) c -> p r c", p=P)
                    sp.dma_start(dst, src).then_inc(ctx_loaded[i % 2], 16)
                load_kv(n0, 0)
                sp.wait_ge(ctx_turned, SB * (b + 1))
                load_wq(n0, 0, first=True)
                with sp.Fori(0, LOOP) as g:
                    load_kv(g + (n0 + 1), g + 1)
                    load_wq(g + (n0 + 1), g + 1)
                    load_wo(g + n0, g)
                load_wo(n0 + LOOP, LOOP, last=True)

        @block.gpsimd
        def _(pool):
            def lo_of(lo, nat, hi, sem_done):
                pool.tensor_tensor(lo, nat, hi.bitcast(F32), ALU.subtract).then_inc(sem_done, 1)

            def split_kv(n):
                pool.wait_ge(kv_hi, n + 2)
                lo_of(a.kv_lo[:, :, :, :], a.kv_nat[:, :, :, :], a.kv_hi[:, :, :, :], kv_lo)

            def split_wq(n):
                pool.wait_ge(wq_hi, n + 2)
                lo_of(a.w_lo[:, :], a.w_nat[:, :], a.w_hi[:, :], wq_lo)

            def split_wo(n):
                pool.wait_ge(wo_hi, n + 2)
                lo_of(a.w_lo[:, :], a.w_nat[:, :], a.w_hi[:, :], wo_lo)

            pool.sem_inc(kv_lo, 1)
            pool.sem_inc(wq_lo, 1)
            pool.sem_inc(wo_lo, 2)
            for b in range(BATCH):
                n0 = KVH * b
                split_kv(n0)
                split_wq(n0)
                with pool.Fori(0, LOOP) as g:
                    split_kv(g + n0 + 1)
                    split_wq(g + n0 + 1)
                    split_wo(g + n0)
                split_wo(n0 + LOOP)

        @block.scalar
        def _(act):
            def split_kv(n):
                act.wait_ge(kv_loaded, 32 * n + 32)
                act.wait_ge(v_filled, 4 * n + 1)
                act.activation(a.kv_hi[:, :, :, :], a.kv_nat[:, :, :, :], ACT.Copy).then_inc(kv_hi, 1)

            def split_wq(n, first=False):
                act.wait_ge(wq_loaded, 16 * n + 16)
                act.wait_ge(out_filled, n + 1 if first else n)
                if not first:
                    act.wait_ge(q_filled, n)
                act.activation(a.w_hi[:, :], a.w_nat[:, :], ACT.Copy).then_inc(wq_hi, 1)

            def split_wo(n, last=False):
                act.wait_ge(wo_loaded, 16 * n + 16)
                if last:
                    act.wait_ge(out_filled, n + 1)
                else:
                    act.wait_ge(q_filled, n + 2)
                act.activation(a.w_hi[:, :], a.w_nat[:, :], ACT.Copy).then_inc(wo_hi, 1)

            def hi_k(n, chunks=range(CH)):
                for c in chunks:
                    act.wait_ge(k_filled, CH * n + c + 1)
                    act.activation(a.k_hi[:, c * HALF:(c + 1) * HALF], J[c % 2][:, :], ACT.Copy).then_inc(k_hi, 1)

            def hi_q(n):
                act.wait_ge(q_filled, n + 1)
                act.activation(a.q_hi[:, :], J[0][:, 0:2 * HD], ACT.Copy).then_inc(q_hi, 1)

            def raw_v(n, c):
                act.wait_ge(v_filled, CH * n + c + 2)
                act.wait_ge(vt_filled, CH * n + c + 1)
                act.activation(a.v_stage[:, c % 2, :], J[(c + 1) % 2][:, :], ACT.Copy).then_inc(v_raw, 1)

            def hi_v(n, c):
                act.wait_ge(vt_filled, CH * n + c + 3)
                act.activation(a.v_hi[:, 4 * c:4 * c + 4, :],
                               R[:, :].rearrange("p (r d) -> p r d", r=4), ACT.Copy).then_inc(vt_hi, 1)

            def v_steps(n):
                raw_v(n, 0)
                for c in range(1, CH):
                    raw_v(n, c)
                    hi_v(n, c - 1)
                hi_v(n, CH - 1)

            def softmax(n, j):
                act.wait_ge(negmax_ready, 2 * n + (j + 1))
                act.activation(a.p[:, j, :], a.p[:, j, :], ACT.Exp, bias=a.negmax[:, j:j + 1],
                               scale=SCALE, accum_out=a.psum[:, j:j + 1]).then_inc(exp_done, 1)

            def hi_p(n, groups):
                for r in groups:
                    act.wait_ge(pt_filled, GR * n + r + 1)
                    act.activation(a.pt_hi[:, r % 3, :], PTB[r % 3][:, :], ACT.Copy).then_inc(pt_hi, 1)

            def weigh_steps(n, last=False):
                hi_p(n, range(EARLY, GR))
                act.wait_ge(rb_filled, n + 1)
                act.activation(a.rb[:, :], R[:, 0:2 * SEQ], ACT.Copy).then_inc(rb_read, 1)
                if not last:
                    split_wo(n)
                act.wait_ge(ot_ready, n + 1)
                act.activation(a.ot_hi[:, :], a.ot[:, :], ACT.Copy).then_inc(ot_hi, 1)

            act.sem_inc(kv_hi, 1)
            act.sem_inc(wq_hi, 1)
            act.sem_inc(wo_hi, 1)
            act.sem_inc(v_raw, 1)
            for b in range(BATCH):
                n0 = KVH * b
                for i in range(SB):
                    u = SB * b + i
                    act.wait_ge(ctx_turned, u + 1)
                    act.activation(a.ctx_hi[:, :, i * P:(i + 1) * P],
                                   t.bank[2 + i % 4][:, :].rearrange("p (c s) -> p c s", c=KC),
                                   ACT.Copy).then_inc(ctx_hi, 1)
                split_kv(n0)
                split_wq(n0, first=True)
                hi_k(n0)
                hi_q(n0)
                v_steps(n0)
                with act.Fori(0, LOOP) as g:
                    n = g + n0
                    split_kv(n + 1)
                    split_wq(n + 1)
                    softmax(n, 0)
                    hi_k(n + 1, range(1))
                    softmax(n, 1)
                    hi_k(n + 1, range(1, CH))
                    hi_p(n, range(EARLY))
                    hi_q(n + 1)
                    weigh_steps(n)
                    v_steps(n + 1)
                softmax(n0 + LOOP, 0)
                softmax(n0 + LOOP, 1)
                split_wo(n0 + LOOP, last=True)
                hi_p(n0 + LOOP, range(EARLY))
                weigh_steps(n0 + LOOP, last=True)

        @block.vector
        def _(dve):
            c = Chain(dve, chain)
            dve.sem_inc(pt_lo, 1)

            def lo_k(n, chunks=range(CH)):
                for ch in chunks:
                    dve.wait_ge(k_hi, CH * n + ch + 1)
                    at = slice(ch * HALF, (ch + 1) * HALF)
                    dve.tensor_tensor(a.k_lo[:, at], J[ch % 2][:, :], a.k_hi[:, at].bitcast(F32),
                                      ALU.subtract).then_inc(k_lo, 1)

            def lo_q(n):
                dve.wait_ge(q_hi, n + 1)
                dve.tensor_tensor(a.q_lo[:, :], J[0][:, 0:2 * HD], a.q_hi[:, :].bitcast(F32),
                                  ALU.subtract).then_inc(q_lo, 1)

            def lo_v(n):
                for ch in range(CH):
                    dve.wait_ge(vt_hi, CH * n + ch + 1)
                    at = (slice(None), slice(4 * ch, 4 * ch + 4), slice(None))
                    dve.tensor_tensor(a.v_lo[at], R[:, :].rearrange("p (r d) -> p r d", r=4),
                                      a.v_hi[at].bitcast(F32), ALU.subtract).then_inc(vt_lo, 1)

            def scores(n):
                for j in range(2):
                    for ch in range(CH):
                        u = j * CH + ch
                        dve.wait_ge(scores_filled, 2 * CH * n + u + 1)
                        dve.memset(a.mark[:, u:u + 1], 0.0)
                        at = slice(ch * HALF, (ch + 1) * HALF)
                        dve.tensor_tensor_reduce(out=a.p[:, j, at], in0=SCB[u][:, :], in1=a.mask_bias[:, at],
                                                 scale=1.0, scalar=LOWEST, op0=ALU.add, op1=ALU.max,
                                                 accum_out=a.chunkmax[:, u:u + 1]).then_inc(scores_read, 1)
                    dve.wait_ge(scores_read, 2 * CH * n + (j + 1) * CH)
                    dve.tensor_reduce(a.rowmax[:, j:j + 1], a.chunkmax[:, j * CH:(j + 1) * CH], AX.X,
                                      ALU.max).then_inc(max_done, 1)
                    dve.wait_ge(max_done, 2 * n + (j + 1))
                    dve.tensor_scalar(a.negmax[:, j:j + 1], a.rowmax[:, j:j + 1], -SCALE, None,
                                      ALU.mult).then_inc(negmax_ready, 1)

            def inverse_sum(n, b):
                dve.wait_ge(exp_done, 2 * n + 2)
                dve.reciprocal(a.rinv[:, :], a.psum[:, :]).then_inc(rinv_done, 1)
                dve.wait_ge(rinv_done, 2 * n + 1)
                dve.tensor_scalar(a.rinv[:, :], a.rinv[:, :], a.any_valid[:, b:b + 1], None,
                                  ALU.mult).then_inc(rinv_done, 1)
                dve.wait_ge(rinv_done, 2 * n + 2)
                for j in range(2):
                    dve.tensor_scalar(a.diag[:, j * SEQ:(j + 1) * SEQ], t.ident[:, :], a.rinv[:, j:j + 1],
                                      None, ALU.mult).then_inc(diag_ready, 1)

            def lo_p(n, groups):
                for r in groups:
                    dve.wait_ge(pt_hi, GR * n + r + 1)
                    dve.tensor_tensor(a.pt_lo[:, r % 3, :], PTB[r % 3][:, :],
                                      a.pt_hi[:, r % 3, :].bitcast(F32), ALU.subtract).then_inc(pt_lo, 1)

            def pv_steps(n):
                lo_p(n, range(EARLY, GR))
                dve.wait_ge(pv_filled, n + 1)
                dve.wait_ge(rb_read, n + 1)
                dve.tensor_tensor(a.ot[:, :], PVB[:, 0:2 * SEQ], a.rb[:, :], ALU.mult).then_inc(ot_ready, 1)
                dve.wait_ge(ot_hi, n + 1)
                dve.tensor_tensor(a.ot_lo[:, :], a.ot[:, :], a.ot_hi[:, :].bitcast(F32),
                                  ALU.subtract).then_inc(ot_lo, 1)

            for b in range(BATCH):
                n0 = KVH * b
                dve.wait_ge(mask_loaded, 16 * (b + 1))
                dve.tensor_copy(a.mask_bias[:, :], a.mask_raw[:, :]).then_inc(mask_ready, 1)
                dve.wait_ge(mask_ready, b + 1)
                c.link(dve.tensor_reduce(a.any_valid[:, b:b + 1], a.mask_bias[:, :], AX.X, ALU.max))
                c.link(dve.tensor_scalar(a.mask_bias[:, :], a.mask_bias[:, :], 1.0, -MASKED,
                                         ALU.subtract, ALU.mult))
                for i in range(SB):
                    dve.wait_ge(ctx_hi, SB * b + i + 1)
                    at = (slice(None), slice(None), slice(i * P, (i + 1) * P))
                    dve.tensor_tensor(a.ctx_lo[at], t.bank[2 + i % 4][:, :].rearrange("p (c s) -> p c s", c=KC),
                                      a.ctx_hi[at].bitcast(F32), ALU.subtract).then_inc(ctx_lo, 1)
                lo_k(n0)
                lo_q(n0)
                lo_v(n0)
                with dve.Fori(0, LOOP) as g:
                    n = g + n0
                    scores(n)
                    lo_k(n + 1, range(2))
                    inverse_sum(n, b)
                    lo_k(n + 1, range(2, CH))
                    lo_p(n, range(EARLY))
                    lo_q(n + 1)
                    pv_steps(n)
                    lo_v(n + 1)
                scores(n0 + LOOP)
                inverse_sum(n0 + LOOP, b)
                lo_p(n0 + LOOP, range(EARLY))
                pv_steps(n0 + LOOP)
                dve.wait_ge(out_filled, KVH * (b + 1) + 1)
                for h in range(2):
                    at = slice(h * HALF, (h + 1) * HALF)
                    dve.tensor_tensor(t.x_res[:, b, at], t.bank[h][:, :], t.x_res[:, b, at],
                                      ALU.add).then_inc(out_read, 1)

        @block.tensor
        def _(pe):
            def project_k(n, after_scores=True):
                pe.wait_ge(kv_lo, n + 2)
                for c in range(CH):
                    if c < 2:
                        pe.wait_ge(v_raw, CH * n + 1)
                        if c == 1 and after_scores:
                            pe.wait_ge(scores_read, 2 * CH * n - 1)
                    else:
                        pe.wait_ge(k_lo, CH * n + (c - 1))
                    at = slice(c * HALF, (c + 1) * HALF)
                    split3(pe, J[c % 2][:, :], [((a.kv_hi[:, 0, k, :], a.kv_lo[:, 0, k, :]),
                                                 (a.ctx_hi[:, k, at], a.ctx_lo[:, k, at])) for k in range(KC)],
                           True, True).then_inc(k_filled, 1)

            def project_q(n, b):
                pe.wait_ge(wq_lo, n + 2)
                pe.wait_ge(k_lo, CH * n + 3)
                at = slice(b * SEQ, (b + 1) * SEQ)
                for j in range(2):
                    ws = [slice(k * 2 * HD + j * HD, k * 2 * HD + (j + 1) * HD) for k in range(KD)]
                    mm = split3(pe, J[0][:, j * SEQ:(j + 1) * SEQ],
                                [((a.w_hi[:, ws[k]], a.w_lo[:, ws[k]]),
                                  (t.xn_hi[:, k, at], t.xn_lo[:, k, at])) for k in range(KD)], True, True)
                mm.then_inc(q_filled, 1)

            def project_v(n, first=False, out_before_last_turn=None):
                def chunk(c):
                    if c < 2:
                        pe.wait_ge(q_lo, n + 1)
                    else:
                        pe.wait_ge(v_raw, CH * n + c)
                    at = slice(c * HALF, (c + 1) * HALF)
                    split3(pe, J[(c + 1) % 2][:, :], [((a.kv_hi[:, 1, k, :], a.kv_lo[:, 1, k, :]),
                                                       (a.ctx_hi[:, k, at], a.ctx_lo[:, k, at])) for k in range(KC)],
                           True, True).then_inc(v_filled, 1)

                def turn(c):
                    pe.wait_ge(v_raw, CH * n + c + 2)
                    if c > 0:
                        pe.wait_ge(vt_lo, CH * n + c)
                    elif not first:
                        pe.wait_ge(rb_read, n)
                    for r in range(4):
                        mm = pe.transpose(R[:, r * P:(r + 1) * P], a.v_stage[:, c % 2, r * P:(r + 1) * P],
                                          t.ident[:, :])
                    mm.then_inc(vt_filled, 1)
                chunk(0)
                for c in range(1, CH):
                    chunk(c)
                    turn(c - 1)
                if out_before_last_turn is None:
                    turn(CH - 1)
                else:
                    project_out(out_before_last_turn, between=lambda: turn(CH - 1))

            def scores(n):
                pe.wait_ge(k_lo, CH * n + CH)
                pe.wait_ge(q_lo, n + 1)
                for j in range(2):
                    for c in range(CH):
                        u = j * CH + c
                        if u == 0:
                            pe.wait_ge(pt_lo, GR * n + 1)
                        elif u >= 4:
                            pe.wait_ge(scores_read, 2 * CH * n + (5 if u == 7 else u - 3))
                        qs, at = slice(j * SEQ, (j + 1) * SEQ), slice(c * HALF, (c + 1) * HALF)
                        split3(pe, SCB[u][:, :], [((a.q_hi[:, qs], a.q_lo[:, qs]),
                                                     (a.k_hi[:, at], a.k_lo[:, at]))],
                               True, True).then_inc(scores_filled, 1)

            def broadcast_inverse(n):
                pe.wait_ge(diag_ready, 2 * n + 2)
                pe.wait_ge(vt_lo, CH * n + CH)
                pe.matmul(R[:, 0:2 * SEQ], t.ones[:, :], a.diag[:, :], start=True, stop=True).then_inc(rb_filled, 1)

            def turn_probs(n, groups, last=False):
                for r in groups:
                    if r == 0:
                        pe.wait_ge(exp_done, 2 * n + 2)
                    if r == 2 and not last:
                        pe.wait_ge(k_lo, CH * n + 2 * CH)
                    if r >= 3:
                        pe.wait_ge(pt_lo, GR * n + r - 1)
                    for q in range(2):
                        for j in range(2):
                            s = (2 * r + q) * P
                            mm = pe.transpose(PTB[r % 3][:, (2 * q + j) * P:(2 * q + j + 1) * P],
                                              a.p[:, j, s:s + P], t.ident[:, :])
                    mm.then_inc(pt_filled, 1)

            def weigh_values(n, last=False):
                def weigh(r):
                    pe.wait_ge(pt_lo, GR * n + r + 2)
                    pairs = [((a.v_hi[:, 2 * r + q, :], a.v_lo[:, 2 * r + q, :]),
                              (a.pt_hi[:, r % 3, q * 2 * SEQ:(q + 1) * 2 * SEQ],
                               a.pt_lo[:, r % 3, q * 2 * SEQ:(q + 1) * 2 * SEQ])) for q in range(2)]
                    return split3(pe, PVB[:, 0:2 * SEQ], pairs, r == 0, r == GR - 1)
                turn_probs(n, range(EARLY, 3), last)
                for r in range(GR):
                    if r == 5:
                        broadcast_inverse(n)
                    mm = weigh(r)
                    if r + 3 < GR:
                        turn_probs(n, (r + 3,))
                mm.then_inc(pv_filled, 1)

            def project_out(n, last=False, between=None):
                pe.wait_ge(wo_lo, n + 3)
                pe.wait_ge(ot_lo, n + 1)
                for j in range(2):
                    at = slice(j * SEQ, (j + 1) * SEQ)
                    for h in range(2):
                        w = slice(j * DM + h * HALF, j * DM + (h + 1) * HALF)
                        mm = split3(pe, t.bank[h][:, :], [((a.ot_hi[:, at], a.ot_lo[:, at]),
                                                           (a.w_hi[:, w], a.w_lo[:, w]))],
                                    False, last and j == 1)
                    if j == 0 and between is not None:
                        between()
                mm.then_inc(out_filled, 1)

            pe.sem_inc(out_filled, 1)
            pe.sem_inc(v_filled, 1)
            pe.sem_inc(vt_filled, 2)
            for b in range(BATCH):
                n0 = KVH * b
                if b:
                    pe.wait_ge(out_read, 2 * b)
                for h in range(2):
                    pe.matmul(t.bank[h][:, :], t.zeros[:, :], t.xn_hi[:, 0:2, :], start=True, stop=False)
                for i in range(SB):
                    u = SB * b + i
                    pe.wait_ge(ctx_loaded[i // 2 % 2], 16 * (SB // 4 * b + i // 4 + 1))
                    if i >= 4:
                        pe.wait_ge(ctx_lo, u - 3)
                    elif b:
                        pe.wait_ge(ot_lo, n0)
                        pe.wait_ge(pt_lo, GR * n0 + 1)
                    half = a.w_nat[:, (i // 2 % 2) * DM + (i % 2) * DC:(i // 2 % 2) * DM + (i % 2 + 1) * DC]
                    for c in range(KC):
                        mm = pe.transpose(t.bank[2 + i % 4][:, c * P:(c + 1) * P], half[:, c * P:(c + 1) * P],
                                          t.ident[:, :])
                    mm.then_inc(ctx_turned, 1)
                pe.wait_ge(ctx_lo, SB * (b + 1))
                project_k(n0, after_scores=False)
                project_q(n0, b)
                project_v(n0, first=b == 0)
                with pe.Fori(0, LOOP) as g:
                    n = g + n0
                    scores(n)
                    project_k(n + 1)
                    turn_probs(n, range(EARLY))
                    project_q(n + 1, b)
                    weigh_values(n)
                    project_v(n + 1, out_before_last_turn=n)
                scores(n0 + LOOP)
                turn_probs(n0 + LOOP, range(EARLY))
                weigh_values(n0 + LOOP, last=True)
                project_out(n0 + LOOP, True)


def project(pe, t, f, out, w, s):
    ks = [slice(k * P, (k + 1) * P) for k in range(KD)]
    return split3(pe, out, [((f.w_hi[:, s, w, ks[k]], f.w_lo[:, s, w, ks[k]]),
                             (t.xn_hi[:, k, :], t.xn_lo[:, k, :])) for k in range(KD)], True, True)


def accumulate(pe, t, f, hi, lo, s, last):
    for b in range(BATCH):
        rows = slice(b * SEQ, (b + 1) * SEQ)
        for h in range(2):
            at = slice(h * HALF, (h + 1) * HALF)
            mm = split3(pe, t.bank[2 * b + h][:, :],
                        [((hi[:, rows], lo[:, rows]), (f.w_hi[:, s, 2, at], f.w_lo[:, s, 2, at]))], False, last)
    return mm


def zero_sums(pe, t):
    for n in range(4):
        pe.matmul(t.bank[n][:, :], t.zeros[:, :], t.xn_hi[:, 0:2, :], start=True, stop=False)


def load_head_tiles(sp, m, in_proj):
    r0 = 2 * INTER
    for w, (r, n) in enumerate(((r0, P), (r0 + P, P), (r0 + 2 * P, SSM_H))):
        sp.dma_start(m.head_rows[0:n, w, :], in_proj[r:r + n, :]).then_inc(m.head_tiles[w], 16)


def mixer_load_rows(sp, m, in_proj, i, w, s):
    for a in range(4):
        src = in_proj[bass.ds(i * P + (0 if w else INTER), P), a * 2 * P:(a + 1) * 2 * P]
        sp.dma_start(m.nat[a * Q:(a + 1) * Q, s, w, :].rearrange("p (b h) -> p b h", b=4),
                     src.rearrange("(b o) h -> o b h", o=Q)).then_inc(m.rows_loaded[w][s], 16)


def mixer_head_block(nc, sem, in_proj, conv_w, conv_b, A_log, dt_bias, D, norm_w, t, m):
    nat, wh, wl = m.head_nat, m.w_hi, m.w_lo
    tiles, consts = m.head_tiles, sem("head_consts")
    arranged = sem("head_arranged")
    turned, hi_w, lo_w = sem("head_turned"), sem("head_hi"), sem("head_lo")
    projected, copied, conved, tanhed, bc_ready = (sem(f"head_{x}") for x in ("proj", "copied", "conved", "tanhed", "bc"))
    g_filled, zdt_ready, exp_dt, w_ready, ln_dt, a_ready, padded, m_zeroed = (
        sem(f"head_{x}") for x in ("g", "zdt", "expdt", "w", "lndt", "a", "padded", "mzero"))
    chain, dtT_ready = sem("head_chain"), sem("head_dtT")
    BANKS = [0, 1, 2, 3, 4]
    with nc.Block() as block:
        @block.sync
        def _(sp):
            sp.dma_start(m.convw[:, :, :], conv_w.rearrange("(i p) o k -> p i (o k)", p=P)).then_inc(consts, 16)
            sp.dma_start(m.convb[:, :], conv_b.rearrange("(i p) -> p i", p=P), allow_slow_non_contiguous=True).then_inc(consts, 16)
            sp.dma_start(m.normw[:, :], norm_w.rearrange("(i p) -> p i", p=P), allow_slow_non_contiguous=True).then_inc(consts, 16)
            for j in range(2):
                src = bc(D.rearrange("(a i two) -> a two i", a=1, two=2)[:, j, :], 0, HP)
                sp.dma_start(m.dcol[j * HP:(j + 1) * HP, :], src, allow_slow_non_contiguous=True).then_inc(consts, 16)
            sp.dma_start(m.dtb[:, :], bc(dt_bias.rearrange("(a h) -> a h", a=1), 0, P)).then_inc(consts, 16)
            sp.dma_start(m.alog[:, :], bc(A_log.rearrange("(a h) -> a h", a=1), 0, P)).then_inc(consts, 16)
            for i in range(2):
                for w in range(2):
                    mixer_load_rows(sp, m, in_proj, i, w, i)

        @block.gpsimd
        def _(pool):
            pool.memset(m.xpad[:, :, :], 0.0).then_inc(padded, 1)
            pool.memset(m.xdt[:, :, :, :], 0.0).then_inc(m_zeroed, 1)
            pool.memset(m.sumsq[:, :], 0.0).then_inc(m_zeroed, 1)
            pool.wait_ge(m_zeroed, 2)

        @block.scalar
        def _(act):
            for w, n in enumerate((P, P, SSM_H)):
                act.wait_ge(tiles[w], 16)
                act.activation(blocks_by_quad(nat[0:n, w, :]), by_quad(m.head_rows[0:n, w, :]), ACT.Copy).then_inc(arranged, 1)
            for q in range(5):
                act.wait_ge(turned, q + 1)
                w, half = q // 2, q % 2
                act.activation(wh[:, 0, w, half * HALF:(half + 1) * HALF], t.bank[q][:, :],
                               ACT.Copy).then_inc(hi_w, 1)
            act.wait_ge(padded, 1)
            for n in range(2):
                act.wait_ge(projected, n + 1)
                if n:
                    act.wait_ge(conved, 1)
                act.activation(m.xpad[:, :, 3:3 + SEQ], t.bank[5 + n][:, 0:TOK].rearrange("p (b s) -> p b s", b=BATCH),
                               ACT.Copy).then_inc(copied, 1)
                act.wait_ge(conved, n + 1)
                if n:
                    act.wait_ge(bc_ready, 1)
                act.activation(m.th[:, :], m.z[:, :], ACT.Tanh, scale=0.5).then_inc(tanhed, 1)
            act.wait_ge(zdt_ready, 1)
            act.activation(m.e_dt[:, :, :], m.nabs[:, :, :], ACT.Exp).then_inc(exp_dt, 1)
            act.activation(m.ea[:, :], m.alog[:, :], ACT.Exp).then_inc(exp_dt, 1)
            act.wait_ge(w_ready, 1)
            act.activation(m.ln_dt[:, :, :], m.w_dt[:, :, :], ACT.Ln).then_inc(ln_dt, 1)
            act.wait_ge(a_ready, 1)
            act.activation(m.a_hi[:, :, :], m.a[:, :, :], ACT.Copy).then_inc(ln_dt, 1)

        @block.vector
        def _(dve):
            c = Chain(dve, chain)
            for q in range(5):
                dve.wait_ge(hi_w, q + 1)
                w, half = q // 2, q % 2
                at = (slice(None), 0, w, slice(half * HALF, (half + 1) * HALF))
                dve.tensor_tensor(wl[at], t.bank[q][:, :], wh[at].bitcast(F32), ALU.subtract).then_inc(lo_w, 1)
            dve.wait_ge(projected, 3)
            dve.tensor_copy(m.dtT[:, :], t.bank[7][0:SSM_H, 0:TOK]).then_inc(dtT_ready, 1)
            dve.wait_ge(consts, 16 * 7)
            for n in range(2):
                dve.wait_ge(copied, n + 1)
                if n:
                    dve.wait_ge(bc_ready, 1)
                conv(dve, chain, c.n, m, XB + n, conved)
                c.n += CONV_LINKS
                dve.wait_ge(tanhed, n + 1)
                dve.scalar_tensor_tensor(m.bc[:, n, :], m.th[:, :], 1.0, m.z[:, :], ALU.add,
                                         ALU.mult).then_inc(bc_ready, 1)
            dve.wait_ge(projected, 4)
            c.link(dve.tensor_tensor(m.zdt[:, :, :], t.bank[1][:, 0:2 * SSM_H].rearrange("p (b h) -> p b h", b=BATCH),
                                     bc(m.dtb[:, :].rearrange("p (a h) -> p a h", a=1), 1, BATCH), ALU.add))
            dve.scalar_tensor_tensor(m.nabs[:, :, :], m.zdt[:, :, :], -1.0, m.zdt[:, :, :], ALU.mult, ALU.min).then_inc(zdt_ready, 1)
            dve.wait_ge(exp_dt, 1)
            dve.tensor_scalar(m.w_dt[:, :, :], m.e_dt[:, :, :], 1.0, None, ALU.add).then_inc(w_ready, 1)
            dve.wait_ge(w_ready, 1)
            c.link(dve.tensor_scalar(m.d_dt[:, :, :], m.w_dt[:, :, :], 1.0, None, ALU.subtract))
            c.link(dve.tensor_scalar(m.is0[:, :, :], m.d_dt[:, :, :], 0.0, None, ALU.is_equal))
            c.link(dve.tensor_tensor(m.d_dt[:, :, :], m.d_dt[:, :, :], m.is0[:, :, :], ALU.add))
            c.link(dve.reciprocal(m.d_dt[:, :, :], m.d_dt[:, :, :]))
            c.link(dve.tensor_tensor(m.d_dt[:, :, :], m.d_dt[:, :, :], m.e_dt[:, :, :], ALU.mult))
            c.link(dve.tensor_tensor(m.is0[:, :, :], m.is0[:, :, :], m.e_dt[:, :, :], ALU.mult))
            dve.wait_ge(ln_dt, 1)
            c.link(dve.tensor_tensor(m.d_dt[:, :, :], m.d_dt[:, :, :], m.ln_dt[:, :, :], ALU.mult))
            c.link(dve.tensor_tensor(m.d_dt[:, :, :], m.d_dt[:, :, :], m.is0[:, :, :], ALU.add))
            c.link(dve.scalar_tensor_tensor(m.zdt[:, :, :], m.zdt[:, :, :], 0.0, m.d_dt[:, :, :], ALU.max, ALU.add))
            dve.tensor_scalar(m.dth[:, :, :], m.zdt[:, :, :], 0.5, None, ALU.mult)
            dve.wait_ge(exp_dt, 2)
            dve.scalar_tensor_tensor(m.a[:, :, :], m.zdt[:, :, :], -1.0,
                                     bc(m.ea[:, :].rearrange("p (a h) -> p a h", a=1), 1, BATCH),
                                     ALU.mult, ALU.mult).then_inc(a_ready, 1)
            dve.wait_ge(ln_dt, 2)
            dve.tensor_tensor(m.a_lo[:, :, :], m.a[:, :, :], m.a_hi[:, :, :].bitcast(F32), ALU.subtract)
            dve.tensor_scalar(m.dcol[:, :], m.dcol[:, :], 0.5, None, ALU.mult)
            c.link(dve.tensor_scalar(m.normw[:, :], m.normw[:, :], 0.5, None, ALU.mult))
            dve.wait_ge(g_filled, 1)
            c.link(dve.scalar_tensor_tensor(m.gm[:, :, :], t.bank[0][:, 0:TOK].rearrange("p (b s) -> p b s", b=BATCH),
                                            0.25, bc(t.tri[:, :].rearrange("p (a l) -> p a l", a=1), 1, BATCH),
                                            ALU.mult, ALU.mult))

        @block.tensor
        def _(pe):
            for w in range(3):
                n = SSM_H if w == 2 else P
                pe.wait_ge(arranged, w + 1)
                for half in range(1 if w == 2 else 2):
                    blocks = KD if w == 2 else 4
                    for r in range(blocks):
                        k = 4 * half + r
                        mm = pe.transpose(t.bank[2 * w + half][:, r * n:(r + 1) * n],
                                          nat[0:n, w, k * P:(k + 1) * P], t.ident[0:n, 0:n])
                    mm.then_inc(turned, 1)
            for w in range(2):
                pe.wait_ge(lo_w, 2 * w + 2)
                ks = [slice(k * P, (k + 1) * P) for k in range(KD)]
                split3(pe, t.bank[5 + w][:, 0:TOK], [((wh[:, 0, w, ks[k]], wl[:, 0, w, ks[k]]),
                                                       (t.xn_hi[:, k, :], t.xn_lo[:, k, :])) for k in range(KD)],
                       True, True).then_inc(projected, 1)
            pe.wait_ge(lo_w, 5)
            hs = [slice(k * SSM_H, (k + 1) * SSM_H) for k in range(KD)]
            split3(pe, t.bank[7][0:SSM_H, 0:TOK],
                   [((wh[:, 0, 2, hs[k]], wl[:, 0, 2, hs[k]]), (t.xn_hi[:, k, :], t.xn_lo[:, k, :]))
                    for k in range(KD)], True, True).then_inc(projected, 1)
            pe.wait_ge(dtT_ready, 1)
            for b in range(BATCH):
                mm = pe.transpose(t.bank[1][:, b * SSM_H:(b + 1) * SSM_H], m.dtT[:, b * SEQ:(b + 1) * SEQ],
                                  t.ident[0:SSM_H, 0:SSM_H])
            mm.then_inc(projected, 1)
            pe.wait_ge(bc_ready, 2)
            for b in range(BATCH):
                at = slice(b * SEQ, (b + 1) * SEQ)
                mm = pe.matmul(t.bank[0][:, at], m.bc[:, 0, at], m.bc[:, 1, at], start=True, stop=True)
            mm.then_inc(g_filled, 1)


CONV_LINKS = 3 * BATCH


def conv(dve, chain, base, m, i, done):
    def col(k):
        return m.convw[:, bass.ds(i, 1), k:k + 1].rearrange("p a k -> p (a k)")
    for k in range(4):
        for b in range(BATCH):
            z, x = m.z[:, b * SEQ:(b + 1) * SEQ], m.xpad[:, b, k:k + SEQ]
            if k:
                dve.wait_ge(chain, base + (BATCH * (k - 1) + b + 1))
                ins = dve.scalar_tensor_tensor(z, x, col(k), z, ALU.mult, ALU.add)
            else:
                ins = dve.tensor_scalar(z, x, col(0), m.convb[:, bass.ds(i, 1)], ALU.mult, ALU.add)
            if k < 3:
                ins.then_inc(chain, 1)
    ins.then_inc(done, 1)


def mixer_block(nc, sem, in_proj, out_proj, t, m):
    SBK, YBK, XBK, GBK = t.bank[4], t.bank[5], t.bank[6], t.bank[7]
    rows_loaded = m.rows_loaded
    cols_loaded = [sem(f"mix_cols{s}") for s in range(2)]
    turned, hi_rows, lo_x, lo_gate = (sem("mix_" + x) for x in ("turned", "hi", "lox", "logate"))
    cols_turned, hi_cols, lo_cols = (sem("mix_" + x) for x in ("colsturned", "hicols", "locols"))
    x_filled, x_copied, conved, tanh_x, xs_ready = (sem("mix_" + x) for x in ("x", "xcopied", "conved", "tanhx", "xs"))
    xt_filled, xdt_ready, atri_ready, s_filled, exp_done, m_ready = (
        sem("mix_" + x) for x in ("xt", "xdt", "atri", "s", "exp", "m"))
    gate_filled, tanh_g, y_filled, y_ready, ynw_ready, sq_done = (
        sem("mix_" + x) for x in ("gate", "tanhg", "y", "yready", "ynw", "sq"))
    yn_hi, yn_lo, mixed, sum_filled, var_ready, std_ready, rstd_ready = (
        sem("mix_" + x) for x in ("ynhi", "ynlo", "mixed", "sum", "var", "std", "rstd"))
    dchain, pchain = sem("mix_dchain"), sem("mix_pchain")
    STEPS = XB
    W = 2
    CREDIT = 4

    with nc.Block() as block:
        @block.sync
        def _(sp):
            def load_rows(i, w, s):
                mixer_load_rows(sp, m, in_proj, i, w, s)

            def load_cols(i, s):
                src = out_proj.rearrange("(h p) i -> p h i", p=P)[:, :, bass.ds(i * P, P)]
                sp.dma_start(m.nat_c[:, s, :].rearrange("p (h i) -> p h i", h=KD), src).then_inc(cols_loaded[s], 16)

            def step(i, u):
                sp.wait_ge(turned, 2 * i + 7)
                load_rows(i + 2, 1, u)
                load_cols(i, u)
                load_rows(i + 3, 0, 1 - u)

            sp.wait_ge(turned, CREDIT + 1)
            load_rows(2, 0, 0)
            with sp.Fori(0, STEPS // W - 2) as r:
                for u in range(W):
                    step(r * W + u, u)
            step(STEPS - 4, 0)
            for i in range(STEPS - 3, STEPS):
                sp.wait_ge(turned, min(2 * i + 7, 2 * STEPS + CREDIT))
                if i + 2 < STEPS:
                    load_rows(i + 2, 1, i % W)
                load_cols(i, i % W)

        @block.gpsimd
        def _(pool):
            def scan_weights(i):
                tri = bc(bc(t.tri[:, :].rearrange("p (x y l) -> p x y l", x=1, y=1), 1, BATCH), 2, 2)
                for dst, src in ((m.atri_hi, m.a_hi[:, :, :].bitcast(F32)), (m.atri_lo, m.a_lo[:, :, :])):
                    col = bc(src[:, :, bass.ds(i * 2, 2)].rearrange("p b (j l) -> p b j l", l=1), 3, SEQ)
                    ins = pool.tensor_tensor(dst[:, :].rearrange("p (b j l) -> p b j l", b=BATCH, j=2), tri, col, ALU.mult)
                ins.then_inc(atri_ready, 1)

            def split_gate(i, s):
                pool.wait_ge(hi_rows, 2 * i + 2)
                pool.tensor_tensor(m.w_lo[:, s, 1, :], m.wt[:, 1, :], m.w_hi[:, s, 1, :].bitcast(F32),
                                   ALU.subtract).then_inc(lo_gate, 1)

            def step(i, u, last=False):
                pool.wait_ge(exp_done, i + 1)
                ev = m.e[:, :].rearrange("p (b j l) -> p b j l", b=BATCH, j=2)
                gm = bc(m.gm[:, :, :].rearrange("p b (x l) -> p b x l", x=1), 2, 2)
                pool.tensor_tensor(m.mt[:, :].rearrange("p (b j l) -> p b j l", b=BATCH, j=2), ev, gm,
                                   ALU.mult).then_inc(m_ready, 1)
                if not last:
                    scan_weights(i + 1)
                    split_gate(i + 1, 1 - u)
                pool.wait_ge(y_ready, i + 1)
                c = Chain(pool, pchain, 2 * i)
                c.link(pool.tensor_tensor(m.yg[:, :], m.y[:, :], m.sg[:, :], ALU.mult))
                c.link(pool.tensor_tensor(m.yg[:, :], m.yg[:, :], m.yg[:, :], ALU.mult))
                pool.tensor_tensor(m.sumsq[:, :], m.sumsq[:, :], m.yg[:, :], ALU.add).then_inc(sq_done, 1)

            pool.sem_inc(sq_done, 1)
            pool.sem_inc(lo_gate, 1)
            scan_weights(0)
            split_gate(0, 0)
            with pool.Fori(0, STEPS // W - 1) as r:
                for u in range(W):
                    step(r * W + u, u)
            for i in range(STEPS - W, STEPS):
                step(i, i % W, i == STEPS - 1)

        @block.scalar
        def _(act):
            def hi(i, w, s):
                act.wait_ge(turned, 2 * i + (w + 1 + CREDIT))
                act.activation(m.w_hi[:, s, w, :], m.wt[:, w, :], ACT.Copy).then_inc(hi_rows, 1)

            def hi_half_cols(i, s, half):
                act.wait_ge(cols_turned, 2 * i + (half + 1 + CREDIT))
                act.activation(m.w_hi[:, s, 2, half * HALF:(half + 1) * HALF], SBK[:, :], ACT.Copy).then_inc(hi_cols, 1)

            def copy_x(i):
                act.wait_ge(x_filled, i + 1)
                act.wait_ge(conved, i + 1)
                act.activation(m.xpad[:, :, 3:3 + SEQ], XBK[:, 0:TOK].rearrange("p (b s) -> p b s", b=BATCH),
                               ACT.Copy).then_inc(x_copied, 1)

            def tanh_of_x(i):
                act.wait_ge(conved, i + 2)
                act.activation(m.th[:, :], m.z[:, :], ACT.Tanh, scale=0.5).then_inc(tanh_x, 1)

            def step(i, u, last=False, rows=True):
                act.wait_ge(s_filled, i + 1)
                act.activation(m.e[:, :], SBK[:, :], ACT.Exp).then_inc(exp_done, 1)
                act.wait_ge(gate_filled, i + 1)
                act.activation(m.thg[:, :], GBK[:, 0:TOK], ACT.Tanh, scale=0.5).then_inc(tanh_g, 1)
                if not last:
                    hi(i + 1, 1, 1 - u)
                hi_half_cols(i, u, 0)
                if rows:
                    hi(i + 2, 0, u)
                if not last:
                    copy_x(i + 1)
                hi_half_cols(i, u, 1)
                if not last:
                    tanh_of_x(i + 1)
                act.wait_ge(ynw_ready, i + 1)
                act.activation(m.yn_hi[:, u, :], m.ynw[:, :], ACT.Copy).then_inc(yn_hi, 1)

            hi(0, 0, 0)
            hi(0, 1, 0)
            copy_x(0)
            hi(1, 0, 1)
            tanh_of_x(0)
            with act.Fori(0, STEPS // W - 1) as r:
                for u in range(W):
                    step(r * W + u, u)
            step(STEPS - 2, 0, rows=False)
            step(STEPS - 1, 1, last=True, rows=False)
            act.wait_ge(var_ready, 1)
            act.activation(m.std[:, :], m.var[:, :], ACT.Sqrt, bias=t.eps[:, 0:1]).then_inc(std_ready, 1)

        @block.vector
        def _(dve):
            def turn_rows(i, w, s, landed):
                dve.wait_ge(lo_gate if w else lo_x, i + 1)
                dve.wait_ge(rows_loaded[w][s], landed)
                dve.transpose(m.wt[:, w, :].rearrange("p (k b o) -> p b k o", k=KD, b=4),
                              m.nat[:, s, w, :].rearrange("p (b k h) -> p b k h", b=4, k=KD)).then_inc(turned, 1)

            def split_x_rows(i, s):
                dve.wait_ge(hi_rows, 2 * i + 1)
                dve.tensor_tensor(m.w_lo[:, s, 0, :], m.wt[:, 0, :], m.w_hi[:, s, 0, :].bitcast(F32),
                                  ALU.subtract).then_inc(lo_x, 1)

            def split_half_cols(i, s, half):
                at = (slice(None), s, 2, slice(half * HALF, (half + 1) * HALF))
                dve.wait_ge(hi_cols, 2 * i + (half + 1))
                dve.tensor_tensor(m.w_lo[at], SBK[:, :], m.w_hi[at].bitcast(F32), ALU.subtract).then_inc(lo_cols, 1)

            def make_x(i, s):
                dve.wait_ge(tanh_x, i + 1)
                dve.scalar_tensor_tensor(m.xs[:, s, :], m.th[:, :], 1.0, m.z[:, :], ALU.add,
                                         ALU.mult).then_inc(xs_ready, 1)

            def convolve(i):
                dve.wait_ge(x_copied, i + 1)
                conv(dve, dchain, CONV_LINKS * i, m, i, conved)

            def step(r, u, last=False, rows=True):
                i = r * W + u
                dve.wait_ge(xt_filled, i + 1)
                for j in range(2):
                    at = slice(j * HP, (j + 1) * HP)
                    ins = dve.tensor_tensor(
                        m.xdt[:, :, j, at],
                        YBK[:, 0:TOK].rearrange("p (b c) -> p b c", b=BATCH)[:, :, at],
                        bc(m.dth[:, :, bass.ds(i * 2 + j, 1)], 2, HP), ALU.mult)
                ins.then_inc(xdt_ready, 1)
                if not last:
                    turn_rows(i + 1, 1, 1 - u, 64 * r + 64 * (1 + u))
                if rows:
                    turn_rows(i + 2, 0, u, 64 * r + 128)
                dve.wait_ge(tanh_g, i + 1)
                dve.wait_ge(sq_done, i + 1)
                dve.scalar_tensor_tensor(m.sg[:, :], m.thg[:, :], 1.0, GBK[:, 0:TOK], ALU.add, ALU.mult)
                split_half_cols(i, u, 0)
                if not last:
                    convolve(i + 1)
                dve.wait_ge(y_filled, i + 1)
                dve.scalar_tensor_tensor(m.y[:, :], m.xs[:, u, :], m.dcol[:, bass.ds(i, 1)], YBK[:, 0:TOK], ALU.mult,
                                         ALU.add).then_inc(y_ready, 1)
                if not last:
                    make_x(i + 1, 1 - u)
                split_half_cols(i, u, 1)
                dve.wait_ge(y_ready, i + 1)
                dve.scalar_tensor_tensor(m.ynw[:, :], m.y[:, :], m.normw[:, bass.ds(i, 1)], m.sg[:, :], ALU.mult,
                                         ALU.mult).then_inc(ynw_ready, 1)
                if rows:
                    split_x_rows(i + 2, u)
                dve.wait_ge(yn_hi, i + 1)
                dve.tensor_tensor(m.yn_lo[:, u, :], m.ynw[:, :], m.yn_hi[:, u, :].bitcast(F32),
                                  ALU.subtract).then_inc(yn_lo, 1)

            dve.sem_inc(turned, CREDIT)
            dve.sem_inc(lo_x, 1)
            dve.sem_inc(lo_cols, 2)
            dve.sem_inc(conved, 1)
            turn_rows(0, 0, 0, 64)
            turn_rows(0, 1, 0, 64)
            split_x_rows(0, 0)
            turn_rows(1, 0, 1, 64)
            split_x_rows(1, 1)
            convolve(0)
            make_x(0, 0)
            with dve.Fori(0, STEPS // W - 1) as r:
                for u in range(W):
                    step(r, u)
            step(STEPS // W - 1, 0, rows=False)
            step(STEPS // W - 1, 1, last=True, rows=False)
            dve.wait_ge(sum_filled, 1)
            dve.tensor_scalar(m.var[:, :], XBK[:, 0:BATCH], 0.25 / INTER, None, ALU.mult).then_inc(var_ready, 1)
            dve.wait_ge(std_ready, 1)
            dve.reciprocal(m.rstd[:, :], m.std[:, :]).then_inc(rstd_ready, 1)
            dve.wait_ge(rstd_ready, 1)
            dve.wait_ge(mixed, 1)
            for b in range(BATCH):
                for h in range(2):
                    at = slice(h * HALF, (h + 1) * HALF)
                    dve.scalar_tensor_tensor(t.x_res[:, b, at], t.bank[2 * b + h][:, :], m.rstd[:, b:b + 1],
                                             t.x_res[:, b, at], ALU.mult, ALU.add)

        @block.tensor
        def _(pe):
            def project_x(i, s):
                pe.wait_ge(lo_x, i + 2)
                project(pe, t, m, XBK[:, 0:TOK], 0, s).then_inc(x_filled, 1)

            def turn_half_cols(i, u, half):
                pe.wait_ge(lo_cols, 2 * i + (half + 2))
                for r in range(4):
                    mm = pe.transpose(SBK[:, r * P:(r + 1) * P],
                                      m.nat_c[:, u, (4 * half + r) * P:(4 * half + r + 1) * P], t.ident[:, :])
                mm.then_inc(cols_turned, 1)

            def sum_products(i, s, last=False):
                pe.wait_ge(lo_cols, 2 * i + 4)
                pe.wait_ge(yn_lo, i + 1)
                mm = accumulate(pe, t, m, m.yn_hi[:, s, :], m.yn_lo[:, s, :], s, last)
                if last:
                    mm.then_inc(mixed, 1)

            def step(r, u, first=False, last=False):
                i = r * W + u
                pe.wait_ge(xs_ready, i + 1)
                for b in range(BATCH):
                    mm = pe.transpose(YBK[:, b * P:(b + 1) * P], m.xs[:, u, b * SEQ:(b + 1) * SEQ], t.ident[:, :])
                mm.then_inc(xt_filled, 1)
                pe.wait_ge(atri_ready, i + 1)
                pe.wait_ge(lo_cols, 2 * i + 2)
                pe.matmul(SBK[:, :], t.after[:, :], m.atri_hi[:, :], start=True, stop=False)
                pe.matmul(SBK[:, :], t.after[:, :], m.atri_lo[:, :], start=False, stop=True).then_inc(s_filled, 1)
                pe.wait_ge(lo_gate, i + 2)
                project(pe, t, m, GBK[:, 0:TOK], 1, u).then_inc(gate_filled, 1)
                pe.wait_ge(cols_loaded[u], 16 * r + 16)
                pe.wait_ge(exp_done, i + 1)
                turn_half_cols(i, u, 0)
                if not last:
                    project_x(i + 1, 1 - u)
                turn_half_cols(i, u, 1)
                pe.wait_ge(xdt_ready, i + 1)
                pe.wait_ge(m_ready, i + 1)
                for b in range(BATCH):
                    for j in range(2):
                        at = (2 * b + j) * SEQ
                        mm = pe.matmul(YBK[:, b * SEQ:(b + 1) * SEQ], m.xdt[:, b, j, :], m.mt[:, at:at + SEQ],
                                       start=j == 0, stop=j == 1)
                mm.then_inc(y_filled, 1)
                if not first:
                    sum_products(i - 1, 1 - u)

            pe.sem_inc(cols_turned, CREDIT)
            zero_sums(pe, t)
            project_x(0, 0)
            step(0, 0, first=True)
            step(0, 1)
            with pe.Fori(1, STEPS // W - 1) as r:
                for u in range(W):
                    step(r, u)
            step(STEPS // W - 1, 0)
            step(STEPS // W - 1, 1, last=True)
            sum_products(STEPS - 1, 1, last=True)
            pe.wait_ge(sq_done, STEPS + 1)
            for b in range(BATCH):
                mm = pe.matmul(XBK[:, b:b + 1], m.sumsq[:, b * SEQ:(b + 1) * SEQ], t.ones[:, 0:1],
                               start=True, stop=True)
            mm.then_inc(sum_filled, 1)


def load_gate_w(sp, f, gate_w):
    for a in range(4):
        sp.dma_start(blocks_by_quad(f.gw[:, :])[:, a], by_quad(gate_w)[:, a]).then_inc(f.gw_loaded, 16)


def router_block(nc, sem, w1, w2, t, r, f):
    loaded = f.gw_loaded
    turned, gw_hi, gw_lo = (sem("rt_" + x) for x in ("turned", "hi", "lo"))
    logits_filled, max_ready, exp_done, comb_ready, comb_turned, combT_ready, spread, spread_read = (
        sem("rt_" + x) for x in ("logits", "max", "exp", "comb", "cturned", "cT", "spread", "sread"))
    logitT_ready = sem("rt_logitT")
    sel_steps, ltri_ready, chain = sem("rt_sel"), sem("rt_ltri"), sem("rt_chain")
    TILES = PAIRS
    with nc.Block() as block:
        @block.sync
        def _(sp):
            ffn_load_rows(sp, f, 0, expert_rows(w1, 0, 0))
            ffn_load_cols(sp, f, 0, expert_cols(w2, 0))
            ffn_load_rows(sp, f, 1, expert_rows(w1, 0, 1))

        @block.gpsimd
        def _(pool):
            pool.memset(r.sel[:, :, :], 0.0).then_inc(sel_steps, 1)
            pool.memset(r.ltri[:, :, :], 1.0).then_inc(sel_steps, 1)
            pool.memset(r.comb[:, TILES:TILES + 1, :], 1.0).then_inc(sel_steps, 1)
            pool.wait_ge(sel_steps, 3)
            pool.affine_select(out=r.ltri[:, :, :], in_=r.ltri[:, :, :], compare_op=ALU.is_gt, fill=0.0, base=0,
                               pattern=[[1, EXPERTS], [-1, EXPERTS]], channel_multiplier=0).then_inc(ltri_ready, 1)
            for half in range(2):
                view = r.sel[:, :, half * HP:(half + 1) * HP]
                pool.affine_select(out=view, in_=view, compare_op=ALU.not_equal, fill=1.0, base=-half,
                                   pattern=[[-2, PAIRS], [0, HP]], channel_multiplier=1).then_inc(sel_steps, 1)

        @block.scalar
        def _(act):
            act.wait_ge(turned, 1)
            act.activation(r.gw_hi[:, :], t.bank[0][:, 0:KD * EXPERTS], ACT.Copy).then_inc(gw_hi, 1)
            for b in range(BATCH):
                act.wait_ge(max_ready, 1)
                act.activation(r.prob[:, b, :], r.logit[:, b, :], ACT.Exp, bias=r.negmax[:, b:b + 1],
                               accum_out=r.psum[:, b:b + 1]).then_inc(exp_done, 1)
            act.wait_ge(comb_turned, 1)
            act.activation(r.combT[:, :], t.bank[7][0:EXPERTS, 0:TOK], ACT.Copy).then_inc(combT_ready, 1)
            for n in range(TILES // 2):
                act.wait_ge(spread, n + 1)
                act.activation(r.comb[:, 2 * n:2 * n + 2, :], t.bank[n % 4 + 3][:, :].rearrange("p (a s) -> p a s", a=2),
                               ACT.Copy).then_inc(spread_read, 1)

        @block.vector
        def _(dve):
            c = Chain(dve, chain)
            dve.wait_ge(gw_hi, 1)
            dve.tensor_tensor(r.gw_lo[:, :], t.bank[0][:, 0:KD * EXPERTS], r.gw_hi[:, :].bitcast(F32),
                              ALU.subtract).then_inc(gw_lo, 1)
            dve.wait_ge(logits_filled, 1)
            dve.tensor_copy(r.logitT[:, :], t.bank[1][0:EXPERTS, 0:TOK]).then_inc(logitT_ready, 1)
            dve.wait_ge(logits_filled, 2)
            c.link(dve.tensor_copy(r.logit[:, :, :], t.bank[2][:, 0:BATCH * EXPERTS].rearrange("p (b e) -> p b e", b=BATCH)))
            c.link(dve.tensor_reduce(r.negmax[:, :], r.logit[:, :, :], AX.X, ALU.max))
            dve.tensor_scalar(r.negmax[:, :], r.negmax[:, :], -1.0, None, ALU.mult).then_inc(max_ready, 1)
            dve.wait_ge(exp_done, 2)
            c.link(dve.reciprocal(r.psum[:, :], r.psum[:, :]))
            dve.wait_ge(ltri_ready, 1)
            for b in range(BATCH):
                c.link(dve.tensor_scalar(r.prob[:, b, :], r.prob[:, b, :], r.psum[:, b:b + 1], None, ALU.mult))
                pj = bc(r.prob[:, b, :].rearrange("p (a j) -> p a j", a=1), 1, EXPERTS)
                pe_ = bc(r.prob[:, b, :].rearrange("p (e a) -> p e a", a=1), 2, EXPERTS)
                c.link(dve.tensor_tensor(r.eq[:, :, :], pj, pe_, ALU.is_equal))
                c.link(dve.tensor_tensor(r.eq[:, :, :], r.eq[:, :, :], r.ltri[:, :, :], ALU.mult))
                c.link(dve.tensor_tensor(r.gt[:, :, :], pj, pe_, ALU.is_gt))
                c.link(dve.tensor_tensor(r.gt[:, :, :], r.gt[:, :, :], r.eq[:, :, :], ALU.add))
                c.link(dve.tensor_reduce(r.rank[:, :], r.gt[:, :, :], AX.X, ALU.add))
                dve.scalar_tensor_tensor(r.weight[:, b, :], r.rank[:, :], TOPK - 0.5, r.prob[:, b, :], ALU.is_lt,
                                         ALU.mult).then_inc(comb_ready, 1)

        @block.tensor
        def _(pe):
            pe.wait_ge(loaded, 64)
            for k in range(KD):
                mm = pe.transpose(t.bank[0][:, k * EXPERTS:(k + 1) * EXPERTS], r.gw[:, k * P:(k + 1) * P],
                                  t.ident[0:EXPERTS, 0:EXPERTS])
            mm.then_inc(turned, 1)
            pe.wait_ge(gw_lo, 1)
            out = t.bank[1][0:EXPERTS, 0:TOK]
            for k in range(KD):
                es = slice(k * EXPERTS, (k + 1) * EXPERTS)
                pe.matmul(out, r.gw_hi[:, es], t.xn_hi[:, k, :], start=k == 0, stop=False)
                pe.matmul(out, r.gw_hi[:, es], t.xn_lo[:, k, :], start=False, stop=False)
                pe.matmul(out, r.gw_lo[:, es], t.xn_hi[:, k, :], start=False, stop=False)
                mm = pe.matmul(out, r.gw_lo[:, es], t.xn_lo[:, k, :], start=False, stop=k == KD - 1)
            mm.then_inc(logits_filled, 1)
            pe.wait_ge(logitT_ready, 1)
            for b in range(BATCH):
                mm = pe.transpose(t.bank[2][:, b * EXPERTS:(b + 1) * EXPERTS], r.logitT[:, b * SEQ:(b + 1) * SEQ],
                                  t.ident[0:EXPERTS, 0:EXPERTS])
            mm.then_inc(logits_filled, 1)
            for b in range(BATCH):
                pe.wait_ge(comb_ready, b + 1)
                mm = pe.transpose(t.bank[7][0:EXPERTS, b * SEQ:(b + 1) * SEQ], r.weight[:, b, :], t.ident[:, :])
            mm.then_inc(comb_turned, 1)
            pe.wait_ge(combT_ready, 1)
            pe.wait_ge(sel_steps, 5)
            for n in range(TILES // 2):
                if n >= 4:
                    pe.wait_ge(spread_read, n - 3)
                for v in range(2):
                    mm = pe.matmul(t.bank[n % 4 + 3][:, v * TOK:(v + 1) * TOK], r.sel[:, 2 * n + v, :],
                                   r.combT[:, :], start=True, stop=True)
                mm.then_inc(spread, 1)


def ffn_slot(j):
    return j % JB % 3


def expert_rows(w1, q, j):
    def src(a):
        return w1.rearrange("e (s o) h -> o (e s) h", s=4)[
            j * Q:(j + 1) * Q, bass.ds(q * 8, 8), a * 2 * P:(a + 1) * 2 * P]
    return src


def expert_cols(w2, q):
    def src(a, col, n):
        at = a % 2 * QW + col
        return w2.rearrange("e (b p) i -> p e b i", p=Q)[
            :, bass.ds(q * 2 + a // 2, 1), :, at:at + n].rearrange("p e b i -> p (e b) i")
    return src


def ffn_load_rows(sp, f, s, src):
    for a in range(4):
        sp.dma_start(f.nat[a * Q:(a + 1) * Q, s, :, :], src(a)).then_inc(f.rows_loaded[s], 16)


def ffn_load_cols(sp, f, c, src):
    n = min(4, JB - 4 * c) * Q
    for a in range(4):
        sp.dma_start(f.nat_c[a * Q:(a + 1) * Q, c, :, 0:n], src(a, 4 * c * Q, n)).then_inc(f.cols_loaded[c], 16)


def ffn_block(nc, sem, w1, w2, sw1, sw2, out, t, f, comb):
    turned, w_hi_done, lo_dve, lo_pool = (sem("ffn_" + x) for x in ("turned", "hi", "lo_dve", "lo_pool"))
    rows_loaded, cols_loaded = f.rows_loaded, f.cols_loaded
    GBK, UBK = t.bank[6], t.bank[7]
    gate_filled, silu_done, sgc_ready, up_filled, act_ready, act_hi, act_lo, summed, y_ready, stored = (
        sem("ffn_" + x) for x in ("gate", "silu", "sgc", "up", "act", "acthi", "actlo", "summed", "y", "stored"))
    cw_ready = sem("ffn_cw")
    SHARED = PAIRS
    CREDIT = 6
    slot = ffn_slot

    def uses(s):
        return len([j for j in range(JB) if slot(j) == s])

    def rows_landed(q, j):
        q, j = q + j // JB, j % JB
        return q * (64 * uses(slot(j))) + 64 * (j // 3 + 1)

    with nc.Block() as block:
        @block.sync
        def _(sp):
            def shared_rows(j):
                def src(a):
                    return sw1.rearrange("(s o) h -> o s h", s=8)[j * Q:(j + 1) * Q, :, a * 2 * P:(a + 1) * 2 * P]
                return src

            def shared_cols(a, col, n):
                return sw2.rearrange("(b p) i -> p b i", p=Q)[:, :, a * QW + col:a * QW + col + n]

            def pair(q, next_rows, next_cols):
                for j in range(JB):
                    sp.wait_ge(turned, 3 * (q * JB + j) + (2 + CREDIT))
                    if j + 2 < JB:
                        ffn_load_rows(sp, f, slot(j + 2), shared_rows(j + 2) if q is SHARED else expert_rows(w1, q, j + 2))
                    elif next_rows is not None:
                        ffn_load_rows(sp, f, slot(j + 2), next_rows(j + 2 - JB))
                    cols = shared_cols if q is SHARED else expert_cols(w2, q)
                    if j in (0, 4):
                        ffn_load_cols(sp, f, 1 + j // 4, cols)
                    elif j == 8 and next_cols is not None:
                        ffn_load_cols(sp, f, 0, next_cols)

            with sp.Fori(0, PAIRS - 1) as q:
                pair(q, lambda j: expert_rows(w1, q + 1, j), expert_cols(w2, q + 1))
            pair(PAIRS - 1, shared_rows, shared_cols)
            pair(SHARED, None, None)
            for b in range(BATCH):
                sp.wait_ge(y_ready, 2 * b + 2)
                sp.dma_start(out[b], t.x_res[:, b, :]).then_inc(stored, 16)
            sp.wait_ge(stored, 16 * BATCH)

        @block.gpsimd
        def _(pool):
            def split_up(step, s):
                pool.wait_ge(w_hi_done, 3 * step + 2)
                pool.tensor_tensor(f.w_lo[:, s, 1, :], f.wt[:, 1, :], f.w_hi[:, s, 1, :].bitcast(F32),
                                   ALU.subtract).then_inc(lo_pool, 1)

            def pair(q, last=False):
                pool.tensor_copy(f.cw[:, :], comb[:, bass.ds(q, 1), :].rearrange("p a s -> p (a s)")).then_inc(cw_ready, 1)
                pool.wait_ge(cw_ready, q + 1)
                for j in range(JB):
                    step = q * JB + j
                    pool.wait_ge(silu_done, step + 2)
                    pool.wait_ge(act_ready, step + 1)
                    pool.tensor_tensor(f.sgc[:, :], f.sg[:, :], f.cw[:, :], ALU.mult).then_inc(sgc_ready, 1)
                    if not (last and j == JB - 1):
                        split_up(step + 1, slot(j + 1))
                pool.wait_ge(sgc_ready, q * JB + (JB + 1))
            pool.sem_inc(lo_pool, 1)
            split_up(0, 0)
            with pool.Fori(0, PAIRS) as q:
                pair(q)
            pair(SHARED, last=True)

        @block.scalar
        def _(act):
            def hi(step, w, s):
                act.wait_ge(turned, 3 * step + (w + 1 + CREDIT))
                act.activation(f.w_hi[:, s, w, :], f.wt[:, w, :], ACT.Copy).then_inc(w_hi_done, 1)

            def silu(step):
                act.wait_ge(gate_filled, step + 1)
                act.wait_ge(sgc_ready, step + 1)
                act.activation(f.sg[:, :], GBK[:, 0:TOK], ACT.Silu).then_inc(silu_done, 1)

            def pair(q, last=False):
                for j in range(JB):
                    step, left = q * JB + j, JB - 1 - j if last else JB
                    if left:
                        hi(step + 1, 1, slot(j + 1))
                    act.wait_ge(act_ready, step + 2)
                    act.activation(f.a_hi[:, :], f.a[:, :], ACT.Copy).then_inc(act_hi, 1)
                    if left:
                        hi(step + 1, 2, slot(j + 1))
                        silu(step + 1)
                    if left > 1:
                        hi(step + 2, 0, slot(j + 2))
            act.sem_inc(silu_done, 1)
            act.sem_inc(sgc_ready, 1)
            for w in range(3):
                hi(0, w, 0)
            silu(0)
            hi(1, 0, 1)
            with act.Fori(0, PAIRS) as q:
                pair(q)
            pair(SHARED, last=True)

        @block.vector
        def _(dve):
            def turn_rows(q, j, w, shared=False):
                step = q * JB + j
                if w == 0:
                    dve.wait_ge(lo_dve, 2 * step + 1)
                else:
                    dve.wait_ge(lo_pool, step + 1)
                if w == 0:
                    dve.wait_ge(rows_loaded[slot(j)], rows_landed(q, j))
                for e in range(2):
                    at = 4 * w + 2 * e if shared else 4 * e + 2 * w
                    ins = dve.transpose(
                        f.wt[:, w, :].rearrange("p (k b o) -> p b k o", k=KD, b=4)[:, 2 * e:2 * e + 2],
                        f.nat[:, slot(j), at:at + 2, :].rearrange("p c (k h) -> p c k h", k=KD))
                ins.then_inc(turned, 1)

            def turn_cols(q, j):
                c, jj = j % JB // 4, j % JB % 4
                dve.wait_ge(lo_dve, 2 * (q * JB + j) + 2)
                dve.wait_ge(cols_loaded[c], (q + j // JB) * 64 + 64)
                dve.transpose(f.wt[:, 2, :].rearrange("p (b h) -> p b h", h=Q),
                              f.nat_c[:, c, :, jj * Q:(jj + 1) * Q]).then_inc(turned, 1)

            def lo(step, w, s):
                dve.wait_ge(w_hi_done, 3 * step + (w + 1))
                dve.tensor_tensor(f.w_lo[:, s, w, :], f.wt[:, w, :], f.w_hi[:, s, w, :].bitcast(F32),
                                  ALU.subtract).then_inc(lo_dve, 1)

            def pair(q, last=False, before_last=False):
                for j in range(JB):
                    step, left = q * JB + j, JB - 1 - j if last else JB
                    if left:
                        lo(step + 1, 0, slot(j + 1))
                        turn_rows(q, j + 1, 1, last or before_last and j + 1 >= JB)
                    dve.wait_ge(up_filled, step + 1)
                    dve.wait_ge(sgc_ready, step + 2)
                    dve.tensor_tensor(f.a[:, :], UBK[:, 0:TOK], f.sgc[:, :], ALU.mult).then_inc(act_ready, 1)
                    if left:
                        turn_cols(q, j + 1)
                    dve.wait_ge(act_hi, step + 1)
                    dve.tensor_tensor(f.a_lo[:, :], f.a[:, :], f.a_hi[:, :].bitcast(F32),
                                      ALU.subtract).then_inc(act_lo, 1)
                    if left > 1:
                        turn_rows(q, j + 2, 0, last or before_last and j + 2 >= JB)
                    if left:
                        lo(step + 1, 2, slot(j + 1))
            dve.sem_inc(turned, CREDIT)
            dve.sem_inc(lo_dve, 2)
            dve.sem_inc(act_ready, 1)
            turn_rows(0, 0, 0)
            turn_rows(0, 0, 1)
            lo(0, 0, 0)
            turn_cols(0, 0)
            turn_rows(0, 1, 0)
            lo(0, 2, 0)
            with dve.Fori(0, PAIRS - 1) as q:
                pair(q)
            pair(PAIRS - 1, before_last=True)
            pair(SHARED, last=True)
            dve.wait_ge(summed, 1)
            for b in range(BATCH):
                for h in range(2):
                    at = slice(h * HALF, (h + 1) * HALF)
                    dve.tensor_tensor(t.x_res[:, b, at], t.bank[2 * b + h][:, :], t.x_res[:, b, at],
                                      ALU.add).then_inc(y_ready, 1)

        @block.tensor
        def _(pe):
            def gate(step, s):
                pe.wait_ge(lo_dve, 2 * step + 3)
                pe.wait_ge(silu_done, step + 1)
                project(pe, t, f, GBK[:, 0:TOK], 0, s).then_inc(gate_filled, 1)

            def pair(q, last=False):
                for j in range(JB):
                    step, end = q * JB + j, last and j == JB - 1
                    pe.wait_ge(lo_pool, step + 2)
                    pe.wait_ge(act_ready, step + 1)
                    project(pe, t, f, UBK[:, 0:TOK], 1, slot(j)).then_inc(up_filled, 1)
                    if not end:
                        gate(step + 1, slot(j + 1))
                    pe.wait_ge(lo_dve, 2 * step + 4)
                    pe.wait_ge(act_lo, step + 1)
                    mm = accumulate(pe, t, f, f.a_hi, f.a_lo, slot(j), end)
                    if end:
                        mm.then_inc(summed, 1)

            zero_sums(pe, t)
            gate(0, 0)
            with pe.Fori(0, PAIRS) as q:
                pair(q)
            pair(SHARED, last=True)


class Tensors:
    pass


def program(nc, x, ctx_1024, mask, Wq, Wk, Wv, Wo, in_proj_w, conv_w, conv_b, A_log, dt_bias, D, norm_w,
            out_proj_w, gate_w, w1, w2, shared_w1, shared_w2, out):
    with ExitStack() as whole:
        def sem(name):
            return whole.enter_context(nc.semaphore(name))

        def maker(stack, prefix):
            def sb(name, shape, dt=F32):
                return stack.enter_context(nc.sbuf_tensor(prefix + name, shape, dt))
            return sb

        t = Tensors()
        sb = maker(whole, "t_")
        t.x_res = sb("x_res", [P, BATCH, DM])
        t.xn_hi = sb("xn_hi", [P, KD, TOK], F32R)
        t.xn_lo = sb("xn_lo", [P, KD, TOK], F32R)
        t.ident = sb("ident", [P, P])
        t.ones = sb("ones", [P, P])
        t.tri = sb("tri", [P, P])
        t.after = sb("after", [P, P], F32R)
        t.zeros = sb("zeros", [P, P], F32R)
        t.eps = sb("eps", [P, 1])
        t.stats = sb("stats", [P, BATCH, 2, 6])
        t.meanvar = sb("meanvar", [P, BATCH, 2])
        t.std = sb("std", [P, BATCH])
        t.rstd = sb("rstd", [P, BATCH])
        t.bank = [whole.enter_context(nc.psum_tensor(f"bank{n}", [P, HALF], F32)) for n in range(8)]

        made = sem("masks_made")
        with nc.sbuf_tensor("after_f", [P, P], F32) as after_f, nc.Block() as block:
            @block.gpsimd
            def _(pool):
                pool.memset(t.ident[:, :], 0.0).then_inc(made, 1)
                pool.memset(t.ones[:, :], 1.0).then_inc(made, 1)
                pool.memset(t.tri[:, :], 1.0).then_inc(made, 1)
                pool.memset(after_f[:, :], 1.0).then_inc(made, 1)
                pool.memset(t.zeros[:, :].bitcast(F32), 0.0).then_inc(made, 1)
                pool.wait_ge(made, 5)
                pool.affine_select(out=t.ident[:, :], in_=t.ident[:, :], compare_op=ALU.not_equal, fill=1.0, base=0,
                                   pattern=[[-1, P]], channel_multiplier=1)
                pool.affine_select(out=t.tri[:, :], in_=t.tri[:, :], compare_op=ALU.is_ge, fill=0.0, base=0,
                                   pattern=[[1, P]], channel_multiplier=-1)
                pool.affine_select(out=after_f[:, :], in_=after_f[:, :], compare_op=ALU.is_gt, fill=0.0, base=0,
                                   pattern=[[-1, P]], channel_multiplier=1).then_inc(made, 1)
                pool.wait_ge(made, 6)
                pool.tensor_copy(t.after[:, :], after_f[:, :])

        def layernorm(**kw):
            with ExitStack() as stack:
                t.xn = stack.enter_context(nc.sbuf_tensor(f"ln{len(normed)}_xn", [P, BATCH, DM], F32))
                layernorm_block(nc, ln_sems, len(normed), t, len(normed) in QUAD_ROUNDS, **kw)
            normed.append(1)
        normed = []
        ln_sems = [sem("ln_" + x) for x in ("x_in", "chain", "var", "std", "xn", "turned", "hi", "lo")]

        layernorm(load_x=x)
        with ExitStack() as stack:
            a = Tensors()
            sb = maker(stack, "a_")
            a.ctx_hi = sb("ctx_hi", [P, KC, CTX], F32R)
            a.ctx_lo = sb("ctx_lo", [P, KC, CTX], F32R)
            a.k_hi = sb("k_hi", [P, CTX], F32R)
            a.k_lo = sb("k_lo", [P, CTX], F32R)
            a.v_hi = sb("v_hi", [P, CTX // P, HD], F32R)
            a.v_lo = sb("v_lo", [P, CTX // P, HD], F32R)
            a.v_stage = sb("v_stage", [P, 2, HALF])
            a.q_hi = sb("q_hi", [P, 2 * SEQ], F32R)
            a.q_lo = sb("q_lo", [P, 2 * SEQ], F32R)
            a.p = sb("p", [P, 2, CTX])
            a.pt_hi = sb("pt_hi", [P, 3, HALF], F32R)
            a.pt_lo = sb("pt_lo", [P, 3, HALF], F32R)
            a.w_nat = sb("w_nat", [P, 2 * DM])
            a.w_hi = sb("w_hi", [P, 2 * DM], F32R)
            a.w_lo = sb("w_lo", [P, 2 * DM], F32R)
            a.kv_nat = sb("kv_nat", [P, 2, KC, HD])
            a.kv_hi = sb("kv_hi", [P, 2, KC, HD], F32R)
            a.kv_lo = sb("kv_lo", [P, 2, KC, HD], F32R)
            a.mask_raw = sb("mask_raw", [P, CTX], U8)
            a.mask_bias = sb("mask_bias", [P, CTX], mybir.dt.bfloat16)
            a.any_valid = sb("any_valid", [P, BATCH])
            a.mark = sb("mark", [P, 8])
            a.chunkmax = sb("chunkmax", [P, 8])
            a.rowmax = sb("rowmax", [P, 2])
            a.negmax = sb("negmax", [P, 2])
            a.psum = sb("psum", [P, 2])
            a.rinv = sb("rinv", [P, 2])
            a.diag = sb("diag", [P, 2 * SEQ])
            a.rb = sb("rb", [P, 2 * SEQ])
            a.ot = sb("ot", [P, 2 * SEQ])
            a.ot_hi = sb("ot_hi", [P, 2 * SEQ], F32R)
            a.ot_lo = sb("ot_lo", [P, 2 * SEQ], F32R)
            attention_block(nc, sem, ctx_1024, mask, Wq, Wk, Wv, Wo, t, a)

        with ExitStack() as stack:
            m = Tensors()
            sb = maker(stack, "m_")
            m.head_rows = sb("head_rows", [P, 3, DM])
            m.head_nat = sb("head_nat", [P, 3, DM])
            m.nat = sb("nat", [P, 2, 2, DM])
            m.nat_c = sb("nat_c", [P, 2, DM])
            m.wt = sb("wt", [P, 2, DM])
            m.w_hi = sb("w_hi", [P, 2, 3, DM], F32R)
            m.w_lo = sb("w_lo", [P, 2, 3, DM], F32R)
            m.convw = sb("convw", [P, XB + 2, 4])
            m.convb = sb("convb", [P, XB + 2])
            m.normw = sb("normw", [P, XB])
            m.dcol = sb("dcol", [P, XB])
            m.dtb = sb("dtb", [P, SSM_H])
            m.alog = sb("alog", [P, SSM_H])
            m.ea = sb("ea", [P, SSM_H])
            m.zdt = sb("zdt", [P, BATCH, SSM_H])
            m.nabs = sb("nabs", [P, BATCH, SSM_H])
            m.e_dt = sb("e_dt", [P, BATCH, SSM_H])
            m.w_dt = sb("w_dt", [P, BATCH, SSM_H])
            m.ln_dt = sb("ln_dt", [P, BATCH, SSM_H])
            m.d_dt = sb("d_dt", [P, BATCH, SSM_H])
            m.is0 = sb("is0", [P, BATCH, SSM_H])
            m.dth = sb("dth", [P, BATCH, SSM_H])
            m.a = sb("a", [P, BATCH, SSM_H])
            m.a_lo = sb("a_lo", [P, BATCH, SSM_H])
            m.a_hi = sb("a_hi", [P, BATCH, SSM_H], F32R)
            m.xpad = sb("xpad", [P, BATCH, SEQ + 3])
            m.z = sb("z", [P, TOK])
            m.th = sb("th", [P, TOK])
            m.xs = sb("xs", [P, 2, TOK])
            m.thg = sb("thg", [P, TOK])
            m.sg = sb("sg", [P, TOK])
            m.y = sb("y", [P, TOK])
            m.ynw = sb("ynw", [P, TOK])
            m.yg = sb("yg", [P, TOK])
            m.sumsq = sb("sumsq", [P, TOK])
            m.dtT = sb("dtT", [SSM_H, TOK])
            m.bc = sb("bc", [P, 2, TOK])
            m.gm = sb("gm", [P, BATCH, SEQ])
            m.xdt = sb("xdt", [P, BATCH, 2, P])
            m.atri_hi = sb("atri_hi", [P, HALF], F32R)
            m.atri_lo = sb("atri_lo", [P, HALF], F32R)
            m.e = sb("e", [P, HALF])
            m.mt = sb("mt", [P, HALF])
            m.yn_hi = sb("yn_hi", [P, 2, TOK], F32R)
            m.yn_lo = sb("yn_lo", [P, 2, TOK], F32R)
            m.var = sb("var", [P, BATCH])
            m.std = sb("std", [P, BATCH])
            m.rstd = sb("rstd", [P, BATCH])
            m.head_tiles = [sem(f"head_tile{w}") for w in range(3)]
            m.rows_loaded = [[sem(f"mix_rows{w}_{s}") for s in range(2)] for w in range(2)]
            layernorm(load_ahead=lambda sp: load_head_tiles(sp, m, in_proj_w))
            mixer_head_block(nc, sem, in_proj_w, conv_w, conv_b, A_log, dt_bias, D, norm_w, t, m)
            mixer_block(nc, sem, in_proj_w, out_proj_w, t, m)

        with ExitStack() as stack:
            comb = stack.enter_context(nc.sbuf_tensor("comb", [P, PAIRS + 1, TOK], F32))
            f = Tensors()
            sb = maker(stack, "f_")
            f.nat = sb("nat", [P, 3, 8, 2 * P])
            f.nat_c = sb("nat_c", [P, 3, DM // Q, 4 * Q])
            f.wt = sb("wt", [P, 3, DM])
            f.w_hi = sb("w_hi", [P, 3, 3, DM], F32R)
            f.w_lo = sb("w_lo", [P, 3, 3, DM], F32R)
            f.sg = sb("sg", [P, TOK])
            f.sgc = sb("sgc", [P, TOK])
            f.a = sb("a", [P, TOK])
            f.cw = sb("cw", [P, TOK])
            f.a_hi = sb("a_hi", [P, TOK], F32R)
            f.a_lo = sb("a_lo", [P, TOK], F32R)
            f.rows_loaded = [sem(f"ffn_rows{s}") for s in range(3)]
            f.cols_loaded = [sem(f"ffn_cols{c}") for c in range(3)]
            f.gw, f.gw_loaded = f.wt[0:EXPERTS, 0, :], sem("rt_loaded")
            layernorm(load_ahead=lambda sp: load_gate_w(sp, f, gate_w))
            with ExitStack() as inner:
                r = Tensors()
                r.comb = comb
                sb = maker(inner, "r_")
                r.gw = f.gw
                r.gw_hi = sb("gw_hi", [P, KD * EXPERTS], F32R)
                r.gw_lo = sb("gw_lo", [P, KD * EXPERTS], F32R)
                r.logit = sb("logit", [P, BATCH, EXPERTS])
                r.prob = sb("prob", [P, BATCH, EXPERTS])
                r.weight = sb("weight", [P, BATCH, EXPERTS])
                r.negmax = sb("negmax", [P, BATCH])
                r.psum = sb("psum", [P, BATCH])
                r.ltri = sb("ltri", [P, EXPERTS, EXPERTS])
                r.eq = sb("eq", [P, EXPERTS, EXPERTS])
                r.gt = sb("gt", [P, EXPERTS, EXPERTS])
                r.logitT = sb("logitT", [EXPERTS, TOK])
                r.rank = sb("rank", [P, EXPERTS])
                r.sel = f.wt[0:EXPERTS, 1, :].rearrange("e (q p) -> e q p", q=PAIRS)
                r.combT = sb("combT", [EXPERTS, TOK])
                router_block(nc, sem, w1, w2, t, r, f)
            ffn_block(nc, sem, w1, w2, shared_w1, shared_w2, out, t, f, comb)


_INS = ["x", "ctx_1024", "mask_BxS2_bf1", "L0_xattn_Wq", "L0_xattn_Wk", "L0_xattn_Wv", "L0_xattn_Wo",
        "L0_attn_in_proj_w", "L0_attn_conv_w", "L0_attn_conv_b", "L0_attn_A_log", "L0_attn_dt_bias", "L0_attn_D",
        "L0_attn_norm_w", "L0_attn_out_proj_w", "L0_ffn_gate_w", "L0_ffn_w1", "L0_ffn_w2", "L0_ffn_shared_w1",
        "L0_ffn_shared_w2"]


def kernel(**inputs):
    import numpy as np
    import concourse.bacc as bacc
    from concourse.bass_utils import run_bass_kernel_spmd

    nc = bacc.Bacc("TRN2", target_bir_lowering=False, num_devices=1)
    arrays, args = {}, []
    for name in _INS:
        v = np.ascontiguousarray(inputs[name])
        if v.dtype == np.bool_:
            v = v.view(np.uint8)
        arrays[f"in_{name}"] = v
        args.append(nc.dram_tensor(f"in_{name}", v.shape, mybir.dt.from_np(v.dtype), kind="ExternalInput").ap())
    args.append(nc.dram_tensor("out", (BATCH, SEQ, DM), F32, kind="ExternalOutput").ap())
    program(nc, *args)
    r = run_bass_kernel_spmd(nc, [arrays], core_ids=[0])
    return r.results[0]["out"]
```
